# Optimizing a Trainium2 kernel written in Bass

```python
import numpy as np
import jax
import jax.numpy as jnp

def _softmax(x, axis=-1):
    return jax.nn.softmax(x, axis=axis)

def _gelu(x):
    return jax.nn.gelu(x, approximate=True)

def _silu(x):
    return jax.nn.silu(x)

def _sigmoid(x):
    return jax.nn.sigmoid(x)

def _layernorm(x, axis=-1, eps=1e-05):
    m = jnp.mean(x, axis=axis, keepdims=True)
    v = jnp.var(x, axis=axis, keepdims=True)
    return (x - m) / jnp.sqrt(v + eps)

def _scatter_add(tgt, idx, src, axis=0):
    return tgt.at[idx].add(src)

def _segment_sum(src, seg, n):
    return jax.ops.segment_sum(src, seg, n)
kernel_name = 'mk_flamingo_gated_d1_seqx_r4_21a56a'

def setup_inputs(seed: int=0):
    np.random.seed(seed)
    _w = jnp.asarray

    def _rec_inputs():
        import jax
        import jax.numpy as jnp
        _rk = jax.random.key(seed)
        x = -0.0003929 + 0.9999 * jax.random.normal(jax.random.fold_in(_rk, 1), (2, 1024, 256), jnp.float32)
        _lenS = 1024 - jax.random.randint(jax.random.fold_in(_rk, 7), (2,), 0, max(1, 1024 // 4) + 1, jnp.int32)
        _lenS2 = 77 - jax.random.randint(jax.random.fold_in(_rk, 8), (2,), 0, max(1, 77 // 4) + 1, jnp.int32)
        _ctx_1024P = jax.random.normal(jax.random.fold_in(_rk, 11), (2, 16, 256), jnp.float32)
        _ctx_1024c = jax.random.dirichlet(jax.random.fold_in(_rk, 511), 0.3 * jnp.ones((16,), jnp.float32), (2, 77))
        _ctx_1024t = jnp.einsum('bsk,bkd->bsd', _ctx_1024c, _ctx_1024P)
        _ctx_1024t = _ctx_1024t * jax.lax.rsqrt(jnp.mean(jnp.square(_ctx_1024t)) + 1e-12) * 0.953939
        ctx_1024 = 0.000227908 + 0.99994 * (_ctx_1024t + 0.3 * jax.random.normal(jax.random.fold_in(_rk, 611), (2, 77, 256), jnp.float32))
        _g = jax.random.normal(jax.random.fold_in(_rk, 9001), (2, 1), jnp.float32)
        _g = jnp.sign(_g) * jnp.maximum(jnp.abs(_g), 1.0) + (_g == 0) * 1.0
        g_xattn = _g[0]
        g_ffn = _g[1]
        return (x, ctx_1024, g_xattn, g_ffn)
    x, ctx_1024, g_xattn, g_ffn = _rec_inputs()

    def _L0_xattn_setup():
        import jax, jax.numpy as jnp
        import numpy as np
        DIM = 256
        HEADS = 16
        HEAD_DIM = 64
        INNER = HEADS * HEAD_DIM
        SCALE = 8.0
        LN_EPS = 1e-05
        NORM_EPS = 1e-12

        def layer_norm(x, g, b):
            m = jnp.mean(x, axis=-1, keepdims=True)
            v = jnp.mean((x - m) ** 2, axis=-1, keepdims=True)
            return (x - m) * jax.lax.rsqrt(v + LN_EPS) * g + b

        def l2_normalize(x):
            n = jnp.sqrt(jnp.sum(x * x, axis=-1, keepdims=True))
            return x / jnp.maximum(n, NORM_EPS)
        key = jax.random.key(seed)
        ks = jax.random.split(key, 8)
        B, N, T = (4, 1024, 64)
        s = 0.02
        return {'x': jax.random.normal(ks[0], (B, N, DIM), jnp.float32), 'context': jax.random.normal(ks[1], (B, T, DIM), jnp.float32), 'Wq': jax.random.normal(ks[2], (DIM, INNER), jnp.float32) * s, 'Wkv': jax.random.normal(ks[3], (DIM, 2 * INNER), jnp.float32) * s, 'Wo': jax.random.normal(ks[4], (INNER, DIM), jnp.float32) * s, 'null_kv': jax.random.normal(ks[5], (2, HEAD_DIM), jnp.float32), 'q_scale': jnp.ones((HEAD_DIM,), jnp.float32), 'k_scale': jnp.ones((HEAD_DIM,), jnp.float32), 'ln_in_g': jnp.ones((DIM,), jnp.float32), 'ln_in_b': jnp.zeros((DIM,), jnp.float32), 'ln_ctx_g': jnp.ones((DIM,), jnp.float32), 'ln_ctx_b': jnp.zeros((DIM,), jnp.float32), 'ln_out_g': jnp.ones((DIM,), jnp.float32), 'ln_out_b': jnp.zeros((DIM,), jnp.float32)}
    _L0_xattn_all = _L0_xattn_setup()
    _L0_xattn_in = {k: v for k, v in _L0_xattn_all.items() if k in ('Wq', 'Wkv', 'Wo', 'null_kv', 'q_scale', 'k_scale', 'ln_in_g', 'ln_in_b', 'ln_ctx_g', 'ln_ctx_b', 'ln_out_g', 'ln_out_b')}
    del _L0_xattn_all

    def _L0_ffn_setup():
        import jax, jax.numpy as jnp
        import numpy as np
        N_EMBD = 256
        ITER_SIZE = 4 * N_EMBD
        FULL_SIZE = 3 * ITER_SIZE
        R = 0.7

        def _topk_mask(ck, k):
            probs = jax.nn.softmax(ck, axis=-1)
            _, idx = jax.lax.top_k(probs, k)
            b = jnp.arange(probs.shape[0])[:, None]
            return jnp.zeros_like(probs).at[b, idx].set(1.0)

        def _forward(x, Wm, Wp, Wc1, Wc2):
            B = x.shape[0]
            base = jnp.zeros((B, FULL_SIZE), x.dtype).at[:, :ITER_SIZE].set(1.0)

            def step(carry, _):
                xc, active, history, done = carry
                h = jnp.einsum('btc,fc->btf', xc, Wm) * active[:, None, :]
                h = jax.nn.relu(h)
                x_new = jnp.einsum('btf,cf->btc', h, Wp)
                pooled = x_new.mean(axis=1)
                ck = jnp.einsum('bd,fd->bf', jax.nn.relu(jnp.einsum('bc,dc->bd', pooled, Wc1)), Wc2)
                new_mask = _topk_mask(ck, ITER_SIZE)
                combined = jnp.clip(history + new_mask, 0.0, 1.0)
                novelty = (combined - history).sum(axis=1).mean() / ITER_SIZE
                done_next = jnp.logical_or(done, novelty < R)
                x_out = jnp.where(done, xc, x_new)
                active_out = jnp.where(done, active, new_mask)
                history_out = jnp.where(done, history, combined)
                return ((x_out, active_out, history_out, done_next), None)
            init = (x, base, base, jnp.array(False))
            (x_fin, _, _, _), _ = jax.lax.scan(step, init, None, length=3)
            return x_fin
        key = jax.random.key(seed)
        ks = jax.random.split(key, 5)
        B, T = (8, 256)
        s = 0.02
        return {'x': jax.random.normal(ks[0], (B, T, N_EMBD), jnp.float32), 'Wm': jax.random.normal(ks[1], (FULL_SIZE, N_EMBD), jnp.float32) * s, 'Wp': jax.random.normal(ks[2], (N_EMBD, FULL_SIZE), jnp.float32) * s, 'Wc1': jax.random.normal(ks[3], (N_EMBD // 4, N_EMBD), jnp.float32) * s, 'Wc2': jax.random.normal(ks[4], (FULL_SIZE, N_EMBD // 4), jnp.float32) * s}
    _L0_ffn_all = _L0_ffn_setup()
    _L0_ffn_in = {k: v for k, v in _L0_ffn_all.items() if k in ('Wm', 'Wp', 'Wc1', 'Wc2')}
    del _L0_ffn_all
    return {'x': x, 'ctx_1024': ctx_1024, 'g_xattn': g_xattn, 'g_ffn': g_ffn, 'L0_xattn_Wq': _L0_xattn_in['Wq'], 'L0_xattn_Wkv': _L0_xattn_in['Wkv'], 'L0_xattn_Wo': _L0_xattn_in['Wo'], 'L0_xattn_null_kv': _L0_xattn_in['null_kv'], 'L0_xattn_q_scale': _L0_xattn_in['q_scale'], 'L0_xattn_k_scale': _L0_xattn_in['k_scale'], 'L0_xattn_ln_in_g': _L0_xattn_in['ln_in_g'], 'L0_xattn_ln_in_b': _L0_xattn_in['ln_in_b'], 'L0_xattn_ln_ctx_g': _L0_xattn_in['ln_ctx_g'], 'L0_xattn_ln_ctx_b': _L0_xattn_in['ln_ctx_b'], 'L0_xattn_ln_out_g': _L0_xattn_in['ln_out_g'], 'L0_xattn_ln_out_b': _L0_xattn_in['ln_out_b'], 'L0_ffn_Wm': _L0_ffn_in['Wm'], 'L0_ffn_Wp': _L0_ffn_in['Wp'], 'L0_ffn_Wc1': _L0_ffn_in['Wc1'], 'L0_ffn_Wc2': _L0_ffn_in['Wc2']}

def reference(x, ctx_1024, g_xattn, g_ffn, L0_xattn_Wq, L0_xattn_Wkv, L0_xattn_Wo, L0_xattn_null_kv, L0_xattn_q_scale, L0_xattn_k_scale, L0_xattn_ln_in_g, L0_xattn_ln_in_b, L0_xattn_ln_ctx_g, L0_xattn_ln_ctx_b, L0_xattn_ln_out_g, L0_xattn_ln_out_b, L0_ffn_Wm, L0_ffn_Wp, L0_ffn_Wc1, L0_ffn_Wc2):
    import jax
    import jax.numpy as jnp

    def _L0_xattn_ref(x, context, Wq, Wkv, Wo, null_kv, q_scale, k_scale, ln_in_g, ln_in_b, ln_ctx_g, ln_ctx_b, ln_out_g, ln_out_b):
        import jax, jax.numpy as jnp
        import numpy as np
        DIM = 256
        HEADS = 16
        HEAD_DIM = 64
        INNER = HEADS * HEAD_DIM
        SCALE = 8.0
        LN_EPS = 1e-05
        NORM_EPS = 1e-12

        def layer_norm(x, g, b):
            m = jnp.mean(x, axis=-1, keepdims=True)
            v = jnp.mean((x - m) ** 2, axis=-1, keepdims=True)
            return (x - m) * jax.lax.rsqrt(v + LN_EPS) * g + b

        def l2_normalize(x):
            n = jnp.sqrt(jnp.sum(x * x, axis=-1, keepdims=True))
            return x / jnp.maximum(n, NORM_EPS)
        B, N, _ = x.shape
        T = context.shape[1]
        xn = layer_norm(x, ln_in_g, ln_in_b)
        cn = layer_norm(context, ln_ctx_g, ln_ctx_b)
        q = xn @ Wq
        kv = cn @ Wkv
        k, v = jnp.split(kv, 2, axis=-1)

        def split_heads(t):
            b, s, _ = t.shape
            return t.reshape(b, s, HEADS, HEAD_DIM).transpose(0, 2, 1, 3)
        q, k, v = (split_heads(q), split_heads(k), split_heads(v))
        nk = jnp.broadcast_to(null_kv[0], (B, HEADS, 1, HEAD_DIM))
        nv = jnp.broadcast_to(null_kv[1], (B, HEADS, 1, HEAD_DIM))
        k = jnp.concatenate([k, nk], axis=2)
        v = jnp.concatenate([v, nv], axis=2)
        q = l2_normalize(q) * q_scale
        k = l2_normalize(k) * k_scale
        scores = jnp.einsum('bhid,bhkd->bhik', q, k) * SCALE
        attn = jax.nn.softmax(scores, axis=-1)
        out = jnp.einsum('bhik,bhkd->bhid', attn, v)
        out = out.transpose(0, 2, 1, 3).reshape(B, N, INNER)
        out = out @ Wo
        return layer_norm(out, ln_out_g, ln_out_b)

    def _L0_ffn_ref(x, Wm, Wp, Wc1, Wc2):
        import jax, jax.numpy as jnp
        import numpy as np
        N_EMBD = 256
        ITER_SIZE = 4 * N_EMBD
        FULL_SIZE = 3 * ITER_SIZE
        R = 0.7

        def _topk_mask(ck, k):
            probs = jax.nn.softmax(ck, axis=-1)
            _, idx = jax.lax.top_k(probs, k)
            b = jnp.arange(probs.shape[0])[:, None]
            return jnp.zeros_like(probs).at[b, idx].set(1.0)

        def _forward(x, Wm, Wp, Wc1, Wc2):
            B = x.shape[0]
            base = jnp.zeros((B, FULL_SIZE), x.dtype).at[:, :ITER_SIZE].set(1.0)

            def step(carry, _):
                xc, active, history, done = carry
                h = jnp.einsum('btc,fc->btf', xc, Wm) * active[:, None, :]
                h = jax.nn.relu(h)
                x_new = jnp.einsum('btf,cf->btc', h, Wp)
                pooled = x_new.mean(axis=1)
                ck = jnp.einsum('bd,fd->bf', jax.nn.relu(jnp.einsum('bc,dc->bd', pooled, Wc1)), Wc2)
                new_mask = _topk_mask(ck, ITER_SIZE)
                combined = jnp.clip(history + new_mask, 0.0, 1.0)
                novelty = (combined - history).sum(axis=1).mean() / ITER_SIZE
                done_next = jnp.logical_or(done, novelty < R)
                x_out = jnp.where(done, xc, x_new)
                active_out = jnp.where(done, active, new_mask)
                history_out = jnp.where(done, history, combined)
                return ((x_out, active_out, history_out, done_next), None)
            init = (x, base, base, jnp.array(False))
            (x_fin, _, _, _), _ = jax.lax.scan(step, init, None, length=3)
            return x_fin
        return _forward(x, Wm, Wp, Wc1, Wc2)
    x = x + jnp.tanh(g_xattn[0]) * _L0_xattn_ref(_layernorm(x, axis=-1), ctx_1024, L0_xattn_Wq, L0_xattn_Wkv, L0_xattn_Wo, L0_xattn_null_kv, L0_xattn_q_scale, L0_xattn_k_scale, L0_xattn_ln_in_g, L0_xattn_ln_in_b, L0_xattn_ln_ctx_g, L0_xattn_ln_ctx_b, L0_xattn_ln_out_g, L0_xattn_ln_out_b)
    x = x + jnp.tanh(g_ffn[0]) * _L0_ffn_ref(_layernorm(x, axis=-1), L0_ffn_Wm, L0_ffn_Wp, L0_ffn_Wc1, L0_ffn_Wc2)
    return x

_drawn_inputs = setup_inputs


def setup_inputs(seed=0):
    import zlib

    import numpy as np

    out = dict(_drawn_inputs(seed))
    spreads = {'L0_xattn_q_scale': (1.0, 0.2),
     'L0_xattn_k_scale': (1.0, 0.2),
     'L0_xattn_ln_in_g': (1.0, 0.2),
     'L0_xattn_ln_in_b': (0.0, 0.31),
     'L0_xattn_ln_ctx_g': (1.0, 0.2),
     'L0_xattn_ln_ctx_b': (0.0, 0.1),
     'L0_xattn_ln_out_g': (1.0, 0.2),
     'L0_xattn_ln_out_b': (0.0, 0.1)}
    factors = {}
    for name, (base, spread) in spreads.items():
        noise = np.random.default_rng([zlib.crc32(name.encode()), seed]).standard_normal(out[name].shape)
        drawn = base * np.exp(spread * noise) if base else spread * noise
        out[name] = jnp.asarray(drawn.astype(out[name].dtype))
    for name, factor in factors.items():
        out[name] = (out[name] * factor).astype(out[name].dtype)
    return out
```

```python
from contextlib import ExitStack

import concourse.bass as bass
from concourse import mybir

F32 = mybir.dt.float32
F32R = mybir.dt.float32r
I32 = mybir.dt.int32
ALU = mybir.AluOpType
ACT = mybir.ActivationFunctionType
AX = mybir.AxisListType

P = 128
HEADS, HD = 16, 64
SCALE = 8.0
LN_EPS = 1e-5
NORM_EPS = 1e-12
R = 0.7
RSQRT_GUESS = float(0x5F3759DF)
SPREAD = 64


class Chain:

    def __init__(self, eng, sem):
        self.eng, self.sem, self.n = eng, sem, 0

    def do(self, instruction):
        self.n += 1
        instruction.then_inc(self.sem, 1)
        self.eng.wait_ge(self.sem, self.n)


def rsqrt(dve, do, y, v, t):
    yi = y.bitcast(I32)
    do(dve.tensor_scalar(yi, v.bitcast(I32), 1, None, ALU.arith_shift_right))
    do(dve.tensor_scalar(yi, yi, -1.0, RSQRT_GUESS, ALU.mult, ALU.add))
    for _ in range(3):
        do(dve.tensor_tensor(t, y, y, ALU.mult))
        do(dve.scalar_tensor_tensor(t, t, -0.5, v, ALU.mult, ALU.mult))
        do(dve.scalar_tensor_tensor(y, t, 1.5, y, ALU.add, ALU.mult))


def flamingo_block(nc, x, ctx_in, g_xattn, g_ffn, Wq, Wkv, Wo, null_kv, q_scale, k_scale,
                   ln_in_g, ln_in_b, ln_ctx_g, ln_ctx_b, ln_out_g, ln_out_b,
                   WmT, WpT, Wc1T, Wc2T, out):
    B, N, D = x.shape
    J = ctx_in.shape[1]
    KEYS = J + 1
    PACK = HEADS * KEYS
    KT = (PACK + P - 1) // P
    PAIRS = HEADS // 2
    INNER = HEADS * HD
    TILES = B * N // P
    CT = 4
    CW = CT * P
    CH = TILES // CT
    CPB = CH // B
    DK = D // P
    FULL = WmT.shape[1]
    ITER = FULL // 3
    FT = ITER // P
    FTF = FULL // P
    HID = Wc1T.shape[1]
    PAIRW = 2 * KEYS
    PADW = P + PAIRW + P
    rows = [min(P, PACK - P * m) for m in range(KT)]
    NEW_MAX = R * ITER * B

    xt = x.rearrange("b (c k p) d -> (b c) p k d", p=P, k=CT)
    ot = out.rearrange("b (c k p) d -> (b c) p k d", p=P, k=CT)
    wm_v = WmT.rearrange("(k p) f -> p k f", p=P)
    wp_v = WpT.rearrange("(j p) c -> p j c", p=P)

    es = ExitStack()
    with es:
        def sem(name):
            return es.enter_context(nc.semaphore(name))

        LO = 16512
        END = nc.sbuf_usable_end
        top = [LO]

        def place(name, shape, dt, offset=None):
            nbytes = 4
            for s in shape[1:]:
                nbytes *= s
            nbytes = (nbytes + 31) // 32 * 32
            if offset is None:
                offset = top[0]
                top[0] += nbytes
                assert top[0] <= END, (name, top[0], END)
            assert offset + nbytes <= END, name
            return nc.alloc_sbuf_tensor_at(name, shape, dt, offset=offset)

        es.enter_context(nc.sbuf_tensor("fence", [P, (END - LO) // 4 - 8], F32))

        ident = place("ident", [P, P], F32)
        ones_b = place("ones_b", [P, P], F32)
        head_of = place("head_of", [P, PAIRS, HEADS], F32)
        small = place("small", [P, 256], F32)
        G = place("G", [P, D], F32)
        TB = place("TB", [P, D], F32)
        resid = place("resid", [P, TILES, D], F32)
        KB = place("KB", [P, B, PAIRS, PAIRW], F32)
        o_vw = top[0]
        VWh = place("VWh", [P, B, KT, D], F32R)
        VWl = place("VWl", [P, B, KT, D], F32R)
        o_wq = top[0]
        Wqh = place("Wqh", [P, DK, INNER], F32R)
        Wql = place("Wql", [P, DK, INNER], F32R)
        o_q = top[0]
        qT = place("qT", [P, PAIRS, CW], F32)
        o_e = top[0]
        E = place("E", [P, 2, PACK], F32)
        ph = place("ph", [P, KT, P], F32R)
        pl = place("pl", [P, KT, P], F32R)
        z = place("z", [P, CT, D], F32)
        zF = place("zF", [P, CT, D], F32)
        xnh = place("xnh", [P, DK, CW], F32R)
        xnl = place("xnl", [P, DK, CW], F32R)
        xf = place("xf", [P, DK, CW], F32)
        sq = xf
        ob = place("ob", [P, 2, D], F32)
        u = place("u", [P, 2, D], F32)
        top[0] += 256
        o_xc = top[0]
        xch = place("xch", [P, DK, CH * CW], F32R)
        xcl = place("xcl", [P, DK, CH * CW], F32R)
        o_raw = top[0]
        wm_raw = place("wm_raw", [P, DK, ITER], F32)
        wp_raw = place("wp_raw", [P, FT, D], F32)
        Wo_s = place("Wo_s", [P, PAIRS, D], F32)
        VB = place("VB", [P, B, PAIRS, PADW], F32, o_xc)
        cx = place("cx", [J, B, D], F32, o_xc + B * PAIRS * PADW * 4)
        cz = place("cz", [J, B, D], F32, o_xc + B * PAIRS * PADW * 4 + B * D * 4)
        cT = place("cT", [P, DK, B * J], F32, o_xc + B * PAIRS * PADW * 4 + 2 * B * D * 4)
        Wkv_s = place("Wkv_s", [P, DK, 2 * INNER], F32, o_e)
        wq_raw = place("wq_raw", [P, DK, INNER], F32, o_vw)
        kn = place("kn", [KEYS, B, INNER], F32, o_raw)
        ksq = place("ksq", [KEYS, B, INNER], F32, o_raw + B * INNER * 4)
        Wmh = place("Wmh", [P, DK, ITER], F32R, o_wq)
        Wml = place("Wml", [P, DK, ITER], F32R, o_wq + DK * ITER * 4)
        Wph = place("Wph", [P, FT, D], F32R, o_q)
        Wpl = place("Wpl", [P, FT, D], F32R, o_q + FT * D * 4)
        hw = FT * CW * 4
        hh = [place("hh0", [P, FT, CW], F32R, o_vw), place("hh1", [P, FT, CW], F32R, o_q + 2 * hw // 2 * 1)]
        hl = [place("hl0", [P, FT, CW], F32R, o_vw + hw), place("hl1", [P, FT, CW], F32R, o_q + hw + hw)]
        assert o_vw + 2 * hw <= o_wq and o_q + 3 * hw <= o_xc, (o_q + 3 * hw, o_xc)
        yo = place("yo", [P, 2, CT, D], F32, o_raw)
        w_c1 = place("w_c1", [P, DK, HID], F32, o_raw + 2 * FT * D * 4)
        rT = place("rT", [HID, P], F32, o_raw + 2 * FT * D * 4 + DK * HID * 4)
        pooled = place("pooled", [B, D], F32, o_raw + 2 * FT * D * 4 + DK * HID * 4 + P * 4)
        w_c2 = place("w_c2", [HID, FULL], F32, o_q + 3 * hw)
        ck = place("ck", [P, FULL], F32, o_vw + 2 * hw)
        over = place("over", [P, FULL], F32, o_vw + 2 * hw + FULL * 4)
        assert o_vw + 2 * hw + 2 * FULL * 4 <= o_wq + 2 * DK * ITER * 4 and o_q + 3 * hw + FULL * 4 <= o_xc

        ps = es.enter_context(nc.psum_tensor("ps", [P, 8, 512], F32))
        BP = (0, 1)
        BS = (2, 3, 4)
        BT = (5, 6)
        BV = 7
        BY = (2, 7)
        BC = (3, 4)
        GP = 3
        SG = [(g, min(GP, PAIRS - GP * g)) for g in range((PAIRS + GP - 1) // GP)]

        col = {}
        used = [0]

        def cols(name, n):
            col[name] = slice(used[0], used[0] + n)
            used[0] += n
            return small[:, col[name]]

        gates = cols("gates", 2)
        tg = cols("tg", 2)
        in_gb = cols("in_gb", 2 * DK).rearrange("p (a k) -> p a k", a=2)
        cx_gb = cols("cx_gb", 2 * DK).rearrange("p (a k) -> p a k", a=2)
        sc2 = cols("sc2", 2)
        qk = cols("qk", 1)
        nv = cols("nv", 1)
        st_a = cols("st_a", 6)
        mv_a = cols("mv_a", 2)
        nw_a = cols("nw_a", 3)
        st_b = cols("st_b", 6)
        mv_b = cols("mv_b", 2)
        nw_b = cols("nw_b", 3)
        st_z = cols("st_z", 6 * CT).rearrange("p (k s) -> p k s", k=CT)
        mv_z = cols("mv_z", 2 * CT).rearrange("p (k s) -> p k s", k=CT)
        nw_z = cols("nw_z", 3 * CT).rearrange("p (s k) -> p s k", s=3)
        hs = cols("hs", FT * CH).rearrange("p (j c) -> p j c", j=FT)
        hb = cols("hb", FT * B).rearrange("p (j b) -> p j b", j=FT)
        plT = cols("plT", DK * B).rearrange("p (k b) -> p k b", k=DK)
        srch = cols("srch", 16)
        big = place("big", [P, 7 * CT * HEADS], F32)
        rq = big[:, 0:CT * HEADS]
        rqv = big[:, 64:128]
        rqt = big[:, 128:192]
        den = big[:, 192:224].rearrange("p (a h) -> p a h", a=2)
        rden = big[:, 224:256].rearrange("p (a h) -> p a h", a=2)
        kss, krk, krt = big[0:KEYS, 256:288], big[0:KEYS, 288:320], big[0:KEYS, 320:352]
        ssT = place("ssT", [HEADS, CW], F32)
        part_i = place("part_i", [P, 1], I32)
        flag = place("flag", [1, 1], I32)
        g_at = [o_vw - B * PAIRS * PAIRW * 4]

        def later(name, shape, dt=F32):
            nbytes = 4
            for s in shape[1:]:
                nbytes *= s
            nbytes = (nbytes + 31) // 32 * 32
            g_at[0] += nbytes
            assert g_at[0] <= o_q + 3 * hw, name
            return place(name, shape, dt, g_at[0] - nbytes)

        TOK = CH * CW
        gx = later("gx", [P, DK, TOK])
        gn = later("gn", [P, DK, TOK])
        ghm = later("ghm", [P, CH, CW])
        gwm = later("gwm", [P, DK, P])
        gwp = later("gwp", [P, D])
        grow = later("grow", [P, FULL])
        gtmp = later("gtmp", [P, FULL])
        geq = later("geq", [P, FULL])
        gidx = later("gidx", [P, FULL])
        gidx_i = later("gidx_i", [P, FULL], I32)
        gfid = later("gfid", [P, FTF])
        gfid_i = later("gfid_i", [P, FTF], I32)
        gones = later("gones", [P, P])
        gr = later("gr", [HID, B, P])
        gmask = later("gmask", [P, 4, B, FTF])
        g_act, g_hist, g_new, g_comb = (gmask[:, a].rearrange("p b j -> p (b j)") for a in range(4))
        gdiff = later("gdiff", [P, B * FTF])
        gck = later("gck", [P, FTF])
        grank = later("grank", [P, 2, FTF])
        gs = later("gs", [P, 32])
        gout = later("gout", [P, 2, CT, D])

        x_in = [sem(f"x_in{c}") for c in range(CH)]
        wq_in, wkv_in, wo_in, ctx_dma, par_in, nullk_in, wm_in, wc_in = map(
            sem, ("wq_in", "wkv_in", "wo_in", "ctx_dma", "par_in", "nullk_in", "wm_in", "wc_in"))
        y_out = [sem(f"y_out{c}") for c in range(CH)]
        consts = sem("consts")
        zeroed = sem("zeroed")
        pool_chain, dve_chain, act_chain = sem("pool_chain"), sem("dve_chain"), sem("act_chain")
        tanh_done, g_done = sem("tanh_done"), sem("g_done")
        wq_hi, wq_lo = sem("wq_hi"), sem("wq_lo")
        z_ready = sem("z_ready")
        pe_xT, xn_full, xn_hi, xn_lo = map(sem, ("pe_xT", "xn_full", "xn_hi", "xn_lo"))
        pe_q, q_copied, q_squared, pe_ss, ss_copied, pe_rT, sums_read = map(
            sem, ("pe_q", "q_copied", "q_squared", "pe_ss", "ss_copied", "pe_rT", "sums_read"))
        pe_scores, scaled, exped, den_ready, normed = map(
            sem, ("pe_scores", "scaled", "exped", "den_ready", "normed"))
        pe_pT, p_hi, p_lo = sem("pe_pT"), sem("p_hi"), sem("p_lo")
        pe_vw, o_copied, u_ready, x1_ready, zf_ready = map(sem, ("pe_vw", "o_copied", "u_ready", "x1_ready", "zf_ready"))
        pe_cT, xc_hi, xc_lo = sem("pe_cT"), sem("xc_hi"), sem("xc_lo")
        pe_h, h_hi, h_lo, pe_y, y_ready = map(sem, ("pe_h", "h_hi", "h_lo", "pe_y", "y_ready"))
        cz_ready, pe_czT, cT_ready, pe_k, k_copied, k_squared, khat_ready = map(
            sem, ("cz_ready", "pe_czT", "cT_ready", "pe_k", "k_copied", "k_squared", "khat_ready"))
        pe_kT, kb_ready, pe_v, vb_ready, nullv_put, pe_vwp, vw_hi, vw_lo = map(
            sem, ("pe_kT", "kb_ready", "pe_v", "vb_ready", "nullv_put", "pe_vwp", "vw_hi", "vw_lo"))
        wmp_hi, wmp_lo = sem("wmp_hi"), sem("wmp_lo")

        search_pe, search_dve, ck_copied, flag_ready = map(
            sem, ("search_pe", "search_dve", "ck_copied", "flag_ready"))
        g_w, g_h, g_relu, g_y, g_add, g_small, g_pe, g_copy, g_iota, g_out, g_sum = map(
            sem, ("g_w", "g_h", "g_relu", "g_y", "g_add", "g_small", "g_pe", "g_copy", "g_iota", "g_out", "g_sum"))
        G_PE = 1 + 2 * B + 1
        G_SMALL = 2 + B + 3
        held = sem("held")
        g_out2 = [sem(f"g_out{c}") for c in range(CH)]

        VG = [(0, 3), (3, 3), (6, 2)]
        VWJ = [(b, m) for b in range(B) for m in range(0, KT, 2)]

        steps = range(TILES + 3)

        block = es.enter_context(nc.Block())

        def general_dve(dve):
            for c in range(CH):
                dve.wait_ge(y_out[c], 16)
            done, more, nov, nn = (gs[:, n:n + 1] for n in range(4))
            gp = gs[:, 8:8 + DK * B]
            dve.wait_ge(g_iota, 3)
            dve.tensor_copy(gidx[:, :], gidx_i[:, :])
            dve.tensor_copy(gfid[:, :], gfid_i[:, :])
            dve.memset(gones[:, :], 1.0)
            dve.memset(gmask[:, :, :, :], 0.0).then_inc(g_sum, 1)
            dve.memset(done, 0.0)
            dve.wait_ge(g_sum, 1)
            dve.memset(gmask[:, 0:2, :, 0:FT], 1.0).then_inc(g_sum, 1)
            dve.tensor_tensor(gx[:, :, :], xch[:, :, :].bitcast(F32), xcl[:, :, :].bitcast(F32),
                              ALU.add).then_inc(g_small, 1)
            dve.wait_ge(g_small, 1)
            dve.wait_ge(g_sum, 2)
            dve.sem_inc(g_y, CH)
            dve.sem_inc(g_relu, CH)
            dve.sem_inc(g_add, CH)
            K = 24 + 4 * B * FTF
            with dve.Fori(0, 3) as s:
                at = [2]

                def do(ins):
                    at[0] += 1
                    ins.then_inc(g_sum, 1)
                    dve.wait_ge(g_sum, s * K + at[0])

                do(dve.memset(gn[:, :, :], 0.0))
                dve.memset(gs[:, 30:31], 0.0)
                with dve.Fori(0, FTF) as j:
                    n0 = CH * (s * FTF + j)
                    for c in range(CH):
                        dve.wait_ge(g_y, n0 + CH + c + 1)
                        dve.wait_ge(g_add, n0 + c + 1)
                        dst = gn[:, :, CW * c:CW * c + CW]
                        src = ps[:, 4 + 2 * (c % 2):6 + 2 * (c % 2), :]
                        dve.tensor_tensor(dst, dst, src, ALU.add).then_inc(g_add, 1)
                dve.wait_ge(g_add, CH * (s * FTF + FTF) + CH)
                do(dve.tensor_reduce(gp, gn[:, :, :].rearrange("p k (b t) -> p (k b) t", b=B), AX.X, ALU.add))
                dve.tensor_scalar(gp, gp, 1.0 / N, None, ALU.mult).then_inc(g_small, 1)
                dve.wait_ge(g_pe, s * G_PE + 1)
                for b in range(B):
                    do(dve.tensor_scalar(gr[:, b, :], ps[0:HID, 7, b:b + 1].to_broadcast([HID, P]), 0.0, None,
                                         ALU.max))
                dve.sem_inc(g_small, 1)
                for b in range(B):
                    dve.wait_ge(g_pe, s * G_PE + 3 + 2 * b)
                    do(dve.tensor_copy(gck[:, :], ps[:, 6, 0:FTF]))
                    base = at[0]
                    dve.memset(gs[:, 30:31], 0.0)
                    with dve.Fori(0, FTF) as j:
                        def link(ins, i):
                            ins.then_inc(g_sum, 1)
                            dve.wait_ge(g_sum, s * K + j * 4 + (base + i))

                        mine = gck[:, bass.ds(j, 1)]
                        link(dve.tensor_scalar(gtmp[:, :], grow[:, :], mine, None, ALU.is_gt, ALU.add,
                                               accum_out=gs[:, 16:17]), 1)
                        link(dve.tensor_scalar(geq[:, :], grow[:, :], mine, None, ALU.is_equal), 2)
                        link(dve.scalar_tensor_tensor(gtmp[:, :], gidx[:, :], gfid[:, bass.ds(j, 1)], geq[:, :],
                                                      ALU.is_lt, ALU.mult, accum_out=gs[:, 17:18]), 3)
                        link(dve.tensor_tensor(grank[:, 0, bass.ds(j, 1)], gs[:, 16:17], gs[:, 17:18], ALU.add), 4)
                    at[0] += 4 * FTF
                    do(dve.tensor_scalar(gmask[:, 2, b, :], grank[:, 0, :], ITER - 0.5, None, ALU.is_lt))
                    dve.sem_inc(g_small, 1)
                do(dve.tensor_tensor(g_comb, g_hist, g_new, ALU.max))
                do(dve.tensor_tensor(gdiff[:, :], g_comb, g_hist, ALU.subtract))
                do(dve.tensor_reduce(nn, gdiff[:, :], AX.X, ALU.add))
                dve.sem_inc(g_small, 1)
                dve.wait_ge(g_pe, s * G_PE + G_PE)
                do(dve.tensor_scalar(more, done, -1.0, 1.0, ALU.mult, ALU.add))
                do(dve.tensor_scalar(gn[:, :, :], gn[:, :, :], more, None, ALU.mult))
                do(dve.scalar_tensor_tensor(gx[:, :, :], gx[:, :, :], done, gn[:, :, :], ALU.mult, ALU.add))
                for old, new in ((g_act, g_new), (g_hist, g_comb)):
                    do(dve.tensor_scalar(new, new, more, None, ALU.mult))
                    do(dve.scalar_tensor_tensor(old, old, done, new, ALU.mult, ALU.add))
                do(dve.tensor_scalar(nov, ps[:, 7, 0:1], NEW_MAX, None, ALU.is_lt))
                do(dve.tensor_tensor(done, done, nov, ALU.max))
                while at[0] < 2 + K:
                    do(dve.memset(gs[:, 31:32], 0.0))
                dve.sem_inc(g_small, 2)
            for t in range(TILES):
                dve.wait_ge(g_pe, 3 * G_PE + t + 1)
                if t >= 2 * CT:
                    dve.wait_ge(g_out2[t // CT - 2], 16)
                dve.scalar_tensor_tensor(gout[:, t // CT % 2, t % CT, :], ps[:, t % 2, 0:D], tg[:, 1:2],
                                         resid[:, t, :], ALU.mult, ALU.add).then_inc(g_out, 1)

        @block.sync
        def _(sp):
            sp.dma_start(resid[:, 0:CT, :], xt[0]).then_inc(x_in[0], 16)
            sp.dma_start(wq_raw[:, :, :], Wq.rearrange("(k p) n -> p k n", p=P)).then_inc(wq_in, 16)
            sp.dma_start(cx[:, :, :], ctx_in.rearrange("b j d -> j b d")).then_inc(ctx_dma, 16)
            sp.dma_start(Wkv_s[:, :, :], Wkv.rearrange("(k p) n -> p k n", p=P)).then_inc(wkv_in, 16)
            sp.dma_start(Wo_s[:, :, :], Wo.rearrange("(i p) n -> p i n", p=P)).then_inc(wo_in, 16)
            for c in range(1, CH):
                sp.dma_start(resid[:, CT * c:CT * c + CT, :], xt[c]).then_inc(x_in[c], 16)
            sp.wait_ge(pe_kT, B * PAIRS)
            sp.dma_start(wm_raw[:, :, :], wm_v[:, :, 0:ITER]).then_inc(wm_in, 16)
            sp.dma_start(wp_raw[:, :, :], wp_v[:, 0:FT, :]).then_inc(wm_in, 16)
            sp.wait_ge(pe_vwp, len(VWJ))
            with nc.allow_non_contiguous_dma(reason="rows of 256 bytes"):
                sp.dma_start(w_c1[:, :, :], Wc1T.rearrange("(k p) h -> p k h", p=P)).then_inc(wc_in, 16)
            sp.wait_ge(x1_ready, TILES)
            sp.wait_ge(pe_q, CH * PAIRS)
            sp.dma_start(w_c2[:, :], Wc2T).then_inc(wc_in, 16)
            for c in range(CH):
                sp.wait_ge(y_ready, CT * c + CT)
                sp.dma_start(ot[c], yo[:, c % 2, :, :]).then_inc(y_out[c], 16)
            for c in range(CH):
                sp.wait_ge(y_out[c], 16)
            sp.wait_ge(flag_ready, 1)
            go = sp.value_load(flag[0:1, 0:1])
            with sp.If(go > 0):
                with sp.Fori(0, 3) as s:
                    with sp.Fori(0, FTF) as j:
                        sp.wait_ge(g_y, CH * (s * FTF + j) + CH)
                        sp.dma_start(gwm[:, :, :], wm_v[:, :, bass.ds(j * P, P)]).then_inc(g_w, 16)
                        sp.dma_start(gwp[:, :], WpT[bass.ds(j * P, P), :]).then_inc(g_w, 16)
                for c in range(CH):
                    sp.wait_ge(g_out, CT * c + CT)
                    sp.dma_start(ot[c], gout[:, c % 2, :, :]).then_inc(g_out2[c], 16)
                for c in range(CH):
                    sp.wait_ge(g_out2[c], 16)
            with sp.Else():
                sp.nop()

        @block.gpsimd
        def _(pool):
            do = Chain(pool, pool_chain).do
            with nc.allow_non_contiguous_dma(reason="columns of parameters"):
                pool.dma_start(gates[:, 0:1], g_xattn.partition_broadcast(P)).then_inc(par_in, 16)
                pool.dma_start(gates[:, 1:2], g_ffn.partition_broadcast(P)).then_inc(par_in, 16)
                pool.dma_start(G[:, :], ln_out_g.partition_broadcast(P)).then_inc(par_in, 16)
                pool.dma_start(TB[:, :], ln_out_b.partition_broadcast(P)).then_inc(par_in, 16)
                for a, src in enumerate((ln_in_g, ln_in_b)):
                    pool.dma_start(in_gb[:, a, :], src.rearrange("(k p) -> p k", p=P)).then_inc(par_in, 16)
                for a, src in enumerate((ln_ctx_g, ln_ctx_b)):
                    pool.dma_start(cx_gb[:, a, :], src.rearrange("(k p) -> p k", p=P)).then_inc(par_in, 16)
                for s in range(2):
                    half = slice(HD * s, HD * s + HD)
                    pool.dma_start(sc2[half, 0:1], q_scale.rearrange("(p o) -> p o", o=1)).then_inc(par_in, 16)
                    pool.dma_start(sc2[half, 1:2], k_scale.rearrange("(p o) -> p o", o=1)).then_inc(par_in, 16)
                    pool.dma_start(nv[half, :], null_kv[1, :].rearrange("(p o) -> p o", o=1)).then_inc(par_in, 16)
            do(pool.memset(ident[:, :], 0.0))
            pool.affine_select(out=ident[:, :], in_=ident[:, :], compare_op=ALU.not_equal, fill=1.0,
                               base=0, pattern=[[-1, P]], channel_multiplier=1).then_inc(consts, 1)
            do(pool.memset(head_of[:, :, :], 0.0))
            for s in range(2):
                for i in range(PAIRS):
                    do(pool.memset(head_of[HD * s:HD * s + HD, i, 2 * i + s:2 * i + s + 1], 1.0))
            do(pool.memset(ones_b[:, :], 0.0))
            for s in range(2):
                do(pool.memset(ones_b[HD * s:HD * s + HD, HD * s:HD * s + HD], 1.0))
            pool.memset(VB[:, :, :, :], 0.0).then_inc(zeroed, 1)
            pool.memset(KB[:, :, :, :], 0.0).then_inc(zeroed, 1)
            pool.iota(part_i[:, :], pattern=[[0, 1]], base=0, channel_multiplier=1).then_inc(g_iota, 1)
            with nc.allow_non_contiguous_dma(reason="the null key for every head"):
                for b in range(B):
                    pool.dma_start(kn[J:KEYS, b, :].rearrange("o (h d) -> o h d", h=HEADS),
                                   null_kv[0:1, :].unsqueeze(1).to_broadcast([1, HEADS, HD])).then_inc(nullk_in, 16)
            pool.wait_ge(tanh_done, 1)
            pool.wait_ge(par_in, 16 * 14)
            gx = tg[:, 0:1]
            pool.tensor_scalar(G[:, :], G[:, :], gx, None, ALU.mult).then_inc(g_done, 1)
            pool.tensor_scalar(TB[:, :], TB[:, :], gx, None, ALU.mult).then_inc(g_done, 1)
            pool.wait_ge(g_done, 2)

            def xn_low(c):
                for k in range(DK):
                    pool.wait_ge(xn_full, DK * c + k + 1)
                    pool.wait_ge(xn_hi, DK * c + k + 1)
                    pool.tensor_tensor(xnl[:, k, :], xf[:, k, :], xnh[:, k, :].bitcast(F32),
                                       ALU.subtract).then_inc(xn_lo, 1)

            for t in steps:
                c, k = t // CT, t % CT
                if k == 0 and c < CH:
                    xn_low(c)
                if t < TILES:
                    pool.wait_ge(den_ready, t + 1)
                    pool.tensor_tensor(
                        E[:, t % 2, :].rearrange("p (h j) -> p h j", h=HEADS),
                        E[:, t % 2, :].rearrange("p (h j) -> p h j", h=HEADS),
                        rden[:, t % 2, :].unsqueeze(2).to_broadcast([P, HEADS, KEYS]),
                        ALU.mult).then_inc(normed, 1)
                if 0 <= t - 2 < TILES:
                    s = t - 2
                    pool.wait_ge(u_ready, s + 1)
                    do(pool.tensor_tensor(u[:, s % 2, :], u[:, s % 2, :], G[:, :], ALU.mult))
                    do(pool.tensor_tensor(u[:, s % 2, :], u[:, s % 2, :], TB[:, :], ALU.add))
                    pool.tensor_tensor(resid[:, s, :], resid[:, s, :], u[:, s % 2, :],
                                       ALU.add).then_inc(x1_ready, 1)

            pool.wait_ge(flag_ready, 1)
            go = pool.value_load(flag[0:1, 0:1])
            with pool.If(go > 0):
                pool.iota(gidx_i[:, :], pattern=[[1, FULL]], base=0, channel_multiplier=0).then_inc(g_iota, 1)
                pool.iota(gfid_i[:, :], pattern=[[P, FTF]], base=0, channel_multiplier=1).then_inc(g_iota, 1)
                pool.wait_ge(g_iota, 3)
            with pool.Else():
                pool.nop()

        @block.scalar
        def _(act):
            act.wait_ge(par_in, 16 * 14)
            act.activation(tg, gates, ACT.Tanh).then_inc(tanh_done, 1)
            act.wait_ge(wq_in, 16)
            for k in range(DK):
                act.activation(Wqh[:, k, :], wq_raw[:, k, :], ACT.Copy).then_inc(wq_hi, 1)

            def setup():
                for b in range(B):
                    for n in range(2):
                        act.wait_ge(pe_k, 2 * b + n + 1)
                        act.activation(kn[0:J, b, 512 * n:512 * n + 512], ps[0:J, BP[n], :],
                                       ACT.Copy).then_inc(k_copied, 1)
                act.wait_ge(k_copied, 2 * B)
                act.wait_ge(nullk_in, 16 * B)
                act.activation(ksq[:, :, :], kn[:, :, :], ACT.Square).then_inc(k_squared, 1)
                act.wait_ge(zeroed, 1)
                for g, (i0, n) in enumerate(VG):
                    act.wait_ge(pe_v, g + 1)
                    for s in range(2):
                        half = slice(HD * s, HD * s + HD)
                        src = ps[half, BS[g], 0:n * B * J].rearrange("p (i b j) -> p i b j", i=n, b=B)
                        at = P + KEYS * s
                        for b in range(B):
                            act.activation(VB[half, b, i0:i0 + n, at:at + J], src[:, :, b, :],
                                           ACT.Copy).then_inc(vb_ready, 1)
                for n, (b, m) in enumerate(VWJ):
                    act.wait_ge(pe_vwp, n + 1)
                    for r in range(2):
                        act.activation(VWh[0:rows[m + r], b, m + r, :],
                                       ps[0:rows[m + r], BP[n % 2], D * r:D * r + D],
                                       ACT.Copy).then_inc(vw_hi, 1)

            def begin(c):
                for k in range(DK):
                    act.wait_ge(xn_full, DK * c + k + 1)
                    act.activation(xnh[:, k, :], xf[:, k, :], ACT.Copy).then_inc(xn_hi, 1)
                act.wait_ge(xn_lo, DK * c + DK)
                for i in range(PAIRS):
                    n = PAIRS * c + i
                    act.wait_ge(pe_q, n + 1)
                    act.activation(qT[:, i, :], ps[:, BP[i % 2], :], ACT.Copy).then_inc(q_copied, 1)
                    if i >= 2:
                        act.wait_ge(pe_ss, n - 1)
                    act.activation(sq[:, i % 2, :], ps[:, BP[i % 2], :], ACT.Square).then_inc(q_squared, 1)

            def xc_high(cc):
                for h in range(DK):
                    act.wait_ge(pe_cT, DK * cc + h + 1)
                    bank = BP[h] if cc < CH - 1 else BC[h]
                    act.activation(xch[:, h, CW * cc:CW * cc + CW], ps[:, bank, :], ACT.Copy).then_inc(xc_hi, 1)

            for t in steps:
                c, k = t // CT, t % CT
                if k == 0 and c < CH:
                    begin(c)
                    if c == 0:
                        setup()
                if t < TILES:
                    act.wait_ge(scaled, t + 1)
                    act.activation(E[:, t % 2, :], E[:, t % 2, :], ACT.Exp).then_inc(exped, 1)
                if 0 <= t - 2 < TILES:
                    act.wait_ge(pe_vw, t - 1)
                    if t - 2 >= 2:
                        act.wait_ge(u_ready, t - 3)
                    act.activation(ob[:, t % 2, :], ps[:, BV, 0:D], ACT.Copy).then_inc(o_copied, 1)
                if k == 3 and 1 <= c < CH:
                    xc_high(c - 1)
                if 0 <= t - 1 < TILES:
                    for g in range(3):
                        n = 3 * (t - 1) + g
                        kt = [4 * g, min(4 * g + 4, KT)]
                        act.wait_ge(pe_pT, n + 1)
                        for m in range(kt[0], kt[1]):
                            pass
                        w = kt[1] - kt[0]
                        if kt[1] == KT:
                            act.activation(ph[:, kt[0]:KT - 1, :],
                                           ps[:, BT[n % 2], 0:P * (w - 1)].rearrange("p (m t) -> p m t", t=P),
                                           ACT.Copy).then_inc(p_hi, 1)
                            r = rows[-1]
                            act.activation(ph[0:r, KT - 1, :], ps[0:r, BT[n % 2], P * (w - 1):P * w],
                                           ACT.Copy).then_inc(p_hi, 1)
                        else:
                            act.activation(ph[:, kt[0]:kt[1], :],
                                           ps[:, BT[n % 2], 0:P * w].rearrange("p (m t) -> p m t", t=P),
                                           ACT.Copy).then_inc(p_hi, 1)
                if t == TILES:
                    act.wait_ge(wm_in, 32)
                    for h in range(DK):
                        act.activation(Wmh[:, h, :], wm_raw[:, h, :], ACT.Copy).then_inc(wmp_hi, 1)
                    act.wait_ge(pe_scores, TILES)
                    for h in range(2):
                        act.activation(Wph[:, 4 * h:4 * h + 4, :], wp_raw[:, 4 * h:4 * h + 4, :],
                                       ACT.Copy).then_inc(wmp_hi, 1)

            for f in range(CH):
                for j in range(FT):
                    n = FT * f + j
                    act.wait_ge(pe_h, n + 1)
                    act.activation(hh[f % 2][:, j, :], ps[:, (BP + BT)[n % 4], :], ACT.Relu,
                                   accum_out=hs[:, j, f:f + 1]).then_inc(h_hi, 1)
                if f == 0:
                    xc_high(CH - 1)
            act.wait_ge(search_pe, 4)
            act.wait_ge(h_lo, FT * CH)
            act.activation(ck[:, 0:1024], ps[:, 0:2, :].rearrange("p b n -> p (b n)"), ACT.Copy).then_inc(ck_copied, 1)
            act.activation(ck[:, 1024:2048], ps[:, 5:7, :].rearrange("p b n -> p (b n)"), ACT.Copy).then_inc(ck_copied, 1)
            act.activation(ck[:, 2048:3072], ps[:, 3:5, :].rearrange("p b n -> p (b n)"), ACT.Copy).then_inc(ck_copied, 1)

            act.wait_ge(flag_ready, 1)
            go = act.value_load(flag[0:1, 0:1])
            with act.If(go > 0):
                with act.Fori(0, 3) as s:
                    with act.Fori(0, FTF) as j:
                        for c in range(CH):
                            act.wait_ge(g_h, CH * (s * FTF + j) + c + 1)
                            act.wait_ge(g_y, CH * (s * FTF + j) + CH)
                            act.sem_inc(held, 1)
                            act.activation(ghm[:, c, :], ps[:, c, :], ACT.Relu,
                                           scale=gmask[:, 0, c // CPB, bass.ds(j, 1)]).then_inc(g_relu, 1)
                    for b in range(B):
                        act.wait_ge(g_pe, s * G_PE + 2 + 2 * b)
                        act.activation(grow[:, :], ps[:, 0:6, :].rearrange("p b n -> p (b n)"),
                                       ACT.Copy).then_inc(g_copy, 1)
            with act.Else():
                act.nop()

        @block.vector
        def _(dve):
            do = Chain(dve, dve_chain).do

            def norm_rows(stats, mv, nw, v, n):
                do(dve.bn_stats(stats, v))
                do(dve.bn_aggr(mv, stats))
                do(dve.tensor_scalar(nw[0:n, 0:1], mv[0:n, 1:2], LN_EPS, None, ALU.add))
                rsqrt(dve, do, nw[0:n, 1:2], nw[0:n, 0:1], nw[0:n, 2:3])

            def first_norm(c):
                dve.wait_ge(x_in[c], 16)
                for k in range(CT):
                    do(dve.bn_stats(st_z[:, k, :], resid[:, CT * c + k, :]))
                    do(dve.bn_aggr(mv_z[:, k, :], st_z[:, k, :]))
                do(dve.tensor_scalar(nw_z[:, 0, :], mv_z[:, :, 1], 1.0 + LN_EPS, LN_EPS * LN_EPS, ALU.mult, ALU.add))
                rsqrt(dve, do, nw_z[:, 1, :], nw_z[:, 0, :], nw_z[:, 2, :])
                if c >= 1:
                    dve.wait_ge(pe_xT, DK * c)
                for k in range(CT):
                    dve.tensor_scalar(z[:, k, :], resid[:, CT * c + k, :], mv_z[:, k, 0:1], nw_z[:, 1, k:k + 1],
                                      ALU.subtract, ALU.mult).then_inc(z_ready, 1)

            def begin(c):
                for k in range(DK):
                    dve.wait_ge(pe_xT, DK * c + k + 1)
                    dve.tensor_scalar(xf[:, k, :], ps[:, BP[k], :], in_gb[:, 0, k:k + 1], in_gb[:, 1, k:k + 1],
                                      ALU.mult, ALU.add).then_inc(xn_full, 1)

            def query_norms(c):
                dve.wait_ge(pe_ss, PAIRS * c + PAIRS)
                dve.tensor_copy(ssT[:, :], ps[0:HEADS, BS[2], :]).then_inc(ss_copied, 1)

            def invert_norms(c):
                dve.wait_ge(pe_rT, c + 1)
                dve.tensor_scalar(rqv, ps[:, BP[0], 0:CT * HEADS], NORM_EPS * NORM_EPS, None,
                                  ALU.max).then_inc(sums_read, 1)
                dve.wait_ge(sums_read, c + 1)
                rsqrt(dve, do, rq, rqv, rqt)

            def scale_scores(t):
                k = t % CT
                dve.wait_ge(pe_scores, t + 1)
                for g, n in SG:
                    w = 2 * n
                    last = dve.tensor_tensor(
                        E[:, t % 2, PAIRW * GP * g:PAIRW * (GP * g + n)].rearrange("p (h j) -> p h j", h=w),
                        ps[:, BS[g], 0:PAIRW * n].rearrange("p (h j) -> p h j", h=w),
                        rq[:, HEADS * k + 2 * GP * g:HEADS * k + 2 * GP * g + w].unsqueeze(2).to_broadcast([P, w, KEYS]),
                        ALU.mult)
                    last.then_inc(scaled, 1) if g == len(SG) - 1 else None

            def sum_exps(t):
                dve.wait_ge(exped, t + 1)
                do(dve.tensor_reduce(den[:, t % 2, :], E[:, t % 2, :].rearrange("p (h j) -> p h j", h=HEADS),
                                     AX.X, ALU.add))
                dve.reciprocal(rden[:, t % 2, :], den[:, t % 2, :]).then_inc(den_ready, 1)

            def out_norm(t):
                v = ob[:, t % 2, :]
                dve.wait_ge(o_copied, t + 1)
                norm_rows(st_a, mv_a, nw_a, v, P)
                if t >= 2:
                    dve.wait_ge(x1_ready, t - 1)
                dve.tensor_scalar(u[:, t % 2, :], v, mv_a[:, 0:1], nw_a[:, 1:2],
                                  ALU.subtract, ALU.mult).then_inc(u_ready, 1)

            def ffn_norm(t):
                dve.wait_ge(x1_ready, t + 1)
                norm_rows(st_b, mv_b, nw_b, resid[:, t, :], P)
                if t >= CT:
                    dve.wait_ge(pe_cT, DK * (t // CT))
                dve.tensor_scalar(zF[:, t % CT, :], resid[:, t, :], mv_b[:, 0:1], nw_b[:, 1:2],
                                  ALU.subtract, ALU.mult).then_inc(zf_ready, 1)

            def probs_low(t):
                for g in range(3):
                    n = 3 * t + g
                    k0, k1 = 4 * g, min(4 * g + 4, KT)
                    w = k1 - k0
                    dve.wait_ge(p_hi, 4 * t + g + 1 if g < 2 else 4 * t + 4)
                    if k1 == KT:
                        r = rows[-1]
                        dve.tensor_tensor(pl[:, k0:KT - 1, :],
                                          ps[:, BT[n % 2], 0:P * (w - 1)].rearrange("p (m t) -> p m t", t=P),
                                          ph[:, k0:KT - 1, :].bitcast(F32), ALU.subtract).then_inc(p_lo, 1)
                        dve.tensor_tensor(pl[0:r, KT - 1, :], ps[0:r, BT[n % 2], P * (w - 1):P * w],
                                          ph[0:r, KT - 1, :].bitcast(F32), ALU.subtract).then_inc(p_lo, 1)
                    else:
                        dve.tensor_tensor(pl[:, k0:k1, :],
                                          ps[:, BT[n % 2], 0:P * w].rearrange("p (m t) -> p m t", t=P),
                                          ph[:, k0:k1, :].bitcast(F32), ALU.subtract).then_inc(p_lo, 1)

            def xc_low(cc):
                for h in range(DK):
                    bank = BP[h] if cc < CH - 1 else BC[h]
                    dve.wait_ge(xc_hi, DK * cc + h + 1)
                    dve.tensor_tensor(xcl[:, h, CW * cc:CW * cc + CW], ps[:, bank, :],
                                      xch[:, h, CW * cc:CW * cc + CW].bitcast(F32), ALU.subtract).then_inc(xc_lo, 1)

            def setup():
                dve.wait_ge(ctx_dma, 16)
                for b in range(B):
                    norm_rows(st_a[0:J, :], mv_a[0:J, :], nw_a, cx[:, b, :], J)
                    do(dve.tensor_scalar(cz[:, b, :], cx[:, b, :], mv_a[0:J, 0:1], nw_a[0:J, 1:2],
                                         ALU.subtract, ALU.mult))
                dve.tensor_scalar(qk, sc2[:, 0:1], sc2[:, 1:2], SCALE, ALU.mult, ALU.mult).then_inc(cz_ready, 1)
                dve.wait_ge(pe_czT, 1)
                for k in range(DK):
                    dve.tensor_scalar(cT[:, k, :], ps[:, BT[0], B * J * k:B * J * k + B * J],
                                      cx_gb[:, 0, k:k + 1], cx_gb[:, 1, k:k + 1],
                                      ALU.mult, ALU.add).then_inc(cT_ready, 1)
                dve.wait_ge(zeroed, 2)
                for s in range(2):
                    half = slice(HD * s, HD * s + HD)
                    at = P + KEYS * s + J
                    dst = VB[half, :, :, at:at + 1].rearrange("p b i o -> p (b i) o")
                    dve.tensor_copy(dst, nv[half, :].unsqueeze(1).to_broadcast([HD, B * PAIRS, 1])).then_inc(nullv_put, 1)
                dve.wait_ge(k_squared, 1)
                do(dve.tensor_reduce(krt, ksq[:, :, :].rearrange("p b (h d) -> p (b h) d", d=HD), AX.X, ALU.add))
                do(dve.tensor_scalar(kss, krt, NORM_EPS * NORM_EPS, None, ALU.max))
                rsqrt(dve, do, krk, kss, krt)
                kv = kn[:, :, :].rearrange("p b (h d) -> p (b h) d", d=HD)
                dve.tensor_tensor(kv, kv, krk.unsqueeze(2).to_broadcast([KEYS, B * HEADS, HD]),
                                  ALU.mult).then_inc(khat_ready, 1)
                for b in range(B):
                    for g in range(2):
                        dve.wait_ge(pe_kT, PAIRS * b + 4 * g + 4)
                        for s in range(2):
                            half = slice(HD * s, HD * s + HD)
                            dve.tensor_scalar(KB[half, b, 4 * g:4 * g + 4, KEYS * s:KEYS * s + KEYS],
                                              ps[half, BT[g], 0:4 * KEYS].rearrange("p (i j) -> p i j", i=4),
                                              qk[half, :], None, ALU.mult).then_inc(kb_ready, 1)
                for n, (b, m) in enumerate(VWJ):
                    dve.wait_ge(vw_hi, 2 * n + 2)
                    for r in range(2):
                        rr = rows[m + r]
                        dve.tensor_tensor(VWl[0:rr, b, m + r, :], ps[0:rr, BP[n % 2], D * r:D * r + D],
                                          VWh[0:rr, b, m + r, :].bitcast(F32), ALU.subtract).then_inc(vw_lo, 1)

            dve.wait_ge(par_in, 16 * 14)
            first_norm(0)
            dve.wait_ge(wq_hi, DK)
            for k in range(DK):
                dve.tensor_tensor(Wql[:, k, :], wq_raw[:, k, :], Wqh[:, k, :].bitcast(F32),
                                  ALU.subtract).then_inc(wq_lo, 1)
            for t in steps:
                c, k = t // CT, t % CT
                if k == 0 and c < CH:
                    begin(c)
                    query_norms(c)
                    if c == 0:
                        setup()
                    invert_norms(c)
                if t < TILES:
                    scale_scores(t)
                if 0 <= t - 3 < TILES:
                    ffn_norm(t - 3)
                if k == 3 and 1 <= c < CH:
                    xc_low(c - 1)
                if t < TILES:
                    sum_exps(t)
                if 0 <= t - 2 < TILES:
                    out_norm(t - 2)
                if 0 <= t - 1 < TILES:
                    probs_low(t - 1)
                if k == 3 and c + 1 < CH:
                    first_norm(c + 1)
                if t == TILES:
                    dve.wait_ge(wmp_hi, DK)
                    for h in range(DK):
                        dve.tensor_tensor(Wml[:, h, :], wm_raw[:, h, :], Wmh[:, h, :].bitcast(F32),
                                          ALU.subtract).then_inc(wmp_lo, 1)
                    dve.wait_ge(wmp_hi, DK + 2)
                    for h in range(2):
                        dve.tensor_tensor(Wpl[:, 4 * h:4 * h + 4, :], wp_raw[:, 4 * h:4 * h + 4, :],
                                          Wph[:, 4 * h:4 * h + 4, :].bitcast(F32), ALU.subtract).then_inc(wmp_lo, 1)
            def h_low(f):
                for j in range(FT):
                    n = FT * f + j
                    dve.wait_ge(h_hi, n + 1)
                    dve.scalar_tensor_tensor(hl[f % 2][:, j, :], ps[:, (BP + BT)[n % 4], :], 0.0,
                                             hh[f % 2][:, j, :].bitcast(F32), ALU.max, ALU.subtract).then_inc(h_lo, 1)

            def add_ffn(f):
                if f >= 2:
                    dve.wait_ge(y_out[f - 2], 16)
                for k in range(CT):
                    t = CT * f + k
                    dve.wait_ge(pe_y, t + 1)
                    dve.scalar_tensor_tensor(yo[:, f % 2, k, :], ps[:, BY[t % 2], 0:D], tg[:, 1:2],
                                             resid[:, t, :], ALU.mult, ALU.add).then_inc(y_ready, 1)

            h_low(0)
            xc_low(CH - 1)
            add_ffn(0)
            h_low(1)
            add_ffn(1)
            h_low(2)
            h_low(3)
            dve.tensor_reduce(hb[:, :, :], hs[:, :, :].rearrange("p j (b c) -> p j b c", b=B), AX.X,
                              ALU.add).then_inc(search_dve, 1)
            add_ffn(2)
            bm, lo, w, pid, thr, cnt, ind, c_old, c_new, short = (srch[:, n:n + 1] for n in range(10))
            dve.wait_ge(search_pe, 1)
            dve.tensor_scalar(pooled[:, :], ps[0:B, BC[0], 0:D], 1.0 / N, None, ALU.mult).then_inc(search_dve, 1)
            dve.wait_ge(search_pe, 2)
            dve.tensor_copy(plT[:, :, :].rearrange("p k b -> p (k b)"), ps[:, BC[1], 0:DK * B]).then_inc(search_dve, 1)
            dve.wait_ge(search_pe, 3)
            for b in range(B):
                dve.tensor_scalar(rT[:, HD * b:HD * b + HD], ps[0:HID, BC[0], b:b + 1].to_broadcast([HID, HD]),
                                  0.0, None, ALU.max).then_inc(search_dve, 1)
            add_ffn(3)
            dve.wait_ge(g_iota, 1)
            do(dve.tensor_copy(pid, part_i[:, :]))
            do(dve.tensor_scalar(thr, pid, SPREAD - 0.5, -float(SPREAD), ALU.is_gt, ALU.mult))
            do(dve.scalar_tensor_tensor(pid, pid, 1.0, thr, ALU.add, ALU.add))
            dve.wait_ge(ck_copied, 3)
            do(dve.tensor_reduce(bm, ck[:, :], AX.X, ALU.max, apply_absolute_value=True))
            do(dve.tensor_scalar(lo, bm, -1.01, -1e-30, ALU.mult, ALU.add))
            do(dve.tensor_scalar(w, bm, 2.02 / SPREAD, 2e-30 / SPREAD, ALU.mult, ALU.add))
            for n in range(2):
                do(dve.tensor_scalar(thr, pid, w, lo, ALU.mult, ALU.add))
                do(dve.tensor_scalar(over[:, :], ck[:, :], thr, None, ALU.is_gt, ALU.add, accum_out=cnt))
                dve.tensor_scalar(ind, cnt, ITER - 0.5, None, ALU.is_gt).then_inc(search_dve, 1)
                dve.wait_ge(search_pe, 5 + n)
                do(dve.tensor_scalar(lo, ps[:, BC[0], 0:1], w, lo, ALU.mult, ALU.add))
                do(dve.tensor_scalar(w, w, 1.0 / SPREAD, None, ALU.mult))
            do(dve.tensor_scalar(over[:, 0:ITER], ck[:, 0:ITER], lo, None, ALU.is_gt, ALU.add, accum_out=c_old))
            do(dve.tensor_scalar(over[:, ITER:FULL], ck[:, ITER:FULL], lo, None, ALU.is_gt, ALU.add, accum_out=c_new))
            do(dve.tensor_tensor(cnt, c_old, c_new, ALU.add))
            dve.tensor_scalar(short, cnt, ITER - 0.5, None, ALU.is_lt).then_inc(search_dve, 1)
            dve.wait_ge(search_pe, 7)
            do(dve.tensor_copy(srch[0:1, 10:12], ps[0:1, BC[1], 0:2]))
            do(dve.tensor_scalar(srch[0:1, 12:13], srch[0:1, 11:12], float(FULL), srch[0:1, 10:11],
                                 ALU.mult, ALU.add))
            dve.tensor_scalar(flag[:, :], srch[0:1, 12:13], NEW_MAX, None, ALU.is_gt).then_inc(flag_ready, 1)
            dve.wait_ge(flag_ready, 1)

            go = dve.value_load(flag[0:1, 0:1])
            with dve.If(go > 0):
                general_dve(dve)
            with dve.Else():
                dve.nop()

        @block.tensor
        def _(pe):
            def three(dst, lh, ll, rh, rl, first, last):
                pe.matmul(dst, lh, rh, start=first, stop=False)
                pe.matmul(dst, lh, rl, start=False, stop=False)
                return pe.matmul(dst, ll, rh, start=False, stop=last)

            def begin(c):
                if c == 0:
                    pe.wait_ge(consts, 1)
                if c >= 2:
                    pe.wait_ge(xc_lo, DK * (c - 1))
                elif c == 1:
                    pe.wait_ge(sums_read, 1)
                for h in range(DK):
                    for k in range(CT):
                        if h == 0:
                            pe.wait_ge(z_ready, CT * c + k + 1)
                        mm = pe.transpose(ps[:, BP[h], P * k:P * k + P], z[:, k, P * h:P * h + P], ident[:, :])
                    mm.then_inc(pe_xT, 1)
                pe.wait_ge(xn_hi, DK * c + DK)
                pe.wait_ge(xn_lo, DK * c + DK)
                if c == 0:
                    pe.wait_ge(wq_lo, DK)
                    pe.wait_ge(wq_hi, DK)
                    pe.wait_ge(consts, 1)
                    pe.wait_ge(pool_chain, 4 + 2 * PAIRS)
                if c >= 1:
                    pe.wait_ge(scaled, CT * c)

                def sums(i):
                    pe.wait_ge(q_squared, PAIRS * c + i + 1)
                    pe.matmul(ps[0:HEADS, BS[2], :], head_of[:, i, :], sq[:, i % 2, :],
                              start=i == 0, stop=i == PAIRS - 1).then_inc(pe_ss, 1)

                for i in range(PAIRS):
                    if i >= 2:
                        pe.wait_ge(q_squared, PAIRS * c + i - 1)
                    for k in range(DK):
                        w = slice(P * i, P * i + P)
                        mm = three(ps[:, BP[i % 2], :], Wqh[:, k, w], Wql[:, k, w], xnh[:, k, :], xnl[:, k, :],
                                   k == 0, k == DK - 1)
                    mm.then_inc(pe_q, 1)
                    if i:
                        sums(i - 1)
                sums(PAIRS - 1)
                if c == 0:
                    setup()
                pe.wait_ge(ss_copied, c + 1)
                for k in range(CT):
                    mm = pe.transpose(ps[:, BP[0], HEADS * k:HEADS * k + HEADS], ssT[:, P * k:P * k + P],
                                      ident[0:HEADS, 0:HEADS])
                mm.then_inc(pe_rT, 1)

            def setup():
                pe.wait_ge(cz_ready, 1)
                for k in range(DK):
                    for b in range(B):
                        mm = pe.transpose(ps[:, BT[0], J * (B * k + b):J * (B * k + b) + J],
                                          cz[:, b, P * k:P * k + P], ident[0:J, 0:J])
                mm.then_inc(pe_czT, 1)
                pe.wait_ge(cT_ready, DK)
                pe.wait_ge(wkv_in, 16)
                pe.wait_ge(q_squared, PAIRS)
                for b in range(B):
                    for n in range(2):
                        if b:
                            pe.wait_ge(k_copied, 2 * b - 1 + n)
                        for k in range(DK):
                            mm = pe.matmul(ps[0:J, BP[n], :], cT[:, k, J * b:J * b + J],
                                           Wkv_s[:, k, 512 * n:512 * n + 512], start=k == 0, stop=k == DK - 1)
                        mm.then_inc(pe_k, 1)
                pe.wait_ge(ss_copied, 1)
                for g, (i0, n) in enumerate(VG):
                    for i in range(n):
                        for k in range(DK):
                            at = INNER + P * (i0 + i)
                            mm = pe.matmul(ps[:, BS[g], B * J * i:B * J * i + B * J], Wkv_s[:, k, at:at + P],
                                           cT[:, k, :], start=k == 0, stop=k == DK - 1)
                    mm.then_inc(pe_v, 1)
                pe.wait_ge(khat_ready, 1)
                for b in range(B):
                    for i in range(PAIRS):
                        if b and i % 4 == 0:
                            pe.wait_ge(kb_ready, 2 * (i // 4) + 2)
                        pe.transpose(ps[:, BT[i // 4], KEYS * (i % 4):KEYS * (i % 4) + KEYS],
                                     kn[:, b, P * i:P * i + P], ident[0:KEYS, 0:KEYS]).then_inc(pe_kT, 1)
                pe.wait_ge(vb_ready, len(VG) * 2 * B)
                pe.wait_ge(nullv_put, 2)
                pe.wait_ge(wo_in, 16)
                pe.wait_ge(k_copied, 2 * B)
                for n, (b, m) in enumerate(VWJ):
                    if n >= 2:
                        pe.wait_ge(vw_lo, 2 * (n - 1))
                    for r in range(2):
                        M = rows[m + r]
                        lo, hi = P * (m + r), P * (m + r) + M
                        over = [i for i in range(PAIRS) if PAIRW * i < hi and PAIRW * (i + 1) > lo]
                        for i in over:
                            at = P + lo - PAIRW * i
                            mm = pe.matmul(ps[0:M, BP[n % 2], D * r:D * r + D], VB[:, b, i, at:at + M],
                                           Wo_s[:, i, :], start=i == over[0], stop=i == over[-1])
                    mm.then_inc(pe_vwp, 1)
                pe.wait_ge(vw_lo, 2 * len(VWJ))
                pe.wait_ge(kb_ready, 4 * B)

            def scores(t):
                k, b = t % CT, t // CT // CPB
                if t:
                    pe.wait_ge(scaled, t)
                pe.wait_ge(q_copied, PAIRS * (t // CT + 1))
                for g, n in SG:
                    for i in range(GP * g, GP * g + n):
                        at = PAIRW * (i - GP * g)
                        mm = pe.matmul(ps[:, BS[g], at:at + PAIRW], qT[:, i, P * k:P * k + P], KB[:, b, i, :],
                                       start=True, stop=True)
                mm.then_inc(pe_scores, 1)

            def attend(t):
                b = t // CT // CPB
                pe.wait_ge(p_hi, 4 * t + 4)
                pe.wait_ge(p_lo, 4 * t + 4)
                if t:
                    pe.wait_ge(o_copied, t)
                dst = ps[:, BV, 0:D]
                for m in range(KT):
                    r = rows[m]
                    mm = three(dst, ph[0:r, m, :], pl[0:r, m, :], VWh[0:r, b, m, :], VWl[0:r, b, m, :],
                               m == 0, m == KT - 1)
                mm.then_inc(pe_vw, 1)

            def turn_probs(t):
                pe.wait_ge(normed, t + 1)
                for g in range(3):
                    n = 3 * t + g
                    if n >= 2:
                        pe.wait_ge(p_lo, 4 * ((n - 2) // 3) + (n - 2) % 3 + (2 if (n - 2) % 3 == 2 else 1))
                    for m in range(4 * g, min(4 * g + 4, KT)):
                        r = rows[m]
                        mm = pe.transpose(ps[0:r, BT[n % 2], P * (m - 4 * g):P * (m - 4 * g) + P],
                                          E[:, t % 2, P * m:P * m + r], ident[:, :])
                    mm.then_inc(pe_pT, 1)

            def turn_ffn_in(cc):
                pe.wait_ge(zf_ready, CT * cc + CT)
                if cc < CH - 1:
                    pe.wait_ge(sums_read, cc + 2)
                for h in range(DK):
                    bank = BP[h] if cc < CH - 1 else BC[h]
                    for k in range(CT):
                        mm = pe.transpose(ps[:, bank, P * k:P * k + P], zF[:, k, P * h:P * h + P], ident[:, :])
                    mm.then_inc(pe_cT, 1)

            for t in steps:
                c, k = t // CT, t % CT
                if t > TILES + 1:
                    break
                if k == 0 and c < CH:
                    begin(c)
                if t < TILES:
                    scores(t)
                if k == 3 and 1 <= c < CH:
                    turn_ffn_in(c - 1)
                if 0 <= t - 2 < TILES:
                    attend(t - 2)
                if 0 <= t - 1 < TILES:
                    turn_probs(t - 1)

            def hidden(f):
                if f == 0:
                    pe.wait_ge(wmp_lo, DK)
                pe.wait_ge(xc_hi, DK * (f + 1))
                pe.wait_ge(xc_lo, DK * (f + 1))
                for j in range(FT):
                    n = FT * f + j
                    if n >= 4:
                        pe.wait_ge(h_lo, n - 3)
                    else:
                        pe.wait_ge(p_lo, 4 * TILES)
                        pe.wait_ge(xc_lo, DK * (CH - 1))
                    for k in range(DK):
                        w = slice(P * j, P * j + P)
                        mm = three(ps[:, (BP + BT)[n % 4], :], Wmh[:, k, w], Wml[:, k, w],
                                   xch[:, k, CW * f:CW * f + CW], xcl[:, k, CW * f:CW * f + CW],
                                   k == 0, k == DK - 1)
                    mm.then_inc(pe_h, 1)

            def project(f):
                if f == 0:
                    pe.wait_ge(wmp_lo, DK + 2)
                for k in range(CT):
                    t = CT * f + k
                    if t >= 2:
                        pe.wait_ge(y_ready, t - 1)
                    for j in range(FT):
                        pe.wait_ge(h_lo, FT * f + j + 1)
                        w = slice(P * k, P * k + P)
                        mm = three(ps[:, BY[t % 2], 0:D], hh[f % 2][:, j, w], hl[f % 2][:, j, w],
                                   Wph[:, j, :], Wpl[:, j, :], j == 0, j == FT - 1)
                    mm.then_inc(pe_y, 1)

            hidden(0)
            turn_ffn_in(CH - 1)
            project(0)
            hidden(1)
            project(1)
            hidden(2)
            hidden(3)
            project(2)
            pe.wait_ge(search_dve, 1)
            pe.wait_ge(wc_in, 32)
            for j in range(FT):
                mm = pe.matmul(ps[0:B, BC[0], 0:D], hb[:, j, :], wp_raw[:, j, :], start=j == 0, stop=j == FT - 1)
            mm.then_inc(search_pe, 1)
            pe.wait_ge(search_dve, 2)
            for k in range(DK):
                mm = pe.transpose(ps[:, BC[1], B * k:B * k + B], pooled[:, P * k:P * k + P], ident[0:B, 0:B])
            mm.then_inc(search_pe, 1)
            pe.wait_ge(search_dve, 3)
            for k in range(DK):
                mm = pe.matmul(ps[0:HID, BC[0], 0:B], w_c1[:, k, :], plT[:, k, :], start=k == 0, stop=k == DK - 1)
            mm.then_inc(search_pe, 1)
            pe.wait_ge(search_dve, 3 + B)
            for j, bank in enumerate((0, 1, 5, 6, 3, 4)):
                mm = pe.matmul(ps[:, bank, :], rT[:, :], w_c2[:, 512 * j:512 * j + 512], start=True, stop=True)
            mm.then_inc(search_pe, 1)
            project(3)
            for n in range(2):
                pe.wait_ge(search_dve, 4 + B + n)
                pe.matmul(ps[:, BC[0], 0:1], ones_b[:, :], srch[:, 6:7], start=True, stop=True).then_inc(search_pe, 1)
            pe.wait_ge(search_dve, 6 + B)
            for n in range(2):
                for h in range(B):
                    mm = pe.matmul(ps[0:1, BC[1], n:n + 1], ident[:, HD * h:HD * h + 1], srch[:, 8 + n:9 + n],
                                   start=h == 0, stop=h == B - 1)
            mm.then_inc(search_pe, 1)

            pe.wait_ge(flag_ready, 1)
            go = pe.value_load(flag[0:1, 0:1])
            with pe.If(go > 0):
                with pe.Fori(0, 3) as s:
                    pe.wait_ge(g_small, s * G_SMALL + 1)
                    pe.sem_inc(held, 1)
                    with pe.Fori(0, FTF) as j:
                        n0 = CH * (s * FTF + j)
                        pe.wait_ge(g_w, (s * FTF + j) * 32 + 32)
                        pe.wait_ge(g_relu, n0 + CH)
                        for c in range(CH):
                            for k in range(DK):
                                mm = pe.matmul(ps[:, c, :], gwm[:, k, :], gx[:, k, CW * c:CW * c + CW],
                                               start=k == 0, stop=k == DK - 1)
                            mm.then_inc(g_h, 1)
                        for c in range(CH):
                            pe.wait_ge(g_relu, n0 + CH + c + 1)
                            pe.wait_ge(g_add, n0 + CH + c - 1)
                            for k in range(DK):
                                mm = pe.matmul(ps[:, 4 + 2 * (c % 2) + k, :], gwp[:, P * k:P * k + P], ghm[:, c, :],
                                               start=True, stop=True)
                            mm.then_inc(g_y, 1)
                    pe.wait_ge(g_small, s * G_SMALL + 2)
                    for k in range(DK):
                        mm = pe.matmul(ps[0:HID, 7, 0:B], w_c1[:, k, :], gs[:, 8 + B * k:8 + B * k + B],
                                       start=k == 0, stop=k == DK - 1)
                    mm.then_inc(g_pe, 1)
                    pe.wait_ge(g_small, s * G_SMALL + 3)
                    for b in range(B):
                        if b:
                            pe.wait_ge(g_small, s * G_SMALL + 3 + b)
                        for j in range(6):
                            mm = pe.matmul(ps[:, j, :], gr[:, b, :], w_c2[:, 512 * j:512 * j + 512],
                                           start=True, stop=True)
                        mm.then_inc(g_pe, 1)
                        pe.wait_ge(g_copy, s * B + b + 1)
                        pe.sem_inc(held, 1)
                        for j in range(FTF):
                            mm = pe.transpose(ps[:, 6, j:j + 1], grow[0:1, P * j:P * j + P], ident[0:1, 0:1])
                        mm.then_inc(g_pe, 1)
                    pe.wait_ge(g_small, s * G_SMALL + 4 + B)
                    pe.matmul(ps[:, 7, 0:1], gones[:, :], gs[:, 3:4], start=True, stop=True).then_inc(g_pe, 1)
                pe.wait_ge(g_small, 3 * G_SMALL + 1)
                for t in range(TILES):
                    if t >= 2:
                        pe.wait_ge(g_out, t - 1)
                    for k in range(DK):
                        mm = pe.transpose(ps[:, t % 2, P * k:P * k + P], gx[:, k, P * t:P * t + P], ident[:, :])
                    mm.then_inc(g_pe, 1)
            with pe.Else():
                pe.nop()


_INS = ["x", "ctx_1024", "g_xattn", "g_ffn", "L0_xattn_Wq", "L0_xattn_Wkv", "L0_xattn_Wo", "L0_xattn_null_kv",
        "L0_xattn_q_scale", "L0_xattn_k_scale", "L0_xattn_ln_in_g", "L0_xattn_ln_in_b", "L0_xattn_ln_ctx_g",
        "L0_xattn_ln_ctx_b", "L0_xattn_ln_out_g", "L0_xattn_ln_out_b", "L0_ffn_Wm", "L0_ffn_Wp", "L0_ffn_Wc1",
        "L0_ffn_Wc2"]


def kernel(**inputs):
    import numpy as _np
    import concourse.bacc as _bacc
    from concourse import mybir as _mybir
    from concourse.bass_utils import run_bass_kernel_spmd as _run

    nc = _bacc.Bacc("TRN2", target_bir_lowering=False, num_devices=1)
    arrays, args = {}, []
    for name in _INS:
        a = _np.asarray(inputs[name])
        if name.startswith("L0_ffn_"):
            a = a.T
        a = _np.ascontiguousarray(a)
        arrays[f"in_{name}_dram"] = a
        args.append(nc.dram_tensor(f"in_{name}_dram", a.shape, _mybir.dt.from_np(a.dtype), kind="ExternalInput").ap())
    shape = inputs["x"].shape
    args.append(nc.dram_tensor("out_0_dram", shape, _mybir.dt.float32, kind="ExternalOutput").ap())
    flamingo_block(nc, *args)
    r = _run(nc, [arrays], core_ids=[0])
    return r.results[0]["out_0_dram"]
```

```python
from contextlib import ExitStack

import concourse.bass as bass
from concourse import mybir

F32 = mybir.dt.float32
F32R = mybir.dt.float32r
I32 = mybir.dt.int32
ALU = mybir.AluOpType
ACT = mybir.ActivationFunctionType
AX = mybir.AxisListType

P = 128
HEADS, HD = 16, 64
SCALE = 8.0
LN_EPS = 1e-5
NORM_EPS = 1e-12
R = 0.7
RSQRT_GUESS = float(0x5F3759DF)
SPREAD = 64


class Chain:

    def __init__(self, eng, sem):
        self.eng, self.sem, self.n = eng, sem, 0

    def do(self, instruction):
        self.n += 1
        instruction.then_inc(self.sem, 1)
        self.eng.wait_ge(self.sem, self.n)


def rsqrt(dve, do, y, v, t):
    yi = y.bitcast(I32)
    do(dve.tensor_scalar(yi, v.bitcast(I32), 1, None, ALU.arith_shift_right))
    do(dve.tensor_scalar(yi, yi, -1.0, RSQRT_GUESS, ALU.mult, ALU.add))
    for _ in range(3):
        do(dve.tensor_tensor(t, y, y, ALU.mult))
        do(dve.scalar_tensor_tensor(t, t, -0.5, v, ALU.mult, ALU.mult))
        do(dve.scalar_tensor_tensor(y, t, 1.5, y, ALU.add, ALU.mult))


def flamingo_block(nc, x, ctx_in, g_xattn, g_ffn, Wq, Wkv, Wo, null_kv, q_scale, k_scale,
                   ln_in_g, ln_in_b, ln_ctx_g, ln_ctx_b, ln_out_g, ln_out_b,
                   WmT, WpT, Wc1T, Wc2T, out):
    B, N, D = x.shape
    J = ctx_in.shape[1]
    KEYS = J + 1
    PACK = HEADS * KEYS
    KT = (PACK + P - 1) // P
    PAIRS = HEADS // 2
    INNER = HEADS * HD
    TILES = B * N // P
    CT = 4
    CW = CT * P
    CH = TILES // CT
    CPB = CH // B
    DK = D // P
    FULL = WmT.shape[1]
    ITER = FULL // 3
    FT = ITER // P
    FTF = FULL // P
    HID = Wc1T.shape[1]
    PAIRW = 2 * KEYS
    PADW = P + PAIRW + P
    NEW_MAX = R * ITER * B

    xt = x.rearrange("b (c k p) d -> (b c) p k d", p=P, k=CT)
    ot = out.rearrange("b (c k p) d -> (b c) p k d", p=P, k=CT)
    wm_v = WmT.rearrange("(k p) f -> p k f", p=P)
    wp_v = WpT.rearrange("(j p) c -> p j c", p=P)

    es = ExitStack()
    with es:
        def sem(name):
            return es.enter_context(nc.semaphore(name))

        LO = 16512
        END = nc.sbuf_usable_end
        top = [LO]

        def place(name, shape, dt, offset=None):
            nbytes = 4
            for s in shape[1:]:
                nbytes *= s
            nbytes = (nbytes + 31) // 32 * 32
            if offset is None:
                offset = top[0]
                top[0] += nbytes
                assert top[0] <= END, (name, top[0], END)
            assert offset + nbytes <= END, name
            return nc.alloc_sbuf_tensor_at(name, shape, dt, offset=offset)

        es.enter_context(nc.sbuf_tensor("fence", [P, (END - LO) // 4 - 8], F32))

        ident = place("ident", [P, P], F32)
        ones_b = place("ones_b", [P, P], F32)
        head_f = place("head_f", [P, PAIRS, HEADS], F32)
        head_of = place("head_of", [P, PAIRS, HEADS], F32R)
        small = place("small", [P, 256], F32)
        G = place("G", [P, D], F32)
        TB = place("TB", [P, D], F32)
        resid = place("resid", [P, TILES, D], F32)
        KB = place("KB", [P, B, PAIRS, PAIRW], F32)
        o_vw = top[0]
        VWh = place("VWh", [P, B, KT, D], F32R)
        VWl = place("VWl", [P, B, KT, D], F32R)
        o_wq = top[0]
        Wqh = place("Wqh", [P, DK, INNER], F32R)
        Wql = place("Wql", [P, DK, INNER], F32R)
        o_q = top[0]
        qT = place("qT", [P, PAIRS, CW], F32)
        o_e = top[0]
        E = place("E", [P, 2, KT * P], F32)
        ph = place("ph", [P, KT, P], F32R)
        pl = place("pl", [P, KT, P], F32R)
        o_z = top[0]
        z = place("z", [P, CT, D], F32)
        zF = place("zF", [P, CT, D], F32)
        xnh = place("xnh", [P, DK, CW], F32R)
        xnl = place("xnl", [P, DK, CW], F32R)
        xf = place("xf", [P, DK, CW], F32)
        sq = xf
        o_ob = top[0]
        ob = place("ob", [P, 2, D], F32)
        u = place("u", [P, 2, D], F32)
        top[0] += 256
        sqh = place("sqh", [P, 2, CW], F32R, o_ob)
        sql = place("sql", [P, 2, CW], F32R, o_z)
        o_xc = top[0]
        xch = place("xch", [P, DK, CH * CW], F32R)
        xcl = place("xcl", [P, DK, CH * CW], F32R)
        o_raw = top[0]
        wm_raw = place("wm_raw", [P, DK, ITER], F32)
        wp_raw = place("wp_raw", [P, FT, D], F32)
        Wo_s = place("Wo_s", [P, PAIRS, D], F32)
        VB = place("VB", [P, B, PAIRS, PADW], F32, o_xc)
        cx = place("cx", [J, B, D], F32, o_xc + B * PAIRS * PADW * 4)
        cz = place("cz", [J, B, D], F32, o_xc + B * PAIRS * PADW * 4 + B * D * 4)
        cT = place("cT", [P, DK, B * J], F32, o_xc + B * PAIRS * PADW * 4 + 2 * B * D * 4)
        Wkv_s = place("Wkv_s", [P, DK, 2 * INNER], F32, o_e)
        wq_raw = place("wq_raw", [P, DK, INNER], F32, o_vw)
        kn = place("kn", [KEYS, B, INNER], F32, o_raw)
        ksq = place("ksq", [KEYS, B, INNER], F32, o_raw + B * INNER * 4)
        Wmh = place("Wmh", [P, DK, ITER], F32R, o_wq)
        Wml = place("Wml", [P, DK, ITER], F32R, o_wq + DK * ITER * 4)
        Wph = place("Wph", [P, FT, D], F32R, o_q)
        Wpl = place("Wpl", [P, FT, D], F32R, o_q + FT * D * 4)
        hw = FT * CW * 4
        hh = [place("hh0", [P, FT, CW], F32R, o_vw), place("hh1", [P, FT, CW], F32R, o_q + 2 * hw // 2 * 1)]
        hl = [place("hl0", [P, FT, CW], F32R, o_vw + hw), place("hl1", [P, FT, CW], F32R, o_q + hw + hw)]
        assert o_vw + 2 * hw <= o_wq and o_q + 3 * hw <= o_xc, (o_q + 3 * hw, o_xc)
        yo = place("yo", [P, 2, CT, D], F32, o_raw)
        w_c1 = place("w_c1", [P, DK, HID], F32, o_raw + 2 * FT * D * 4)
        rT = place("rT", [HID, P], F32, o_raw + 2 * FT * D * 4 + DK * HID * 4)
        pooled = place("pooled", [B, D], F32, o_raw + 2 * FT * D * 4 + DK * HID * 4 + P * 4)
        w_c2 = place("w_c2", [HID, FULL], F32, o_q + 3 * hw)
        ck = place("ck", [P, FULL], F32, o_vw + 2 * hw)
        over = place("over", [P, FULL], F32, o_vw + 2 * hw + FULL * 4)
        assert o_vw + 2 * hw + 2 * FULL * 4 <= o_wq + 2 * DK * ITER * 4 and o_q + 3 * hw + FULL * 4 <= o_xc

        ps = es.enter_context(nc.psum_tensor("ps", [P, 8, 512], F32))
        BP = (0, 1)
        BS = (2, 3, 4)
        BT = (5, 6)
        BV = 7
        BY = (2, 7)
        BC = (3, 4)
        GP = 3
        SG = [(g, min(GP, PAIRS - GP * g)) for g in range((PAIRS + GP - 1) // GP)]

        col = {}
        used = [0]

        def cols(name, n):
            col[name] = slice(used[0], used[0] + n)
            used[0] += n
            return small[:, col[name]]

        gates = cols("gates", 2)
        tg = cols("tg", 2)
        in_gb = cols("in_gb", 2 * DK).rearrange("p (a k) -> p a k", a=2)
        cx_gb = cols("cx_gb", 2 * DK).rearrange("p (a k) -> p a k", a=2)
        sc2 = cols("sc2", 2)
        qk = cols("qk", 1)
        nv = cols("nv", 1)
        st_a = cols("st_a", 6)
        mv_a = cols("mv_a", 2)
        nw_a = cols("nw_a", 3)
        st_n = cols("st_n", 18).rearrange("p (n s) -> p n s", n=3)
        mv_n = cols("mv_n", 12).rearrange("p (q n s) -> p q n s", q=2, n=3)
        var_n = cols("var_n", 6).rearrange("p (q n) -> p q n", q=2)
        rs_n = cols("rs_n", 6).rearrange("p (q n) -> p q n", q=2)
        rt_n = cols("rt_n", 6).rearrange("p (q n) -> p q n", q=2)
        nb_n = cols("nb_n", 6).rearrange("p (q n) -> p q n", q=2)
        st_z = cols("st_z", 6 * CT).rearrange("p (k s) -> p k s", k=CT)
        mv_z = cols("mv_z", 2 * CT).rearrange("p (k s) -> p k s", k=CT)
        nw_z = cols("nw_z", 3 * CT).rearrange("p (s k) -> p s k", s=3)
        hs = cols("hs", FT * CH).rearrange("p (j c) -> p j c", j=FT)
        hb = cols("hb", FT * B).rearrange("p (j b) -> p j b", j=FT)
        plT = cols("plT", DK * B).rearrange("p (k b) -> p k b", k=DK)
        srch = cols("srch", 16)
        big = place("big", [P, 7 * CT * HEADS], F32)
        rq = big[:, 0:CT * HEADS]
        rqv = big[:, 64:128]
        rqt = big[:, 128:192]
        den = big[:, 192:224].rearrange("p (a h) -> p a h", a=2)
        rden = big[:, 224:256].rearrange("p (a h) -> p a h", a=2)
        kss, krk, krt = big[0:KEYS, 256:288], big[0:KEYS, 288:320], big[0:KEYS, 320:352]
        ssT = place("ssT", [HEADS, CW], F32)
        part_i = place("part_i", [P, 1], I32)
        flag = place("flag", [1, 1], I32)
        g_at = [o_vw - B * PAIRS * PAIRW * 4]

        def later(name, shape, dt=F32):
            nbytes = 4
            for s in shape[1:]:
                nbytes *= s
            nbytes = (nbytes + 31) // 32 * 32
            g_at[0] += nbytes
            assert g_at[0] <= o_q + 3 * hw, name
            return place(name, shape, dt, g_at[0] - nbytes)

        TOK = CH * CW
        gx = later("gx", [P, DK, TOK])
        gn = later("gn", [P, DK, TOK])
        ghm = later("ghm", [P, CH, CW])
        gwm = later("gwm", [P, DK, P])
        gwp = later("gwp", [P, D])
        grow = later("grow", [P, FULL])
        gtmp = later("gtmp", [P, FULL])
        geq = later("geq", [P, FULL])
        gidx = later("gidx", [P, FULL])
        gidx_i = later("gidx_i", [P, FULL], I32)
        gfid = later("gfid", [P, FTF])
        gfid_i = later("gfid_i", [P, FTF], I32)
        gones = later("gones", [P, P])
        gr = later("gr", [HID, B, P])
        gmask = later("gmask", [P, 4, B, FTF])
        g_act, g_hist, g_new, g_comb = (gmask[:, a].rearrange("p b j -> p (b j)") for a in range(4))
        gdiff = later("gdiff", [P, B * FTF])
        gck = later("gck", [P, FTF])
        grank = later("grank", [P, 2, FTF])
        gs = later("gs", [P, 32])
        gout = later("gout", [P, 2, CT, D])

        x_in = [sem(f"x_in{c}") for c in range(CH)]
        gate_in = sem("gate_in")
        wq_in, wkv_in, wo_in, ctx_dma, par_in, nullk_in, wm_in, wc_in = map(
            sem, ("wq_in", "wkv_in", "wo_in", "ctx_dma", "par_in", "nullk_in", "wm_in", "wc_in"))
        y_out = [sem(f"y_out{c}") for c in range(CH)]
        consts = sem("consts")
        zeroed = sem("zeroed")
        pool_chain, dve_chain, act_chain = sem("pool_chain"), sem("dve_chain"), sem("act_chain")
        tanh_done, g_done = sem("tanh_done"), sem("g_done")
        wq_hi, wq_lo = sem("wq_hi"), sem("wq_lo")
        z_ready = sem("z_ready")
        pe_xT, xn_full, xn_hi, xn_lo = map(sem, ("pe_xT", "xn_full", "xn_hi", "xn_lo"))
        sq_full, sq_hi, sq_lo = sem("sq_full"), sem("sq_hi"), sem("sq_lo")
        head_ready, e_zeroed = sem("head_ready"), sem("e_zeroed")
        wk_in, wv_in = sem("wk_in"), sem("wv_in")
        pe_q, q_copied, q_squared, pe_ss, ss_copied, pe_rT, sums_read = map(
            sem, ("pe_q", "q_copied", "q_squared", "pe_ss", "ss_copied", "pe_rT", "sums_read"))
        pe_scores, scaled, exped, den_ready, normed = map(
            sem, ("pe_scores", "scaled", "exped", "den_ready", "normed"))
        pe_pT, p_hi, p_lo = sem("pe_pT"), sem("p_hi"), sem("p_lo")
        var_ready, rs_guess, rs_ready = sem("var_ready"), sem("rs_guess"), sem("rs_ready")
        pe_vw, o_copied, u_ready, x1_ready, zf_ready = map(sem, ("pe_vw", "o_copied", "u_ready", "x1_ready", "zf_ready"))
        pe_cT, xc_hi, xc_lo = sem("pe_cT"), sem("xc_hi"), sem("xc_lo")
        pe_h, h_hi, h_lo, pe_y, y_ready = map(sem, ("pe_h", "h_hi", "h_lo", "pe_y", "y_ready"))
        cz_ready, pe_czT, cT_ready, pe_k, k_copied, k_squared, khat_ready = map(
            sem, ("cz_ready", "pe_czT", "cT_ready", "pe_k", "k_copied", "k_squared", "khat_ready"))
        pe_kT, kb_ready, pe_v, vb_ready, nullv_put, pe_vwp, vw_hi, vw_lo = map(
            sem, ("pe_kT", "kb_ready", "pe_v", "vb_ready", "nullv_put", "pe_vwp", "vw_hi", "vw_lo"))
        wmp_hi, wmp_lo = sem("wmp_hi"), sem("wmp_lo")

        search_pe, search_dve, ck_copied, flag_ready = map(
            sem, ("search_pe", "search_dve", "ck_copied", "flag_ready"))
        g_w, g_h, g_relu, g_y, g_add, g_small, g_pe, g_copy, g_iota, g_out, g_sum = map(
            sem, ("g_w", "g_h", "g_relu", "g_y", "g_add", "g_small", "g_pe", "g_copy", "g_iota", "g_out", "g_sum"))
        G_PE = 1 + 2 * B + 1
        G_SMALL = 2 + B + 3
        held = sem("held")
        g_out2 = [sem(f"g_out{c}") for c in range(CH)]

        VG = [(0, 3), (3, 3), (6, 2)]
        VBK = (BS[0], BS[1], BV)
        VWJ = [(b, m) for b in range(B) for m in range(0, KT, 2)]
        VWS = {0: range(0, 3), 1: range(3, 5), 4: range(5, 7), 5: range(7, 9), 6: range(9, 10)}

        def norms(t):
            n0 = 0 if t < TILES - CT else 1 if t < TILES + 2 else 2
            return n0, 3 if t >= 3 else 2 if t >= 2 else 1

        steps = range(TILES + 3)

        block = es.enter_context(nc.Block())

        def general_dve(dve):
            for c in range(CH):
                dve.wait_ge(y_out[c], 16)
            done, more, nov, nn = (gs[:, n:n + 1] for n in range(4))
            gp = gs[:, 8:8 + DK * B]
            dve.wait_ge(g_iota, 3)
            dve.tensor_copy(gidx[:, :], gidx_i[:, :])
            dve.tensor_copy(gfid[:, :], gfid_i[:, :])
            dve.memset(gones[:, :], 1.0)
            dve.memset(gmask[:, :, :, :], 0.0).then_inc(g_sum, 1)
            dve.memset(done, 0.0)
            dve.wait_ge(g_sum, 1)
            dve.memset(gmask[:, 0:2, :, 0:FT], 1.0).then_inc(g_sum, 1)
            dve.tensor_tensor(gx[:, :, :], xch[:, :, :].bitcast(F32), xcl[:, :, :].bitcast(F32),
                              ALU.add).then_inc(g_small, 1)
            dve.wait_ge(g_small, 1)
            dve.wait_ge(g_sum, 2)
            dve.sem_inc(g_y, CH)
            dve.sem_inc(g_relu, CH)
            dve.sem_inc(g_add, CH)
            K = 24 + 4 * B * FTF
            with dve.Fori(0, 3) as s:
                at = [2]

                def do(ins):
                    at[0] += 1
                    ins.then_inc(g_sum, 1)
                    dve.wait_ge(g_sum, s * K + at[0])

                do(dve.memset(gn[:, :, :], 0.0))
                dve.memset(gs[:, 30:31], 0.0)
                with dve.Fori(0, FTF) as j:
                    n0 = CH * (s * FTF + j)
                    for c in range(CH):
                        dve.wait_ge(g_y, n0 + CH + c + 1)
                        dve.wait_ge(g_add, n0 + c + 1)
                        dst = gn[:, :, CW * c:CW * c + CW]
                        src = ps[:, 4 + 2 * (c % 2):6 + 2 * (c % 2), :]
                        dve.tensor_tensor(dst, dst, src, ALU.add).then_inc(g_add, 1)
                dve.wait_ge(g_add, CH * (s * FTF + FTF) + CH)
                do(dve.tensor_reduce(gp, gn[:, :, :].rearrange("p k (b t) -> p (k b) t", b=B), AX.X, ALU.add))
                dve.tensor_scalar(gp, gp, 1.0 / N, None, ALU.mult).then_inc(g_small, 1)
                dve.wait_ge(g_pe, s * G_PE + 1)
                for b in range(B):
                    do(dve.tensor_scalar(gr[:, b, :], ps[0:HID, 7, b:b + 1].to_broadcast([HID, P]), 0.0, None,
                                         ALU.max))
                dve.sem_inc(g_small, 1)
                for b in range(B):
                    dve.wait_ge(g_pe, s * G_PE + 3 + 2 * b)
                    do(dve.tensor_copy(gck[:, :], ps[:, 6, 0:FTF]))
                    base = at[0]
                    dve.memset(gs[:, 30:31], 0.0)
                    with dve.Fori(0, FTF) as j:
                        def link(ins, i):
                            ins.then_inc(g_sum, 1)
                            dve.wait_ge(g_sum, s * K + j * 4 + (base + i))

                        mine = gck[:, bass.ds(j, 1)]
                        link(dve.tensor_scalar(gtmp[:, :], grow[:, :], mine, None, ALU.is_gt, ALU.add,
                                               accum_out=gs[:, 16:17]), 1)
                        link(dve.tensor_scalar(geq[:, :], grow[:, :], mine, None, ALU.is_equal), 2)
                        link(dve.scalar_tensor_tensor(gtmp[:, :], gidx[:, :], gfid[:, bass.ds(j, 1)], geq[:, :],
                                                      ALU.is_lt, ALU.mult, accum_out=gs[:, 17:18]), 3)
                        link(dve.tensor_tensor(grank[:, 0, bass.ds(j, 1)], gs[:, 16:17], gs[:, 17:18], ALU.add), 4)
                    at[0] += 4 * FTF
                    do(dve.tensor_scalar(gmask[:, 2, b, :], grank[:, 0, :], ITER - 0.5, None, ALU.is_lt))
                    dve.sem_inc(g_small, 1)
                do(dve.tensor_tensor(g_comb, g_hist, g_new, ALU.max))
                do(dve.tensor_tensor(gdiff[:, :], g_comb, g_hist, ALU.subtract))
                do(dve.tensor_reduce(nn, gdiff[:, :], AX.X, ALU.add))
                dve.sem_inc(g_small, 1)
                dve.wait_ge(g_pe, s * G_PE + G_PE)
                do(dve.tensor_scalar(more, done, -1.0, 1.0, ALU.mult, ALU.add))
                do(dve.tensor_scalar(gn[:, :, :], gn[:, :, :], more, None, ALU.mult))
                do(dve.scalar_tensor_tensor(gx[:, :, :], gx[:, :, :], done, gn[:, :, :], ALU.mult, ALU.add))
                for old, new in ((g_act, g_new), (g_hist, g_comb)):
                    do(dve.tensor_scalar(new, new, more, None, ALU.mult))
                    do(dve.scalar_tensor_tensor(old, old, done, new, ALU.mult, ALU.add))
                do(dve.tensor_scalar(nov, ps[:, 7, 0:1], NEW_MAX, None, ALU.is_lt))
                do(dve.tensor_tensor(done, done, nov, ALU.max))
                while at[0] < 2 + K:
                    do(dve.memset(gs[:, 31:32], 0.0))
                dve.sem_inc(g_small, 2)
            for t in range(TILES):
                dve.wait_ge(g_pe, 3 * G_PE + t + 1)
                if t >= 2 * CT:
                    dve.wait_ge(g_out2[t // CT - 2], 16)
                dve.scalar_tensor_tensor(gout[:, t // CT % 2, t % CT, :], ps[:, t % 2, 0:D], tg[:, 1:2],
                                         resid[:, t, :], ALU.mult, ALU.add).then_inc(g_out, 1)

        @block.sync
        def _(sp):
            sp.dma_start(resid[:, 0:CT, :], xt[0]).then_inc(x_in[0], 16)
            sp.dma_start(cx[:, :, :], ctx_in.rearrange("b j d -> j b d")).then_inc(ctx_dma, 16)
            sp.dma_start(wq_raw[:, :, :], Wq.rearrange("(k p) n -> p k n", p=P)).then_inc(wq_in, 16)
            wkv_v = Wkv.rearrange("(k p) n -> p k n", p=P)
            sp.dma_start(Wkv_s[:, :, 0:INNER], wkv_v[:, :, 0:INNER]).then_inc(wk_in, 16)
            sp.dma_start(Wkv_s[:, :, INNER:], wkv_v[:, :, INNER:]).then_inc(wv_in, 16)
            sp.dma_start(Wo_s[:, :, :], Wo.rearrange("(i p) n -> p i n", p=P)).then_inc(wo_in, 16)
            for c in range(1, CH):
                sp.dma_start(resid[:, CT * c:CT * c + CT, :], xt[c]).then_inc(x_in[c], 16)
            sp.wait_ge(pe_kT, B * PAIRS)
            sp.dma_start(wm_raw[:, :, :], wm_v[:, :, 0:ITER]).then_inc(wm_in, 16)
            sp.dma_start(wp_raw[:, :, :], wp_v[:, 0:FT, :]).then_inc(wm_in, 16)
            sp.wait_ge(pe_vwp, len(VWJ))
            with nc.allow_non_contiguous_dma(reason="rows of 256 bytes"):
                sp.dma_start(w_c1[:, :, :], Wc1T.rearrange("(k p) h -> p k h", p=P)).then_inc(wc_in, 16)
            sp.wait_ge(x1_ready, TILES)
            sp.wait_ge(pe_q, CH * PAIRS)
            sp.dma_start(w_c2[:, :], Wc2T).then_inc(wc_in, 16)
            for c in range(CH):
                sp.wait_ge(y_ready, CT * c + CT)
                sp.dma_start(ot[c], yo[:, c % 2, :, :]).then_inc(y_out[c], 16)
            for c in range(CH):
                sp.wait_ge(y_out[c], 16)
            sp.wait_ge(flag_ready, 1)
            go = sp.value_load(flag[0:1, 0:1])
            with sp.If(go > 0):
                with sp.Fori(0, 3) as s:
                    with sp.Fori(0, FTF) as j:
                        sp.wait_ge(g_y, CH * (s * FTF + j) + CH)
                        sp.dma_start(gwm[:, :, :], wm_v[:, :, bass.ds(j * P, P)]).then_inc(g_w, 16)
                        sp.dma_start(gwp[:, :], WpT[bass.ds(j * P, P), :]).then_inc(g_w, 16)
                for c in range(CH):
                    sp.wait_ge(g_out, CT * c + CT)
                    sp.dma_start(ot[c], gout[:, c % 2, :, :]).then_inc(g_out2[c], 16)
                for c in range(CH):
                    sp.wait_ge(g_out2[c], 16)
            with sp.Else():
                sp.nop()

        @block.gpsimd
        def _(pool):
            do = Chain(pool, pool_chain).do
            do(pool.memset(ident[:, :], 0.0))
            pool.affine_select(out=ident[:, :], in_=ident[:, :], compare_op=ALU.not_equal, fill=1.0,
                               base=0, pattern=[[-1, P]], channel_multiplier=1).then_inc(consts, 1)
            do(pool.memset(head_f[:, :, :], 0.0))
            for s in range(2):
                for i in range(PAIRS):
                    do(pool.memset(head_f[HD * s:HD * s + HD, i, 2 * i + s:2 * i + s + 1], 1.0))
            pool.tensor_copy(head_of[:, :, :], head_f[:, :, :]).then_inc(head_ready, 1)
            do(pool.memset(ones_b[:, :], 0.0))
            for s in range(2):
                do(pool.memset(ones_b[HD * s:HD * s + HD, HD * s:HD * s + HD], 1.0))
            pool.memset(VB[:, :, :, :], 0.0).then_inc(zeroed, 1)
            pool.memset(KB[:, :, :, :], 0.0).then_inc(zeroed, 1)
            pool.iota(part_i[:, :], pattern=[[0, 1]], base=0, channel_multiplier=1).then_inc(g_iota, 1)
            with nc.allow_non_contiguous_dma(reason="the null key for every head"):
                for b in range(B):
                    pool.dma_start(kn[J:KEYS, b, :].rearrange("o (h d) -> o h d", h=HEADS),
                                   null_kv[0:1, :].unsqueeze(1).to_broadcast([1, HEADS, HD])).then_inc(nullk_in, 16)
            pool.wait_ge(tanh_done, 1)
            pool.wait_ge(gate_in, 16 * 4)
            gx = tg[:, 0:1]
            pool.tensor_scalar(G[:, :], G[:, :], gx, None, ALU.mult).then_inc(g_done, 1)
            pool.tensor_scalar(TB[:, :], TB[:, :], gx, None, ALU.mult).then_inc(g_done, 1)
            pool.wait_ge(g_done, 2)

            def xn_low(c):
                for k in range(DK):
                    pool.wait_ge(xn_full, DK * c + k + 1)
                    pool.wait_ge(xn_hi, DK * c + k + 1)
                    pool.tensor_tensor(xnl[:, k, :], xf[:, k, :], xnh[:, k, :].bitcast(F32),
                                       ALU.subtract).then_inc(xn_lo, 1)

            for t in steps:
                c, k = t // CT, t % CT
                if k == 0 and c < CH:
                    xn_low(c)
                if t == 0:
                    pool.wait_ge(pe_v, len(VG))
                    pool.memset(E[:, :, PACK:], 0.0).then_inc(e_zeroed, 1)
                if t < TILES:
                    pool.wait_ge(den_ready, t + 1)
                    pool.tensor_tensor(
                        E[:, t % 2, 0:PACK].rearrange("p (h j) -> p h j", h=HEADS),
                        E[:, t % 2, 0:PACK].rearrange("p (h j) -> p h j", h=HEADS),
                        rden[:, t % 2, :].unsqueeze(2).to_broadcast([P, HEADS, KEYS]),
                        ALU.mult).then_inc(normed, 1)
                if 0 <= t - 2 < TILES:
                    s = t - 2
                    pool.wait_ge(u_ready, s + 1)
                    do(pool.tensor_tensor(u[:, s % 2, :], u[:, s % 2, :], G[:, :], ALU.mult))
                    do(pool.tensor_tensor(u[:, s % 2, :], u[:, s % 2, :], TB[:, :], ALU.add))
                    pool.tensor_tensor(resid[:, s, :], resid[:, s, :], u[:, s % 2, :],
                                       ALU.add).then_inc(x1_ready, 1)

            pool.wait_ge(flag_ready, 1)
            go = pool.value_load(flag[0:1, 0:1])
            with pool.If(go > 0):
                pool.iota(gidx_i[:, :], pattern=[[1, FULL]], base=0, channel_multiplier=0).then_inc(g_iota, 1)
                pool.iota(gfid_i[:, :], pattern=[[P, FTF]], base=0, channel_multiplier=1).then_inc(g_iota, 1)
                pool.wait_ge(g_iota, 3)
            with pool.Else():
                pool.nop()

        @block.scalar
        def _(act):
            with nc.allow_non_contiguous_dma(reason="columns of parameters"):
                for a, src in enumerate((ln_in_g, ln_in_b)):
                    act.dma_start(in_gb[:, a, :], src.rearrange("(k p) -> p k", p=P)).then_inc(par_in, 16)
                for a, src in enumerate((ln_ctx_g, ln_ctx_b)):
                    act.dma_start(cx_gb[:, a, :], src.rearrange("(k p) -> p k", p=P)).then_inc(par_in, 16)
                for s in range(2):
                    half = slice(HD * s, HD * s + HD)
                    act.dma_start(sc2[half, 0:1], q_scale.rearrange("(p o) -> p o", o=1)).then_inc(par_in, 16)
                    act.dma_start(sc2[half, 1:2], k_scale.rearrange("(p o) -> p o", o=1)).then_inc(par_in, 16)
                    act.dma_start(nv[half, :], null_kv[1, :].rearrange("(p o) -> p o", o=1)).then_inc(par_in, 16)
                act.dma_start(gates[:, 0:1], g_xattn.partition_broadcast(P)).then_inc(gate_in, 16)
                act.dma_start(gates[:, 1:2], g_ffn.partition_broadcast(P)).then_inc(gate_in, 16)
                act.dma_start(G[:, :], ln_out_g.partition_broadcast(P)).then_inc(gate_in, 16)
                act.dma_start(TB[:, :], ln_out_b.partition_broadcast(P)).then_inc(gate_in, 16)
            act.wait_ge(wq_in, 16)
            for k in range(DK):
                act.activation(Wqh[:, k, :], wq_raw[:, k, :], ACT.Copy).then_inc(wq_hi, 1)
            act.wait_ge(gate_in, 16 * 4)
            act.activation(tg, gates, ACT.Tanh).then_inc(tanh_done, 1)
            act.preload_act_table_set("natural_log_exp_and_others")

            def keys():
                for b in range(B):
                    for n in range(2):
                        act.wait_ge(pe_k, 2 * b + n + 1)
                        act.activation(kn[0:J, b, 512 * n:512 * n + 512], ps[0:J, BT[n], :],
                                       ACT.Copy).then_inc(k_copied, 1)
                act.wait_ge(k_copied, 2 * B)
                act.wait_ge(nullk_in, 16 * B)
                act.activation(ksq[:, :, :], kn[:, :, :], ACT.Square).then_inc(k_squared, 1)

            def values():
                act.wait_ge(zeroed, 1)
                for g, (i0, n) in enumerate(VG):
                    act.wait_ge(pe_v, g + 1)
                    for s in range(2):
                        half = slice(HD * s, HD * s + HD)
                        src = ps[half, VBK[g], 0:n * B * J].rearrange("p (i b j) -> p i b j", i=n, b=B)
                        at = P + KEYS * s
                        for b in range(B):
                            act.activation(VB[half, b, i0:i0 + n, at:at + J], src[:, :, b, :],
                                           ACT.Copy).then_inc(vb_ready, 1)

            def values_out(jobs):
                for n in jobs:
                    b, m = VWJ[n]
                    act.wait_ge(pe_vwp, n + 1)
                    act.activation(VWh[:, b, m:m + 2, :], ps[:, BP[n % 2], :].rearrange("p (r c) -> p r c", r=2),
                                   ACT.Copy).then_inc(vw_hi, 1)

            def queries(c, lo, hi):
                if c:
                    act.wait_ge(x1_ready, CT * c - 2)
                for i in range(lo, hi):
                    n = PAIRS * c + i
                    act.wait_ge(pe_q, n + 1)
                    act.activation(qT[:, i, :], ps[:, BP[i % 2], :], ACT.Copy).then_inc(q_copied, 1)
                    if i >= 2:
                        act.wait_ge(pe_ss, n - 1)
                    act.activation(sqh[:, i % 2, :], ps[:, BP[i % 2], :], ACT.Square).then_inc(sq_hi, 1)

            def begin(c):
                for k in range(DK):
                    act.wait_ge(xn_full, DK * c + k + 1)
                    act.activation(xnh[:, k, :], xf[:, k, :], ACT.Copy).then_inc(xn_hi, 1)
                if c == 0:
                    queries(c, 0, 4)
                    keys()
                    queries(c, 4, PAIRS)
                    values()
                else:
                    queries(c, 0, PAIRS)

            def xc_high(cc):
                for h in range(DK):
                    act.wait_ge(pe_cT, DK * cc + h + 1)
                    bank = BP[h] if cc < CH - 1 else BC[h]
                    act.activation(xch[:, h, CW * cc:CW * cc + CW], ps[:, bank, :], ACT.Copy).then_inc(xc_hi, 1)

            for t in steps:
                c, k = t // CT, t % CT
                par = t % 2
                if k == 0 and c < CH:
                    begin(c)
                    act.wait_ge(pe_ss, PAIRS * c + PAIRS)
                if t < TILES:
                    act.wait_ge(scaled, t + 1)
                    act.activation(E[:, par, 0:PACK], E[:, par, 0:PACK], ACT.Exp).then_inc(exped, 1)
                values_out(VWS.get(t, ()))
                if 0 <= t - 2 < TILES:
                    act.wait_ge(pe_vw, t - 1)
                    act.activation(ob[:, par, :], ps[:, BV, 0:D], ACT.Copy).then_inc(o_copied, 1)
                n0, n1 = norms(t)
                if n1 > n0:
                    act.wait_ge(var_ready, t + 1)
                    act.activation(rt_n[:, par, n0:n1], var_n[:, par, n0:n1], ACT.Ln).then_inc(act_chain, 1)
                    act.wait_ge(act_chain, t + 1)
                    act.activation(rs_n[:, par, n0:n1], rt_n[:, par, n0:n1], ACT.Exp, scale=-0.5).then_inc(rs_guess, 1)
                if 0 <= t - 1 < TILES:
                    for g in range(3):
                        n = 3 * (t - 1) + g
                        k0, k1 = 4 * g, min(4 * g + 4, KT)
                        act.wait_ge(pe_pT, n + 1)
                        act.activation(ph[:, k0:k1, :],
                                       ps[:, BT[n % 2], 0:P * (k1 - k0)].rearrange("p (m t) -> p m t", t=P),
                                       ACT.Copy).then_inc(p_hi, 1)
                if k == 3 and 1 <= c < CH:
                    xc_high(c - 1)
                if n1 > n0:
                    act.wait_ge(rs_ready, t + 1)
                if 0 <= t - 2 < TILES:
                    if t >= 4:
                        act.wait_ge(x1_ready, t - 3)
                    act.activation(u[:, par, :], ob[:, par, :], ACT.Identity, scale=rs_n[:, par, 1:2],
                                   bias=nb_n[:, par, 1:2]).then_inc(u_ready, 1)
                if t < TILES - CT:
                    if k == 0:
                        act.wait_ge(pe_xT, DK * (c + 1))
                    act.activation(z[:, k, :], resid[:, t + CT, :], ACT.Identity, scale=rs_n[:, par, 0:1],
                                   bias=nb_n[:, par, 0:1]).then_inc(z_ready, 1)
                if 0 <= t - 3 < TILES:
                    if t - 3 >= CT:
                        act.wait_ge(pe_cT, DK * ((t - 3) // CT))
                    act.activation(zF[:, (t - 3) % CT, :], resid[:, t - 3, :], ACT.Identity, scale=rs_n[:, par, 2:3],
                                   bias=nb_n[:, par, 2:3]).then_inc(zf_ready, 1)
                if t == TILES - 1:
                    act.wait_ge(wm_in, 32)
                    for h in range(DK):
                        act.activation(Wmh[:, h, :], wm_raw[:, h, :], ACT.Copy).then_inc(wmp_hi, 1)
                if t == TILES:
                    act.wait_ge(pe_scores, TILES)
                    for h in range(2):
                        act.activation(Wph[:, 4 * h:4 * h + 4, :], wp_raw[:, 4 * h:4 * h + 4, :],
                                       ACT.Copy).then_inc(wmp_hi, 1)

            for f in range(CH):
                for j in range(FT):
                    n = FT * f + j
                    act.wait_ge(pe_h, n + 1)
                    act.activation(hh[f % 2][:, j, :], ps[:, (BP + BT)[n % 4], :], ACT.Relu,
                                   accum_out=hs[:, j, f:f + 1]).then_inc(h_hi, 1)
                if f == 0:
                    xc_high(CH - 1)
            act.wait_ge(search_pe, 4)
            act.wait_ge(h_lo, FT * CH)
            act.activation(ck[:, 0:1024], ps[:, 0:2, :].rearrange("p b n -> p (b n)"), ACT.Copy).then_inc(ck_copied, 1)
            act.activation(ck[:, 1024:2048], ps[:, 5:7, :].rearrange("p b n -> p (b n)"), ACT.Copy).then_inc(ck_copied, 1)
            act.activation(ck[:, 2048:3072], ps[:, 3:5, :].rearrange("p b n -> p (b n)"), ACT.Copy).then_inc(ck_copied, 1)

            act.wait_ge(flag_ready, 1)
            go = act.value_load(flag[0:1, 0:1])
            with act.If(go > 0):
                with act.Fori(0, 3) as s:
                    with act.Fori(0, FTF) as j:
                        for c in range(CH):
                            act.wait_ge(g_h, CH * (s * FTF + j) + c + 1)
                            act.wait_ge(g_y, CH * (s * FTF + j) + CH)
                            act.sem_inc(held, 1)
                            act.activation(ghm[:, c, :], ps[:, c, :], ACT.Relu,
                                           scale=gmask[:, 0, c // CPB, bass.ds(j, 1)]).then_inc(g_relu, 1)
                    for b in range(B):
                        act.wait_ge(g_pe, s * G_PE + 2 + 2 * b)
                        act.activation(grow[:, :], ps[:, 0:6, :].rearrange("p b n -> p (b n)"),
                                       ACT.Copy).then_inc(g_copy, 1)
            with act.Else():
                act.nop()

        @block.vector
        def _(dve):
            do = Chain(dve, dve_chain).do

            def first_norm(c):
                dve.wait_ge(x_in[c], 16)
                for k in range(CT):
                    do(dve.bn_stats(st_z[:, k, :], resid[:, CT * c + k, :]))
                    do(dve.bn_aggr(mv_z[:, k, :], st_z[:, k, :]))
                do(dve.tensor_scalar(nw_z[:, 0, :], mv_z[:, :, 1], 1.0 + LN_EPS, LN_EPS * LN_EPS, ALU.mult, ALU.add))
                rsqrt(dve, do, nw_z[:, 1, :], nw_z[:, 0, :], nw_z[:, 2, :])
                for k in range(CT):
                    dve.tensor_scalar(z[:, k, :], resid[:, CT * c + k, :], mv_z[:, k, 0:1], nw_z[:, 1, k:k + 1],
                                      ALU.subtract, ALU.mult).then_inc(z_ready, 1)

            def begin(c):
                for k in range(DK):
                    dve.wait_ge(pe_xT, DK * c + k + 1)
                    if c:
                        dve.wait_ge(sq_lo, PAIRS * c)
                    dve.tensor_scalar(xf[:, k, :], ps[:, BP[k], :], in_gb[:, 0, k:k + 1], in_gb[:, 1, k:k + 1],
                                      ALU.mult, ALU.add).then_inc(xn_full, 1)
                dve.wait_ge(xn_lo, DK * c + DK)

            def squares(c, lo, hi):
                for i in range(lo, hi):
                    n = PAIRS * c + i
                    dve.wait_ge(q_copied, n + 1)
                    dve.tensor_tensor(sq[:, i % 2, :], qT[:, i, :], qT[:, i, :], ALU.mult).then_inc(sq_full, 1)
                    dve.wait_ge(sq_full, n + 1)
                    dve.wait_ge(sq_hi, n + 1)
                    dve.tensor_tensor(sql[:, i % 2, :], sq[:, i % 2, :], sqh[:, i % 2, :].bitcast(F32),
                                      ALU.subtract).then_inc(sq_lo, 1)

            def query_norms(c):
                dve.wait_ge(pe_ss, PAIRS * c + PAIRS)
                dve.tensor_copy(ssT[:, :], ps[0:HEADS, BS[2], :]).then_inc(ss_copied, 1)

            def invert_norms(c):
                dve.wait_ge(pe_rT, c + 1)
                dve.tensor_scalar(rqv, ps[:, BP[0], 0:CT * HEADS], NORM_EPS * NORM_EPS, None,
                                  ALU.max).then_inc(sums_read, 1)
                dve.wait_ge(sums_read, c + 1)
                rsqrt(dve, do, rq, rqv, rqt)

            def scale_scores(t):
                k = t % CT
                dve.wait_ge(pe_scores, t + 1)
                w = 2 * GP
                r = rq[:, HEADS * k:HEADS * k + HEADS]
                dve.tensor_tensor(
                    E[:, t % 2, 0:2 * PAIRW * GP].rearrange("p (g h j) -> p g h j", g=2, h=w),
                    ps[:, BS[0]:BS[0] + 2, 0:PAIRW * GP].rearrange("p g (h j) -> p g h j", h=w),
                    r[:, 0:2 * w].rearrange("p (g h) -> p g h", g=2).unsqueeze(3).to_broadcast([P, 2, w, KEYS]),
                    ALU.mult)
                w = HEADS - 2 * w
                dve.tensor_tensor(
                    E[:, t % 2, 2 * PAIRW * GP:PACK].rearrange("p (h j) -> p h j", h=w),
                    ps[:, BS[2], 0:w * KEYS].rearrange("p (h j) -> p h j", h=w),
                    r[:, HEADS - w:].unsqueeze(2).to_broadcast([P, w, KEYS]), ALU.mult).then_inc(scaled, 1)

            def sum_exps(t):
                dve.wait_ge(exped, t + 1)
                do(dve.tensor_reduce(den[:, t % 2, :], E[:, t % 2, 0:PACK].rearrange("p (h j) -> p h j", h=HEADS),
                                     AX.X, ALU.add))
                dve.reciprocal(rden[:, t % 2, :], den[:, t % 2, :]).then_inc(den_ready, 1)

            def stats(t, n):
                if n == 0:
                    if t % CT == 0:
                        dve.wait_ge(x_in[t // CT + 1], 16)
                    v = resid[:, t + CT, :]
                elif n == 1:
                    dve.wait_ge(o_copied, t - 1)
                    v = ob[:, t % 2, :]
                else:
                    dve.wait_ge(x1_ready, t - 2)
                    v = resid[:, t - 3, :]
                do(dve.bn_stats(st_n[:, n, :], v))
                do(dve.bn_aggr(mv_n[:, t % 2, n, :], st_n[:, n, :]))

            def variances(t):
                n0, n1 = norms(t)
                par = t % 2
                if n0 == 0:
                    ins = dve.tensor_scalar(var_n[:, par, 0:1], mv_n[:, par, 0, 1:2], 1.0 + LN_EPS, LN_EPS * LN_EPS,
                                            ALU.mult, ALU.add)
                    if n1 == 1:
                        ins.then_inc(var_ready, 1)
                m0 = max(n0, 1)
                if n1 > m0:
                    dve.tensor_scalar(var_n[:, par, m0:n1], mv_n[:, par, m0:n1, 1], LN_EPS, None,
                                      ALU.add).then_inc(var_ready, 1)

            def inverse_roots(t):
                n0, n1 = norms(t)
                par = t % 2
                y, v, tt = rs_n[:, par, n0:n1], var_n[:, par, n0:n1], rt_n[:, par, n0:n1]
                dve.wait_ge(rs_guess, t + 1)
                do(dve.tensor_tensor(tt, y, y, ALU.mult))
                do(dve.scalar_tensor_tensor(tt, tt, -0.5, v, ALU.mult, ALU.mult))
                do(dve.scalar_tensor_tensor(y, tt, 1.5, y, ALU.add, ALU.mult))
                dve.scalar_tensor_tensor(nb_n[:, par, n0:n1], mv_n[:, par, n0:n1, 0], -1.0, y,
                                         ALU.mult, ALU.mult).then_inc(rs_ready, 1)

            def probs_low(t):
                for g in range(3):
                    n = 3 * t + g
                    k0, k1 = 4 * g, min(4 * g + 4, KT)
                    dve.wait_ge(p_hi, n + 1)
                    dve.tensor_tensor(pl[:, k0:k1, :],
                                      ps[:, BT[n % 2], 0:P * (k1 - k0)].rearrange("p (m t) -> p m t", t=P),
                                      ph[:, k0:k1, :].bitcast(F32), ALU.subtract).then_inc(p_lo, 1)

            def xc_low(cc):
                for h in range(DK):
                    bank = BP[h] if cc < CH - 1 else BC[h]
                    dve.wait_ge(xc_hi, DK * cc + h + 1)
                    dve.tensor_tensor(xcl[:, h, CW * cc:CW * cc + CW], ps[:, bank, :],
                                      xch[:, h, CW * cc:CW * cc + CW].bitcast(F32), ALU.subtract).then_inc(xc_lo, 1)

            def context():
                dve.wait_ge(ctx_dma, 16)
                for b in range(B):
                    do(dve.bn_stats(st_a[0:J, :], cx[:, b, :]))
                    do(dve.bn_aggr(mv_a[0:J, :], st_a[0:J, :]))
                    do(dve.tensor_scalar(nw_a[0:J, 0:1], mv_a[0:J, 1:2], LN_EPS, None, ALU.add))
                    rsqrt(dve, do, nw_a[0:J, 1:2], nw_a[0:J, 0:1], nw_a[0:J, 2:3])
                    dve.tensor_scalar(cz[:, b, :], cx[:, b, :], mv_a[0:J, 0:1], nw_a[0:J, 1:2],
                                      ALU.subtract, ALU.mult).then_inc(cz_ready, 1)
                    dve.wait_ge(cz_ready, b + 1)
                dve.tensor_scalar(qk, sc2[:, 0:1], sc2[:, 1:2], SCALE, ALU.mult, ALU.mult).then_inc(cz_ready, 1)

            def context_turned():
                dve.wait_ge(pe_czT, 1)
                for k in range(DK):
                    dve.tensor_scalar(cT[:, k, :], ps[:, BT[0], B * J * k:B * J * k + B * J],
                                      cx_gb[:, 0, k:k + 1], cx_gb[:, 1, k:k + 1],
                                      ALU.mult, ALU.add).then_inc(cT_ready, 1)

            def null_values():
                dve.wait_ge(zeroed, 1)
                for s in range(2):
                    half = slice(HD * s, HD * s + HD)
                    at = P + KEYS * s + J
                    dst = VB[half, :, :, at:at + 1].rearrange("p b i o -> p (b i) o")
                    dve.tensor_copy(dst, nv[half, :].unsqueeze(1).to_broadcast([HD, B * PAIRS, 1])).then_inc(nullv_put, 1)

            def key_norms():
                dve.wait_ge(k_squared, 1)
                do(dve.tensor_reduce(krt, ksq[:, :, :].rearrange("p b (h d) -> p (b h) d", d=HD), AX.X, ALU.add))
                do(dve.tensor_scalar(kss, krt, NORM_EPS * NORM_EPS, None, ALU.max))
                rsqrt(dve, do, krk, kss, krt)
                kv = kn[:, :, :].rearrange("p b (h d) -> p (b h) d", d=HD)
                dve.tensor_tensor(kv, kv, krk.unsqueeze(2).to_broadcast([KEYS, B * HEADS, HD]),
                                  ALU.mult).then_inc(khat_ready, 1)

            def key_blocks():
                dve.wait_ge(zeroed, 2)
                for b in range(B):
                    for g in range(2):
                        dve.wait_ge(pe_kT, PAIRS * b + 4 * g + 4)
                        for s in range(2):
                            half = slice(HD * s, HD * s + HD)
                            dve.tensor_scalar(KB[half, b, 4 * g:4 * g + 4, KEYS * s:KEYS * s + KEYS],
                                              ps[half, BT[g], 0:4 * KEYS].rearrange("p (i j) -> p i j", i=4),
                                              qk[half, :], None, ALU.mult).then_inc(kb_ready, 1)

            def values_low(jobs):
                for n in jobs:
                    b, m = VWJ[n]
                    dve.wait_ge(vw_hi, n + 1)
                    dve.tensor_tensor(VWl[:, b, m:m + 2, :], ps[:, BP[n % 2], :].rearrange("p (r c) -> p r c", r=2),
                                      VWh[:, b, m:m + 2, :].bitcast(F32), ALU.subtract).then_inc(vw_lo, 1)

            first_norm(0)
            dve.wait_ge(par_in, 16 * 10)
            context()
            dve.wait_ge(wq_hi, DK)
            for h in range(DK):
                dve.tensor_tensor(Wql[:, h, :], wq_raw[:, h, :], Wqh[:, h, :].bitcast(F32),
                                  ALU.subtract).then_inc(wq_lo, 1)
            for t in steps:
                c, k = t // CT, t % CT
                if k == 0 and c < CH:
                    begin(c)
                    if c == 0:
                        context_turned()
                        squares(c, 0, 4)
                        null_values()
                        key_norms()
                        squares(c, 4, PAIRS)
                        query_norms(c)
                        key_blocks()
                    else:
                        squares(c, 0, PAIRS)
                        query_norms(c)
                    invert_norms(c)
                if t < TILES:
                    scale_scores(t)
                if t < TILES - CT:
                    stats(t, 0)
                if 0 <= t - 3 < TILES:
                    stats(t, 2)
                if 0 <= t - 2 < TILES:
                    stats(t, 1)
                variances(t)
                values_low(VWS.get(t, ()))
                if t < TILES:
                    sum_exps(t)
                if norms(t)[1] > norms(t)[0]:
                    inverse_roots(t)
                if 0 <= t - 1 < TILES:
                    probs_low(t - 1)
                if k == 3 and 1 <= c < CH:
                    xc_low(c - 1)
                if t == TILES - 1:
                    dve.wait_ge(wmp_hi, DK)
                    for h in range(DK):
                        dve.tensor_tensor(Wml[:, h, :], wm_raw[:, h, :], Wmh[:, h, :].bitcast(F32),
                                          ALU.subtract).then_inc(wmp_lo, 1)
                if t == TILES:
                    dve.wait_ge(wmp_hi, DK + 2)
                    for h in range(2):
                        dve.tensor_tensor(Wpl[:, 4 * h:4 * h + 4, :], wp_raw[:, 4 * h:4 * h + 4, :],
                                          Wph[:, 4 * h:4 * h + 4, :].bitcast(F32), ALU.subtract).then_inc(wmp_lo, 1)

            def h_low(f):
                for j in range(FT):
                    n = FT * f + j
                    dve.wait_ge(h_hi, n + 1)
                    dve.scalar_tensor_tensor(hl[f % 2][:, j, :], ps[:, (BP + BT)[n % 4], :], 0.0,
                                             hh[f % 2][:, j, :].bitcast(F32), ALU.max, ALU.subtract).then_inc(h_lo, 1)

            def add_ffn(f):
                if f >= 2:
                    dve.wait_ge(y_out[f - 2], 16)
                for k in range(CT):
                    t = CT * f + k
                    dve.wait_ge(pe_y, t + 1)
                    dve.scalar_tensor_tensor(yo[:, f % 2, k, :], ps[:, BY[t % 2], 0:D], tg[:, 1:2],
                                             resid[:, t, :], ALU.mult, ALU.add).then_inc(y_ready, 1)

            h_low(0)
            xc_low(CH - 1)
            add_ffn(0)
            h_low(1)
            add_ffn(1)
            h_low(2)
            h_low(3)
            dve.tensor_reduce(hb[:, :, :], hs[:, :, :].rearrange("p j (b c) -> p j b c", b=B), AX.X,
                              ALU.add).then_inc(search_dve, 1)
            add_ffn(2)
            bm, lo, w, pid, thr, cnt, ind, c_old, c_new, short = (srch[:, n:n + 1] for n in range(10))
            dve.wait_ge(search_pe, 1)
            dve.tensor_scalar(pooled[:, :], ps[0:B, BC[0], 0:D], 1.0 / N, None, ALU.mult).then_inc(search_dve, 1)
            dve.wait_ge(search_pe, 2)
            dve.tensor_copy(plT[:, :, :].rearrange("p k b -> p (k b)"), ps[:, BC[1], 0:DK * B]).then_inc(search_dve, 1)
            dve.wait_ge(search_pe, 3)
            for b in range(B):
                dve.tensor_scalar(rT[:, HD * b:HD * b + HD], ps[0:HID, BC[0], b:b + 1].to_broadcast([HID, HD]),
                                  0.0, None, ALU.max).then_inc(search_dve, 1)
            add_ffn(3)
            dve.wait_ge(g_iota, 1)
            do(dve.tensor_copy(pid, part_i[:, :]))
            do(dve.tensor_scalar(thr, pid, SPREAD - 0.5, -float(SPREAD), ALU.is_gt, ALU.mult))
            do(dve.scalar_tensor_tensor(pid, pid, 1.0, thr, ALU.add, ALU.add))
            dve.wait_ge(ck_copied, 3)
            do(dve.tensor_reduce(bm, ck[:, :], AX.X, ALU.max, apply_absolute_value=True))
            do(dve.tensor_scalar(lo, bm, -1.01, -1e-30, ALU.mult, ALU.add))
            do(dve.tensor_scalar(w, bm, 2.02 / SPREAD, 2e-30 / SPREAD, ALU.mult, ALU.add))
            for n in range(2):
                do(dve.tensor_scalar(thr, pid, w, lo, ALU.mult, ALU.add))
                do(dve.tensor_scalar(over[:, :], ck[:, :], thr, None, ALU.is_gt, ALU.add, accum_out=cnt))
                dve.tensor_scalar(ind, cnt, ITER - 0.5, None, ALU.is_gt).then_inc(search_dve, 1)
                dve.wait_ge(search_pe, 5 + n)
                do(dve.tensor_scalar(lo, ps[:, BC[0], 0:1], w, lo, ALU.mult, ALU.add))
                do(dve.tensor_scalar(w, w, 1.0 / SPREAD, None, ALU.mult))
            do(dve.tensor_scalar(over[:, 0:ITER], ck[:, 0:ITER], lo, None, ALU.is_gt, ALU.add, accum_out=c_old))
            do(dve.tensor_scalar(over[:, ITER:FULL], ck[:, ITER:FULL], lo, None, ALU.is_gt, ALU.add, accum_out=c_new))
            do(dve.tensor_tensor(cnt, c_old, c_new, ALU.add))
            dve.tensor_scalar(short, cnt, ITER - 0.5, None, ALU.is_lt).then_inc(search_dve, 1)
            dve.wait_ge(search_pe, 7)
            do(dve.tensor_copy(srch[0:1, 10:12], ps[0:1, BC[1], 0:2]))
            do(dve.tensor_scalar(srch[0:1, 12:13], srch[0:1, 11:12], float(FULL), srch[0:1, 10:11],
                                 ALU.mult, ALU.add))
            dve.tensor_scalar(flag[:, :], srch[0:1, 12:13], NEW_MAX, None, ALU.is_gt).then_inc(flag_ready, 1)
            dve.wait_ge(flag_ready, 1)

            go = dve.value_load(flag[0:1, 0:1])
            with dve.If(go > 0):
                general_dve(dve)
            with dve.Else():
                dve.nop()

        @block.tensor
        def _(pe):
            def three(dst, lh, ll, rh, rl, first, last):
                pe.matmul(dst, lh, rh, start=first, stop=False)
                pe.matmul(dst, lh, rl, start=False, stop=False)
                return pe.matmul(dst, ll, rh, start=False, stop=last)

            def sums(c, i):
                pe.wait_ge(sq_hi, PAIRS * c + i + 1)
                pe.wait_ge(sq_lo, PAIRS * c + i + 1)
                dst = ps[0:HEADS, BS[2], :]
                pe.matmul(dst, head_of[:, i, :], sqh[:, i % 2, :], start=i == 0, stop=False)
                pe.matmul(dst, head_of[:, i, :], sql[:, i % 2, :], start=False, stop=i == PAIRS - 1).then_inc(pe_ss, 1)

            def queries(c, lo, hi):
                for i in range(lo, hi):
                    if i >= 2:
                        pe.wait_ge(sq_hi, PAIRS * c + i - 1)
                    for k in range(DK):
                        w = slice(P * i, P * i + P)
                        mm = three(ps[:, BP[i % 2], :], Wqh[:, k, w], Wql[:, k, w], xnh[:, k, :], xnl[:, k, :],
                                   k == 0, k == DK - 1)
                    mm.then_inc(pe_q, 1)
                    if i:
                        sums(c, i - 1)

            def begin(c):
                if c == 0:
                    pe.wait_ge(consts, 1)
                if c >= 2:
                    pe.wait_ge(xc_lo, DK * (c - 1))
                elif c == 1:
                    pe.wait_ge(sums_read, 1)
                for h in range(DK):
                    for k in range(CT):
                        if h == 0:
                            pe.wait_ge(z_ready, CT * c + k + 1)
                        mm = pe.transpose(ps[:, BP[h], P * k:P * k + P], z[:, k, P * h:P * h + P], ident[:, :])
                    mm.then_inc(pe_xT, 1)
                if c == 0:
                    context_turn()
                pe.wait_ge(xn_hi, DK * c + DK)
                pe.wait_ge(xn_lo, DK * c + DK)
                if c == 0:
                    pe.wait_ge(wq_lo, DK)
                    pe.wait_ge(wq_hi, DK)
                    pe.wait_ge(head_ready, 1)
                    queries(c, 0, 4)
                    keys()
                    queries(c, 4, PAIRS)
                    sums(c, PAIRS - 1)
                    values()
                    key_turns()
                    pe.wait_ge(kb_ready, 4 * B)
                else:
                    pe.wait_ge(scaled, CT * c)
                    queries(c, 0, PAIRS)
                    sums(c, PAIRS - 1)
                pe.wait_ge(ss_copied, c + 1)
                for k in range(CT):
                    mm = pe.transpose(ps[:, BP[0], HEADS * k:HEADS * k + HEADS], ssT[:, P * k:P * k + P],
                                      ident[0:HEADS, 0:HEADS])
                mm.then_inc(pe_rT, 1)

            def context_turn():
                pe.wait_ge(cz_ready, B)
                for k in range(DK):
                    for b in range(B):
                        mm = pe.transpose(ps[:, BT[0], J * (B * k + b):J * (B * k + b) + J],
                                          cz[:, b, P * k:P * k + P], ident[0:J, 0:J])
                mm.then_inc(pe_czT, 1)

            def keys():
                pe.wait_ge(cT_ready, DK)
                pe.wait_ge(wk_in, 16)
                for b in range(B):
                    for n in range(2):
                        if b:
                            pe.wait_ge(k_copied, 2 * b - 1 + n)
                        for k in range(DK):
                            mm = pe.matmul(ps[0:J, BT[n], :], cT[:, k, J * b:J * b + J],
                                           Wkv_s[:, k, 512 * n:512 * n + 512], start=k == 0, stop=k == DK - 1)
                        mm.then_inc(pe_k, 1)

            def values():
                pe.wait_ge(wv_in, 16)
                for g, (i0, n) in enumerate(VG):
                    for i in range(n):
                        for k in range(DK):
                            at = INNER + P * (i0 + i)
                            mm = pe.matmul(ps[:, VBK[g], B * J * i:B * J * i + B * J], Wkv_s[:, k, at:at + P],
                                           cT[:, k, :], start=k == 0, stop=k == DK - 1)
                    mm.then_inc(pe_v, 1)

            def key_turns():
                pe.wait_ge(khat_ready, 1)
                for b in range(B):
                    for i in range(PAIRS):
                        if b and i % 4 == 0:
                            pe.wait_ge(kb_ready, 2 * (i // 4) + 2)
                        pe.transpose(ps[:, BT[i // 4], KEYS * (i % 4):KEYS * (i % 4) + KEYS],
                                     kn[:, b, P * i:P * i + P], ident[0:KEYS, 0:KEYS]).then_inc(pe_kT, 1)

            def values_times_wo(jobs):
                if 0 in jobs:
                    pe.wait_ge(vb_ready, len(VG) * 2 * B)
                    pe.wait_ge(nullv_put, 2)
                    pe.wait_ge(wo_in, 16)
                for n in jobs:
                    b, m = VWJ[n]
                    if n >= 2:
                        pe.wait_ge(vw_lo, n - 1)
                    for r in range(2):
                        lo, hi = P * (m + r), min(P * (m + r) + P, PACK)
                        over = [i for i in range(PAIRS) if PAIRW * i < hi and PAIRW * (i + 1) > lo]
                        for i in over:
                            at = P + lo - PAIRW * i
                            mm = pe.matmul(ps[:, BP[n % 2], D * r:D * r + D], VB[:, b, i, at:at + P],
                                           Wo_s[:, i, :], start=i == over[0], stop=i == over[-1])
                    mm.then_inc(pe_vwp, 1)

            def scores(t):
                k, b = t % CT, t // CT // CPB
                if t:
                    pe.wait_ge(scaled, t)
                else:
                    pe.wait_ge(vb_ready, len(VG) * 2 * B)
                pe.wait_ge(q_copied, PAIRS * (t // CT + 1))
                for g, n in SG:
                    for i in range(GP * g, GP * g + n):
                        at = PAIRW * (i - GP * g)
                        mm = pe.matmul(ps[:, BS[g], at:at + PAIRW], qT[:, i, P * k:P * k + P], KB[:, b, i, :],
                                       start=True, stop=True)
                mm.then_inc(pe_scores, 1)

            def attend(t):
                b = t // CT // CPB
                pe.wait_ge(p_hi, 3 * t + 3)
                pe.wait_ge(p_lo, 3 * t + 3)
                if t % (TILES // B) == 0:
                    pe.wait_ge(vw_lo, (b + 1) * len(VWJ) // B)
                if t:
                    pe.wait_ge(o_copied, t)
                dst = ps[:, BV, 0:D]
                for m in range(KT):
                    mm = three(dst, ph[:, m, :], pl[:, m, :], VWh[:, b, m, :], VWl[:, b, m, :],
                               m == 0, m == KT - 1)
                mm.then_inc(pe_vw, 1)

            def turn_probs(t):
                if t < 2:
                    pe.wait_ge(e_zeroed, 1)
                pe.wait_ge(normed, t + 1)
                for g in range(3):
                    n = 3 * t + g
                    if n >= 2:
                        pe.wait_ge(p_lo, n - 1)
                    for m in range(4 * g, min(4 * g + 4, KT)):
                        mm = pe.transpose(ps[:, BT[n % 2], P * (m - 4 * g):P * (m - 4 * g) + P],
                                          E[:, t % 2, P * m:P * m + P], ident[:, :])
                    mm.then_inc(pe_pT, 1)

            def turn_ffn_in(cc):
                pe.wait_ge(zf_ready, CT * cc + CT)
                if cc < CH - 1:
                    pe.wait_ge(sums_read, cc + 2)
                for h in range(DK):
                    bank = BP[h] if cc < CH - 1 else BC[h]
                    for k in range(CT):
                        mm = pe.transpose(ps[:, bank, P * k:P * k + P], zF[:, k, P * h:P * h + P], ident[:, :])
                    mm.then_inc(pe_cT, 1)

            for t in steps:
                c, k = t // CT, t % CT
                if t > TILES + 1:
                    break
                if k == 0 and c < CH:
                    begin(c)
                if t < TILES:
                    scores(t)
                if t in VWS:
                    pe.wait_ge(sums_read, c + 1)
                    values_times_wo(VWS[t])
                if k == 3 and 1 <= c < CH:
                    turn_ffn_in(c - 1)
                if 0 <= t - 2 < TILES:
                    attend(t - 2)
                if 0 <= t - 1 < TILES:
                    turn_probs(t - 1)

            def hidden(f):
                if f == 0:
                    pe.wait_ge(wmp_lo, DK)
                pe.wait_ge(xc_hi, DK * (f + 1))
                pe.wait_ge(xc_lo, DK * (f + 1))
                for j in range(FT):
                    n = FT * f + j
                    if n >= 4:
                        pe.wait_ge(h_lo, n - 3)
                    else:
                        pe.wait_ge(p_lo, 3 * TILES)
                        pe.wait_ge(xc_lo, DK * (CH - 1))
                    for k in range(DK):
                        w = slice(P * j, P * j + P)
                        mm = three(ps[:, (BP + BT)[n % 4], :], Wmh[:, k, w], Wml[:, k, w],
                                   xch[:, k, CW * f:CW * f + CW], xcl[:, k, CW * f:CW * f + CW],
                                   k == 0, k == DK - 1)
                    mm.then_inc(pe_h, 1)

            def project(f):
                if f == 0:
                    pe.wait_ge(wmp_lo, DK + 2)
                for k in range(CT):
                    t = CT * f + k
                    if t >= 2:
                        pe.wait_ge(y_ready, t - 1)
                    for j in range(FT):
                        pe.wait_ge(h_lo, FT * f + j + 1)
                        w = slice(P * k, P * k + P)
                        mm = three(ps[:, BY[t % 2], 0:D], hh[f % 2][:, j, w], hl[f % 2][:, j, w],
                                   Wph[:, j, :], Wpl[:, j, :], j == 0, j == FT - 1)
                    mm.then_inc(pe_y, 1)

            hidden(0)
            turn_ffn_in(CH - 1)
            project(0)
            hidden(1)
            project(1)
            hidden(2)
            hidden(3)
            project(2)
            pe.wait_ge(search_dve, 1)
            pe.wait_ge(wc_in, 32)
            for j in range(FT):
                mm = pe.matmul(ps[0:B, BC[0], 0:D], hb[:, j, :], wp_raw[:, j, :], start=j == 0, stop=j == FT - 1)
            mm.then_inc(search_pe, 1)
            pe.wait_ge(search_dve, 2)
            for k in range(DK):
                mm = pe.transpose(ps[:, BC[1], B * k:B * k + B], pooled[:, P * k:P * k + P], ident[0:B, 0:B])
            mm.then_inc(search_pe, 1)
            pe.wait_ge(search_dve, 3)
            for k in range(DK):
                mm = pe.matmul(ps[0:HID, BC[0], 0:B], w_c1[:, k, :], plT[:, k, :], start=k == 0, stop=k == DK - 1)
            mm.then_inc(search_pe, 1)
            pe.wait_ge(search_dve, 3 + B)
            for j, bank in enumerate((0, 1, 5, 6, 3, 4)):
                mm = pe.matmul(ps[:, bank, :], rT[:, :], w_c2[:, 512 * j:512 * j + 512], start=True, stop=True)
            mm.then_inc(search_pe, 1)
            project(3)
            for n in range(2):
                pe.wait_ge(search_dve, 4 + B + n)
                pe.matmul(ps[:, BC[0], 0:1], ones_b[:, :], srch[:, 6:7], start=True, stop=True).then_inc(search_pe, 1)
            pe.wait_ge(search_dve, 6 + B)
            for n in range(2):
                for h in range(B):
                    mm = pe.matmul(ps[0:1, BC[1], n:n + 1], ident[:, HD * h:HD * h + 1], srch[:, 8 + n:9 + n],
                                   start=h == 0, stop=h == B - 1)
            mm.then_inc(search_pe, 1)

            pe.wait_ge(flag_ready, 1)
            go = pe.value_load(flag[0:1, 0:1])
            with pe.If(go > 0):
                with pe.Fori(0, 3) as s:
                    pe.wait_ge(g_small, s * G_SMALL + 1)
                    pe.sem_inc(held, 1)
                    with pe.Fori(0, FTF) as j:
                        n0 = CH * (s * FTF + j)
                        pe.wait_ge(g_w, (s * FTF + j) * 32 + 32)
                        pe.wait_ge(g_relu, n0 + CH)
                        for c in range(CH):
                            for k in range(DK):
                                mm = pe.matmul(ps[:, c, :], gwm[:, k, :], gx[:, k, CW * c:CW * c + CW],
                                               start=k == 0, stop=k == DK - 1)
                            mm.then_inc(g_h, 1)
                        for c in range(CH):
                            pe.wait_ge(g_relu, n0 + CH + c + 1)
                            pe.wait_ge(g_add, n0 + CH + c - 1)
                            for k in range(DK):
                                mm = pe.matmul(ps[:, 4 + 2 * (c % 2) + k, :], gwp[:, P * k:P * k + P], ghm[:, c, :],
                                               start=True, stop=True)
                            mm.then_inc(g_y, 1)
                    pe.wait_ge(g_small, s * G_SMALL + 2)
                    for k in range(DK):
                        mm = pe.matmul(ps[0:HID, 7, 0:B], w_c1[:, k, :], gs[:, 8 + B * k:8 + B * k + B],
                                       start=k == 0, stop=k == DK - 1)
                    mm.then_inc(g_pe, 1)
                    pe.wait_ge(g_small, s * G_SMALL + 3)
                    for b in range(B):
                        if b:
                            pe.wait_ge(g_small, s * G_SMALL + 3 + b)
                        for j in range(6):
                            mm = pe.matmul(ps[:, j, :], gr[:, b, :], w_c2[:, 512 * j:512 * j + 512],
                                           start=True, stop=True)
                        mm.then_inc(g_pe, 1)
                        pe.wait_ge(g_copy, s * B + b + 1)
                        pe.sem_inc(held, 1)
                        for j in range(FTF):
                            mm = pe.transpose(ps[:, 6, j:j + 1], grow[0:1, P * j:P * j + P], ident[0:1, 0:1])
                        mm.then_inc(g_pe, 1)
                    pe.wait_ge(g_small, s * G_SMALL + 4 + B)
                    pe.matmul(ps[:, 7, 0:1], gones[:, :], gs[:, 3:4], start=True, stop=True).then_inc(g_pe, 1)
                pe.wait_ge(g_small, 3 * G_SMALL + 1)
                for t in range(TILES):
                    if t >= 2:
                        pe.wait_ge(g_out, t - 1)
                    for k in range(DK):
                        mm = pe.transpose(ps[:, t % 2, P * k:P * k + P], gx[:, k, P * t:P * t + P], ident[:, :])
                    mm.then_inc(g_pe, 1)
            with pe.Else():
                pe.nop()


_INS = ["x", "ctx_1024", "g_xattn", "g_ffn", "L0_xattn_Wq", "L0_xattn_Wkv", "L0_xattn_Wo", "L0_xattn_null_kv",
        "L0_xattn_q_scale", "L0_xattn_k_scale", "L0_xattn_ln_in_g", "L0_xattn_ln_in_b", "L0_xattn_ln_ctx_g",
        "L0_xattn_ln_ctx_b", "L0_xattn_ln_out_g", "L0_xattn_ln_out_b", "L0_ffn_Wm", "L0_ffn_Wp", "L0_ffn_Wc1",
        "L0_ffn_Wc2"]


def kernel(**inputs):
    import numpy as _np
    import concourse.bacc as _bacc
    from concourse import mybir as _mybir
    from concourse.bass_utils import run_bass_kernel_spmd as _run

    nc = _bacc.Bacc("TRN2", target_bir_lowering=False, num_devices=1)
    arrays, args = {}, []
    for name in _INS:
        a = _np.asarray(inputs[name])
        if name.startswith("L0_ffn_"):
            a = a.T
        a = _np.ascontiguousarray(a)
        arrays[f"in_{name}_dram"] = a
        args.append(nc.dram_tensor(f"in_{name}_dram", a.shape, _mybir.dt.from_np(a.dtype), kind="ExternalInput").ap())
    shape = inputs["x"].shape
    args.append(nc.dram_tensor("out_0_dram", shape, _mybir.dt.float32, kind="ExternalOutput").ap())
    flamingo_block(nc, *args)
    r = _run(nc, [arrays], core_ids=[0])
    return r.results[0]["out_0_dram"]
```

```python
from contextlib import ExitStack

import concourse.bass as bass
from concourse import mybir

F32 = mybir.dt.float32
F32R = mybir.dt.float32r
I32 = mybir.dt.int32
ALU = mybir.AluOpType
ACT = mybir.ActivationFunctionType
AX = mybir.AxisListType

P = 128
HEADS, HD = 16, 64
SCALE = 8.0
LN_EPS = 1e-5
NORM_EPS = 1e-12
R = 0.7
RSQRT_GUESS = float(0x5F3759DF)
SPREAD = 64


class Chain:

    def __init__(self, eng, sem):
        self.eng, self.sem, self.n = eng, sem, 0

    def put(self, instruction):
        self.n += 1
        instruction.then_inc(self.sem, 1)

    def do(self, instruction):
        self.put(instruction)
        self.eng.wait_ge(self.sem, self.n)


def rsqrt(dve, do, y, v, t):
    yi = y.bitcast(I32)
    do(dve.tensor_scalar(yi, v.bitcast(I32), 1, None, ALU.arith_shift_right))
    do(dve.tensor_scalar(yi, yi, -1.0, RSQRT_GUESS, ALU.mult, ALU.add))
    for _ in range(3):
        do(dve.tensor_tensor(t, y, y, ALU.mult))
        do(dve.scalar_tensor_tensor(t, t, -0.5, v, ALU.mult, ALU.mult))
        do(dve.scalar_tensor_tensor(y, t, 1.5, y, ALU.add, ALU.mult))


def flamingo_block(nc, x, ctx_in, g_xattn, g_ffn, Wq, Wkv, Wo, null_kv, q_scale, k_scale,
                   ln_in_g, ln_in_b, ln_ctx_g, ln_ctx_b, ln_out_g, ln_out_b,
                   WmT, WpT, Wc1T, Wc2T, out):
    B, N, D = x.shape
    J = ctx_in.shape[1]
    KEYS = J + 1
    PACK = HEADS * KEYS
    KT = (PACK + P - 1) // P
    PAIRS = HEADS // 2
    INNER = HEADS * HD
    TILES = B * N // P
    CT = 4
    CW = CT * P
    CH = TILES // CT
    CPB = CH // B
    DK = D // P
    FULL = WmT.shape[1]
    ITER = FULL // 3
    FT = ITER // P
    FTF = FULL // P
    HID = Wc1T.shape[1]
    PAIRW = 2 * KEYS
    PADW = P + PAIRW + P
    WIN = 256
    QT = 2
    QW = QT * P
    QC = TILES // QT
    QPB = QC // B
    QG = PAIRS // 2
    NEW_MAX = R * ITER * B

    xt = x.rearrange("b (c k p) d -> (b c) p k d", p=P, k=CT)
    ot = out.rearrange("b (c k p) d -> (b c) p k d", p=P, k=CT)
    wm_v = WmT.rearrange("(k p) f -> p k f", p=P)
    wp_v = WpT.rearrange("(j p) c -> p j c", p=P)

    es = ExitStack()
    with es:
        def sem(name):
            return es.enter_context(nc.semaphore(name))

        LO = 16512
        END = nc.sbuf_usable_end
        top = [LO]

        def place(name, shape, dt, offset=None):
            nbytes = 4
            for s in shape[1:]:
                nbytes *= s
            nbytes = (nbytes + 31) // 32 * 32
            if offset is None:
                offset = top[0]
                top[0] += nbytes
                assert top[0] <= END, (name, top[0], END)
            assert offset + nbytes <= END, name
            return nc.alloc_sbuf_tensor_at(name, shape, dt, offset=offset)

        es.enter_context(nc.sbuf_tensor("fence", [P, (END - LO) // 4 - 8], F32))

        ident = place("ident", [P, P], F32)
        ones_b = place("ones_b", [P, P], F32)
        head_f = place("head_f", [P, PAIRS, HEADS], F32)
        head_of = place("head_of", [P, PAIRS, HEADS], F32R)
        small = place("small", [P, 624], F32)
        ssT = place("ssT", [HEADS, QW], F32)
        part_i = place("part_i", [P, 1], I32)
        flag = place("flag", [1, 1], I32)
        G = place("G", [P, D], F32)
        TB = place("TB", [P, D], F32)
        resid = place("resid", [P, TILES, D], F32)
        o_kb = top[0]
        KBh = place("KBh", [P, B * PAIRS * PAIRW + WIN - PAIRW], F32R)
        KBl = place("KBl", [P, B * PAIRS * PAIRW + WIN - PAIRW], F32R)
        o_vw = top[0]
        VWh = place("VWh", [P, B, KT, D], F32R)
        VWl = place("VWl", [P, B, KT, D], F32R)
        o_wq = top[0]
        Wqh = place("Wqh", [P, DK, INNER], F32R)
        Wql = place("Wql", [P, DK, INNER], F32R)
        o_q = top[0]
        qh, ql = [], []
        for a in range(2):
            qh.append(place(f"qh{a}", [P, PAIRS, QW], F32R))
            ql.append(place(f"ql{a}", [P, PAIRS, QW], F32R))
        E = place("E", [P, 2, KT * P], F32)
        o_p = top[0]
        ph = place("ph", [P, KT, P], F32R)
        pl = place("pl", [P, KT, P], F32R)
        o_z = top[0]
        z = place("z", [P, CT, D], F32)
        o_sq = top[0]
        sq = place("sq", [P, 2 * QW], F32)
        sqh = place("sqh", [P, 2, 2 * QW], F32R)
        sql = place("sql", [P, 2 * QW], F32R)
        qf = place("qf", [P, 2 * QW], F32)
        o_xn = top[0]
        xf = place("xf", [P, DK, QW], F32)
        xnh = place("xnh", [P, DK, QW], F32R)
        xnl = place("xnl", [P, DK, QW], F32R)
        o_ob = top[0]
        ob = place("ob", [P, 2, D], F32)
        o_u = top[0]
        u = place("u", [P, 2, D], F32)
        o_xc = top[0]
        xch = place("xch", [P, 2, DK, CW], F32R)
        xcl = place("xcl", [P, 2, DK, CW], F32R)
        o_raw = top[0]
        wm_raw = place("wm_raw", [P, DK, ITER], F32)
        o_wp = top[0]
        wp_raw = place("wp_raw", [P, FT, D], F32)
        Wo_s = place("Wo_s", [P, PAIRS, D], F32, o_raw)
        VB = place("VB", [P, PAIRS, PADW], F32, o_xc)
        VC = place("VC", [P, PAIRS, J], F32, o_xc + PAIRS * PADW * 4)
        assert o_xc + PAIRS * (PADW + J) * 4 <= o_raw
        wq_raw = place("wq_raw", [P, DK, INNER], F32, o_vw)
        Wkv_s = place("Wkv_s", [P, DK, 2 * INNER], F32, o_q + 2 * PAIRS * QW * 4)
        kn = place("kn", [KEYS, B, INNER], F32, o_wp)
        ksq = place("ksq", [KEYS, B, INNER], F32, o_p)
        cT = place("cT", [P, DK, B * J], F32, o_p + B * INNER * 4)
        assert B * INNER * 4 + DK * B * J * 4 <= 2 * KT * P * 4
        cx = place("cx", [J, B, D], F32, o_ob)
        cz = place("cz", [J, B, D], F32, o_u)
        Wmh = place("Wmh", [P, DK, ITER], F32R, o_wq)
        Wml = place("Wml", [P, DK, ITER], F32R, o_wq + DK * ITER * 4)
        Wph = place("Wph", [P, FT, D], F32R, o_q)
        Wpl = place("Wpl", [P, FT, D], F32R, o_q + FT * D * 4)
        hw = FT * CW * 4
        hh = [place("hh0", [P, FT, CW], F32R, o_vw), place("hh1", [P, FT, CW], F32R, o_q + hw)]
        hl = [place("hl0", [P, FT, CW], F32R, o_vw + B * KT * D * 4), place("hl1", [P, FT, CW], F32R, o_q + 2 * hw)]
        o_ck = o_vw + B * KT * D * 4 + hw
        assert 2 * FT * D * 4 <= hw <= B * KT * D * 4 and o_ck <= o_wq and o_q + 3 * hw <= o_z
        EARLY = KT * D // CW
        zF = place("zF", [P, CT, D], F32, o_sq)
        w_c2 = place("w_c2", [HID, FULL], F32, o_xc - FULL * 4)
        assert o_xc - FULL * 4 >= o_sq + CT * D * 4
        w_c1 = place("w_c1", [P, DK, HID], F32, o_z)
        rT = place("rT", [HID, P], F32, o_z + DK * HID * 4)
        pooled = place("pooled", [B, D], F32, o_z + DK * HID * 4 + P * 4)
        yo = place("yo", [P, 2, CT, D], F32, o_raw)
        ck = place("ck", [P, FULL], F32, o_ck)
        over = place("over", [P, FULL], F32, o_kb)
        assert o_ck + FULL * 4 <= o_wq + 2 * DK * ITER * 4 and FULL * 4 <= o_vw - o_kb

        ps = es.enter_context(nc.psum_tensor("ps", [P, 8, 512], F32))
        BQ = 0
        BX = 1
        BS = (2, 3, 4)
        BT = (5, 6)
        BV = 7
        BH = (0, 1, 5, 6)
        BY = (2, 7)
        BC = (3, 4)
        BCF = ((0, 1), (3, 4), (3, 4), (3, 4))

        col = {}
        used = [0]

        def cols(name, n):
            col[name] = slice(used[0], used[0] + n)
            used[0] += n
            return small[:, col[name]]

        gates = cols("gates", 2)
        tg = cols("tg", 2)
        in_gb = cols("in_gb", 2 * DK).rearrange("p (a k) -> p a k", a=2)
        cx_gb = cols("cx_gb", 2 * DK).rearrange("p (a k) -> p a k", a=2)
        sc2 = cols("sc2", 2)
        qk = cols("qk", 1)
        nv = cols("nv", 1)
        st_a = cols("st_a", 6 * B).rearrange("p (b s) -> p b s", b=B)
        mv_a = cols("mv_a", 2 * B).rearrange("p (b s) -> p b s", b=B)
        nw_a = cols("nw_a", 3 * B).rearrange("p (s b) -> p s b", b=B)
        st_n = cols("st_n", 18).rearrange("p (n s) -> p n s", n=3)
        mv_n = cols("mv_n", 12).rearrange("p (q n s) -> p q n s", q=2, n=3)
        var_n = cols("var_n", 6).rearrange("p (q n) -> p q n", q=2)
        rs_n = cols("rs_n", 3 * (TILES + 3)).rearrange("p (t n) -> p t n", n=3)
        nb_n = cols("nb_n", 3 * (TILES + 3)).rearrange("p (t n) -> p t n", n=3)
        rt_n = cols("rt_n", 6).rearrange("p (q n) -> p q n", q=2)
        rs_f, nb_f = (a[:, 3:, 2] for a in (rs_n, nb_n))
        st_z = cols("st_z", 6 * CT).rearrange("p (k s) -> p k s", k=CT)
        mv_z = cols("mv_z", 2 * CT).rearrange("p (k s) -> p k s", k=CT)
        nw_z = cols("nw_z", 3 * CT).rearrange("p (s k) -> p s k", s=3)
        rq = cols("rq", QT * HEADS)
        rqv = cols("rqv", QT * HEADS)
        rqt = cols("rqt", QT * HEADS)
        den = cols("den", 2 * HEADS).rearrange("p (a h) -> p a h", a=2)
        rden = cols("rden", 2 * HEADS).rearrange("p (a h) -> p a h", a=2)
        kss = cols("kss", B * HEADS)[0:KEYS]
        krk = cols("krk", B * HEADS)[0:KEYS]
        krt = cols("krt", B * HEADS)[0:KEYS]
        hs = cols("hs", FT * CH).rearrange("p (j c) -> p j c", j=FT)
        hb = cols("hb", FT * B).rearrange("p (j b) -> p j b", j=FT)
        plT = cols("plT", DK * B).rearrange("p (k b) -> p k b", k=DK)
        srch = cols("srch", 16)
        cmax = cols("cmax", 3)
        assert used[0] <= 624, used[0]
        g_at = [o_kb]

        def later(name, shape, dt=F32):
            nbytes = 4
            for s in shape[1:]:
                nbytes *= s
            nbytes = (nbytes + 31) // 32 * 32
            g_at[0] += nbytes
            assert g_at[0] <= o_z, name
            return place(name, shape, dt, g_at[0] - nbytes)

        TOK = CH * CW
        gx = later("gx", [P, DK, TOK])
        gn = later("gn", [P, DK, TOK])
        ghm = later("ghm", [P, CH, CW])
        gwm = later("gwm", [P, DK, P])
        gwp = later("gwp", [P, D])
        grow = later("grow", [P, FULL])
        gtmp = later("gtmp", [P, FULL])
        geq = later("geq", [P, FULL])
        gidx = later("gidx", [P, FULL])
        gidx_i = later("gidx_i", [P, FULL], I32)
        gfid = later("gfid", [P, FTF])
        gfid_i = later("gfid_i", [P, FTF], I32)
        gones = later("gones", [P, P])
        gr = later("gr", [HID, B, P])
        gmask = later("gmask", [P, 4, B, FTF])
        g_act, g_hist, g_new, g_comb = (gmask[:, a].rearrange("p b j -> p (b j)") for a in range(4))
        gdiff = later("gdiff", [P, B * FTF])
        gck = later("gck", [P, FTF])
        grank = later("grank", [P, 2, FTF])
        gs = later("gs", [P, 32])
        gout = later("gout", [P, 2, CT, D])

        x_in = [sem(f"x_in{c}") for c in range(CH)]
        gate_in, wq_in, wk_in, wv_in, wo_in, ctx_dma, par_in, nullk_in, wm_in, wc_in = map(
            sem, ("gate_in", "wq_in", "wk_in", "wv_in", "wo_in", "ctx_dma", "par_in", "nullk_in", "wm_in", "wc_in"))
        y_out = [sem(f"y_out{c}") for c in range(CH)]
        y_last = sem("y_last")
        consts = sem("consts")
        head_ready = sem("head_ready")
        zeroed = sem("zeroed")
        pool_chain, dve_chain, act_chain = sem("pool_chain"), sem("dve_chain"), sem("act_chain")
        tanh_done, g_done = sem("tanh_done"), sem("g_done")
        wq_hi, wq_lo = sem("wq_hi"), sem("wq_lo")
        z_ready, pe_xT, xn_full, xn_hi, xn_lo = map(sem, ("z_ready", "pe_xT", "xn_full", "xn_hi", "xn_lo"))
        pe_q, q_full, q_hi, q_lo, sq_hi, sq_lo, pe_ss = map(sem, ("pe_q", "q_full", "q_hi", "q_lo", "sq_hi", "sq_lo", "pe_ss"))
        ss_copied, pe_rT, sums_read, rq_guess, rq_ready = map(
            sem, ("ss_copied", "pe_rT", "sums_read", "rq_guess", "rq_ready"))
        pe_scores, scaled, exped, den_ready, normed = map(
            sem, ("pe_scores", "scaled", "exped", "den_ready", "normed"))
        pe_pT, p_hi, p_lo = sem("pe_pT"), sem("p_hi"), sem("p_lo")
        pe_vw, o_copied, u_ready, x1_ready = map(sem, ("pe_vw", "o_copied", "u_ready", "x1_ready"))
        var_ready, rs_guess, rs_ready = sem("var_ready"), sem("rs_guess"), sem("rs_ready")
        out_in = sem("out_in")
        gb_in, qk_ready, kss_ready, kr_guess = map(sem, ("gb_in", "qk_ready", "kss_ready", "kr_guess"))
        wm_hi, wm_lo, wp_hi, wp_lo = map(sem, ("wm_hi", "wm_lo", "wp_hi", "wp_lo"))
        zf_ready, pe_cT, xc_hi, xc_lo = map(sem, ("zf_ready", "pe_cT", "xc_hi", "xc_lo"))
        pe_h, h_hi, h_lo, pe_y, y_ready = map(sem, ("pe_h", "h_hi", "h_lo", "pe_y", "y_ready"))
        cz_ready, pe_czT, cT_ready, pe_k, k_copied, k_squared, khat_ready = map(
            sem, ("cz_ready", "pe_czT", "cT_ready", "pe_k", "k_copied", "k_squared", "khat_ready"))
        pe_kT, kb_hi, kb_lo, pe_v, vb_ready, vb_again, nullv_put, pe_vwp, vw_hi, vw_lo = map(
            sem, ("pe_kT", "kb_hi", "kb_lo", "pe_v", "vb_ready", "vb_again", "nullv_put", "pe_vwp", "vw_hi", "vw_lo"))

        search_pe, search_dve, ck_copied, flag_ready = map(
            sem, ("search_pe", "search_dve", "ck_copied", "flag_ready"))
        g_w, g_h, g_relu, g_y, g_add, g_small, g_pe, g_copy, g_iota, g_out, g_sum, g_z, g_turn = map(
            sem, ("g_w", "g_h", "g_relu", "g_y", "g_add", "g_small", "g_pe", "g_copy", "g_iota", "g_out", "g_sum",
                  "g_z", "g_turn"))
        G_PE = 1 + 2 * B + 1
        G_SMALL = 2 + B + 3
        held = sem("held")
        g_out2 = [sem(f"g_out{c}") for c in range(CH)]

        VG = [(0, 3), (3, 3), (6, 2)]
        VBK = (BS[0], BS[1], BV)
        VWJ = [(b, m) for b in range(B) for m in range(0, KT, 2)]
        VWN = len(VWJ) // B
        VW_BANK = [(BV, BS[2])[n % 2] if n < VWN else BQ for n in range(len(VWJ))]
        VW_STEP = {2 + n: VWN + n for n in range(VWN)}

        PG = [(k0, min(k0 + 4, KT)) for k0 in range(0, KT, 4)]

        def norms(t):
            n0 = 0 if t < TILES - CT else 1 if t < TILES + 2 else 2
            return n0, 3 if t >= 3 else 2 if t >= 2 else 1

        steps = range(TILES + 3)

        def hidden_bank(n):
            return BH[n % 2] if n < EARLY else BH[n % 4]

        VW_AT = {n: t for t, n in VW_STEP.items()}

        def kb_block(KB, b, g, s):
            at = (b * PAIRS + 4 * g) * PAIRW
            return KB[HD * s:HD * s + HD, at:at + 4 * PAIRW].rearrange(
                "p (i j) -> p i j", i=4)[:, :, KEYS * s:KEYS * s + KEYS]

        def kt_block(g, half):
            return ps[half, BT[g], 0:4 * KEYS].rearrange("p (i j) -> p i j", i=4)

        block = es.enter_context(nc.Block())

        def general_dve(dve):
            for c in range(CH):
                dve.wait_ge(y_out[c], 16)
            dve.wait_ge(y_last, 16)
            done, more, nov, nn = (gs[:, n:n + 1] for n in range(4))
            gp = gs[:, 8:8 + DK * B]
            dve.wait_ge(g_iota, 3)
            dve.tensor_copy(gidx[:, :], gidx_i[:, :])
            dve.tensor_copy(gfid[:, :], gfid_i[:, :])
            dve.memset(gones[:, :], 1.0)
            dve.memset(gmask[:, :, :, :], 0.0).then_inc(g_sum, 1)
            dve.memset(done, 0.0)
            dve.wait_ge(g_sum, 1)
            dve.memset(gmask[:, 0:2, :, 0:FT], 1.0).then_inc(g_sum, 1)
            for t in range(TILES):
                dve.tensor_scalar(zF[:, 0, :], resid[:, t, :], rs_f[:, t:t + 1], nb_f[:, t:t + 1],
                                  ALU.mult, ALU.add).then_inc(g_z, 1)
                dve.wait_ge(g_turn, t + 1)
                dve.tensor_copy(gx[:, :, P * t:P * t + P], ps[:, t % 2, 0:D].rearrange("p (k n) -> p k n", k=DK)).then_inc(g_z, 1)
            dve.wait_ge(g_z, 2 * TILES)
            dve.sem_inc(g_small, 1)
            dve.wait_ge(g_small, 1)
            dve.wait_ge(g_sum, 2)
            dve.sem_inc(g_y, CH)
            dve.sem_inc(g_relu, CH)
            dve.sem_inc(g_add, CH)
            K = 24 + 4 * B * FTF
            with dve.Fori(0, 3) as s:
                at = [2]

                def do(ins):
                    at[0] += 1
                    ins.then_inc(g_sum, 1)
                    dve.wait_ge(g_sum, s * K + at[0])

                do(dve.memset(gn[:, :, :], 0.0))
                dve.memset(gs[:, 30:31], 0.0)
                with dve.Fori(0, FTF) as j:
                    n0 = CH * (s * FTF + j)
                    for c in range(CH):
                        dve.wait_ge(g_y, n0 + CH + c + 1)
                        dve.wait_ge(g_add, n0 + c + 1)
                        dst = gn[:, :, CW * c:CW * c + CW]
                        src = ps[:, 4 + 2 * (c % 2):6 + 2 * (c % 2), :]
                        dve.tensor_tensor(dst, dst, src, ALU.add).then_inc(g_add, 1)
                dve.wait_ge(g_add, CH * (s * FTF + FTF) + CH)
                do(dve.tensor_reduce(gp, gn[:, :, :].rearrange("p k (b t) -> p (k b) t", b=B), AX.X, ALU.add))
                dve.tensor_scalar(gp, gp, 1.0 / N, None, ALU.mult).then_inc(g_small, 1)
                dve.wait_ge(g_pe, s * G_PE + 1)
                for b in range(B):
                    do(dve.tensor_scalar(gr[:, b, :], ps[0:HID, 7, b:b + 1].to_broadcast([HID, P]), 0.0, None,
                                         ALU.max))
                dve.sem_inc(g_small, 1)
                for b in range(B):
                    dve.wait_ge(g_pe, s * G_PE + 3 + 2 * b)
                    do(dve.tensor_copy(gck[:, :], ps[:, 6, 0:FTF]))
                    base = at[0]
                    dve.memset(gs[:, 30:31], 0.0)
                    with dve.Fori(0, FTF) as j:
                        def link(ins, i):
                            ins.then_inc(g_sum, 1)
                            dve.wait_ge(g_sum, s * K + j * 4 + (base + i))

                        mine = gck[:, bass.ds(j, 1)]
                        link(dve.tensor_scalar(gtmp[:, :], grow[:, :], mine, None, ALU.is_gt, ALU.add,
                                               accum_out=gs[:, 16:17]), 1)
                        link(dve.tensor_scalar(geq[:, :], grow[:, :], mine, None, ALU.is_equal), 2)
                        link(dve.scalar_tensor_tensor(gtmp[:, :], gidx[:, :], gfid[:, bass.ds(j, 1)], geq[:, :],
                                                      ALU.is_lt, ALU.mult, accum_out=gs[:, 17:18]), 3)
                        link(dve.tensor_tensor(grank[:, 0, bass.ds(j, 1)], gs[:, 16:17], gs[:, 17:18], ALU.add), 4)
                    at[0] += 4 * FTF
                    do(dve.tensor_scalar(gmask[:, 2, b, :], grank[:, 0, :], ITER - 0.5, None, ALU.is_lt))
                    dve.sem_inc(g_small, 1)
                do(dve.tensor_tensor(g_comb, g_hist, g_new, ALU.max))
                do(dve.tensor_tensor(gdiff[:, :], g_comb, g_hist, ALU.subtract))
                do(dve.tensor_reduce(nn, gdiff[:, :], AX.X, ALU.add))
                dve.sem_inc(g_small, 1)
                dve.wait_ge(g_pe, s * G_PE + G_PE)
                do(dve.tensor_scalar(more, done, -1.0, 1.0, ALU.mult, ALU.add))
                do(dve.tensor_scalar(gn[:, :, :], gn[:, :, :], more, None, ALU.mult))
                do(dve.scalar_tensor_tensor(gx[:, :, :], gx[:, :, :], done, gn[:, :, :], ALU.mult, ALU.add))
                for old, new in ((g_act, g_new), (g_hist, g_comb)):
                    do(dve.tensor_scalar(new, new, more, None, ALU.mult))
                    do(dve.scalar_tensor_tensor(old, old, done, new, ALU.mult, ALU.add))
                do(dve.tensor_scalar(nov, ps[:, 7, 0:1], NEW_MAX, None, ALU.is_lt))
                do(dve.tensor_tensor(done, done, nov, ALU.max))
                while at[0] < 2 + K:
                    do(dve.memset(gs[:, 31:32], 0.0))
                dve.sem_inc(g_small, 2)
            for t in range(TILES):
                dve.wait_ge(g_pe, 3 * G_PE + t + 1)
                if t >= 2 * CT:
                    dve.wait_ge(g_out2[t // CT - 2], 16)
                dve.scalar_tensor_tensor(gout[:, t // CT % 2, t % CT, :], ps[:, t % 2, 0:D], tg[:, 1:2],
                                         resid[:, t, :], ALU.mult, ALU.add).then_inc(g_out, 1)

        @block.sync
        def _(sp):
            sp.dma_start(resid[:, 0:CT, :], xt[0]).then_inc(x_in[0], 16)
            sp.dma_start(cx[:, :, :], ctx_in.rearrange("b j d -> j b d")).then_inc(ctx_dma, 16)
            sp.dma_start(wq_raw[:, :, :], Wq.rearrange("(k p) n -> p k n", p=P)).then_inc(wq_in, 16)
            wkv_v = Wkv.rearrange("(k p) n -> p k n", p=P)
            sp.dma_start(Wkv_s[:, :, 0:INNER], wkv_v[:, :, 0:INNER]).then_inc(wk_in, 16)
            sp.dma_start(Wkv_s[:, :, INNER:], wkv_v[:, :, INNER:]).then_inc(wv_in, 16)
            with nc.allow_non_contiguous_dma(reason="columns of parameters"):
                for s in range(2):
                    half = slice(HD * s, HD * s + HD)
                    sp.dma_start(sc2[half, 0:1], q_scale.rearrange("(p o) -> p o", o=1)).then_inc(par_in, 16)
                    sp.dma_start(sc2[half, 1:2], k_scale.rearrange("(p o) -> p o", o=1)).then_inc(par_in, 16)
                    sp.dma_start(nv[half, :], null_kv[1, :].rearrange("(p o) -> p o", o=1)).then_inc(par_in, 16)
                sp.dma_start(G[:, :], ln_out_g.partition_broadcast(P)).then_inc(out_in, 16)
                sp.dma_start(TB[:, :], ln_out_b.partition_broadcast(P)).then_inc(out_in, 16)
            sp.dma_start(Wo_s[:, :, :], Wo.rearrange("(i p) n -> p i n", p=P)).then_inc(wo_in, 16)
            for c in range(1, CH):
                sp.dma_start(resid[:, CT * c:CT * c + CT, :], xt[c]).then_inc(x_in[c], 16)
            sp.wait_ge(pe_kT, B * PAIRS)
            sp.dma_start(wp_raw[:, :, :], wp_v[:, 0:FT, :]).then_inc(wm_in, 16)
            sp.wait_ge(pe_vwp, len(VWJ))
            sp.dma_start(wm_raw[:, :, :], wm_v[:, :, 0:ITER]).then_inc(wm_in, 16)
            sp.wait_ge(pe_xT, QC)
            with nc.allow_non_contiguous_dma(reason="rows of 256 bytes"):
                sp.dma_start(w_c1[:, :, :], Wc1T.rearrange("(k p) h -> p k h", p=P)).then_inc(wc_in, 16)
            sp.wait_ge(x1_ready, TILES)
            sp.wait_ge(pe_q, QC * QG)
            sp.dma_start(w_c2[:, :], Wc2T).then_inc(wc_in, 16)
            for c in range(CH - 1):
                sp.wait_ge(y_ready, CT * c + CT)
                sp.dma_start(ot[c], yo[:, c % 2, :, :]).then_inc(y_out[c], 16)
            c = CH - 1
            for k0, k1, done in ((0, CT - 1, y_out[c]), (CT - 1, CT, y_last)):
                sp.wait_ge(y_ready, CT * c + k1)
                sp.dma_start(ot[c][:, k0:k1, :], yo[:, c % 2, k0:k1, :]).then_inc(done, 16)
            sp.wait_ge(y_last, 16)
            for c in range(CH):
                sp.wait_ge(y_out[c], 16)
            sp.wait_ge(flag_ready, 1)
            go = sp.value_load(flag[0:1, 0:1])
            with sp.If(go > 0):
                with sp.Fori(0, 3) as s:
                    with sp.Fori(0, FTF) as j:
                        sp.wait_ge(g_y, CH * (s * FTF + j) + CH)
                        sp.dma_start(gwm[:, :, :], wm_v[:, :, bass.ds(j * P, P)]).then_inc(g_w, 16)
                        sp.dma_start(gwp[:, :], WpT[bass.ds(j * P, P), :]).then_inc(g_w, 16)
                for c in range(CH):
                    sp.wait_ge(g_out, CT * c + CT)
                    sp.dma_start(ot[c], gout[:, c % 2, :, :]).then_inc(g_out2[c], 16)
                for c in range(CH):
                    sp.wait_ge(g_out2[c], 16)
            with sp.Else():
                sp.nop()

        @block.gpsimd
        def _(pool):
            do = Chain(pool, pool_chain).do
            do(pool.memset(ident[:, :], 0.0))
            pool.affine_select(out=ident[:, :], in_=ident[:, :], compare_op=ALU.not_equal, fill=1.0,
                               base=0, pattern=[[-1, P]], channel_multiplier=1).then_inc(consts, 1)
            do(pool.memset(head_f[:, :, :], 0.0))
            for s in range(2):
                for i in range(PAIRS):
                    do(pool.memset(head_f[HD * s:HD * s + HD, i, 2 * i + s:2 * i + s + 1], 1.0))
            pool.tensor_copy(head_of[:, :, :], head_f[:, :, :]).then_inc(head_ready, 1)
            with nc.allow_non_contiguous_dma(reason="the null key for every head"):
                for b in range(B):
                    pool.dma_start(kn[J:KEYS, b, :].rearrange("o (h d) -> o h d", h=HEADS),
                                   null_kv[0:1, :].unsqueeze(1).to_broadcast([1, HEADS, HD])).then_inc(nullk_in, 16)
            pool.memset(VB[:, :, :], 0.0).then_inc(zeroed, 1)

            def xn_low(c):
                if c >= QC:
                    return
                pool.wait_ge(xn_full, DK * c + DK)
                pool.wait_ge(xn_hi, c + 1)
                if c:
                    pool.wait_ge(pe_q, QG * c)
                pool.tensor_tensor(xnl[:, :, :], xf[:, :, :], xnh[:, :, :].bitcast(F32),
                                   ALU.subtract).then_inc(xn_lo, 1)

            def squares_low(n):
                if n >= QC * QG:
                    return
                pool.wait_ge(sq_hi, n + 1)
                if n:
                    pool.wait_ge(pe_ss, n)
                pool.tensor_tensor(sql[:, :], sq[:, :], sqh[:, n % 2, :].bitcast(F32), ALU.subtract).then_inc(sq_lo, 1)

            def normalise(t):
                if t >= TILES:
                    return
                pool.wait_ge(den_ready, t + 1)
                pool.tensor_tensor(
                    E[:, t % 2, 0:PACK].rearrange("p (h j) -> p h j", h=HEADS),
                    E[:, t % 2, 0:PACK].rearrange("p (h j) -> p h j", h=HEADS),
                    rden[:, t % 2, :].unsqueeze(2).to_broadcast([P, HEADS, KEYS]),
                    ALU.mult).then_inc(normed, 1)

            def last_values(t):
                if t != 1:
                    return
                pool.wait_ge(pe_vwp, VWN)
                pool.wait_ge(sq_lo, 2 * QG)
                for s in range(2):
                    half = slice(HD * s, HD * s + HD)
                    at = P + KEYS * s
                    pool.tensor_copy(VB[half, :, at:at + J], VC[half, :, :]).then_inc(vb_again, 1)
                    pool.wait_ge(vb_again, s + 1)

            def add_attention(s):
                if not 0 <= s < TILES:
                    return
                pool.wait_ge(u_ready, s + 1)
                do(pool.tensor_tensor(u[:, s % 2, :], u[:, s % 2, :], G[:, :], ALU.mult))
                do(pool.tensor_tensor(u[:, s % 2, :], u[:, s % 2, :], TB[:, :], ALU.add))
                pool.tensor_tensor(resid[:, s, :], resid[:, s, :], u[:, s % 2, :],
                                   ALU.add).then_inc(x1_ready, 1)

            xn_low(0)
            pool.memset(KBh[:, :].bitcast(F32), 0.0).then_inc(zeroed, 1)
            squares_low(0)
            pool.memset(KBl[:, :].bitcast(F32), 0.0).then_inc(zeroed, 1)
            squares_low(1)
            pool.memset(E[:, :, PACK:], 0.0).then_inc(zeroed, 1)
            squares_low(2)
            squares_low(3)
            do(pool.memset(ones_b[:, :], 0.0))
            for s in range(2):
                do(pool.memset(ones_b[HD * s:HD * s + HD, HD * s:HD * s + HD], 1.0))
            pool.iota(part_i[:, :], pattern=[[0, 1]], base=0, channel_multiplier=1).then_inc(g_iota, 1)
            pool.wait_ge(tanh_done, 1)
            pool.wait_ge(out_in, 16 * 2)
            gx = tg[:, 0:1]
            pool.tensor_scalar(G[:, :], G[:, :], gx, None, ALU.mult).then_inc(g_done, 1)
            pool.tensor_scalar(TB[:, :], TB[:, :], gx, None, ALU.mult).then_inc(g_done, 1)
            pool.wait_ge(g_done, 2)

            for t in range(TILES - QT):
                c = t // QT + 1
                nxt = QG * c + t % QT * 2
                if t % QT == 0:
                    xn_low(c)
                    squares_low(nxt)
                    squares_low(nxt + 1)
                    normalise(t)
                    add_attention(t - 2)
                else:
                    squares_low(nxt)
                    squares_low(nxt + 1)
                    normalise(t)
                    last_values(t)
                    add_attention(t - 2)
            t = TILES - 2
            normalise(t)
            add_attention(t - 2)
            t += 1
            normalise(t)
            add_attention(t - 2)
            t += 1
            add_attention(t - 2)
            for h in range(2):
                pool.wait_ge(wp_hi, h + 1)
                pool.tensor_tensor(Wpl[:, 4 * h:4 * h + 4, :], wp_raw[:, 4 * h:4 * h + 4, :],
                                   Wph[:, 4 * h:4 * h + 4, :].bitcast(F32), ALU.subtract).then_inc(wp_lo, 1)
            for t in (TILES + 1, TILES + 2):
                add_attention(t - 2)

            pool.wait_ge(flag_ready, 1)
            go = pool.value_load(flag[0:1, 0:1])
            with pool.If(go > 0):
                pool.iota(gidx_i[:, :], pattern=[[1, FULL]], base=0, channel_multiplier=0).then_inc(g_iota, 1)
                pool.iota(gfid_i[:, :], pattern=[[P, FTF]], base=0, channel_multiplier=1).then_inc(g_iota, 1)
                pool.wait_ge(g_iota, 3)
            with pool.Else():
                pool.nop()

        @block.scalar
        def _(act):
            with nc.allow_non_contiguous_dma(reason="columns of parameters"):
                for a, src in enumerate((ln_in_g, ln_in_b)):
                    act.dma_start(in_gb[:, a, :], src.rearrange("(k p) -> p k", p=P)).then_inc(gb_in, 16)
                for a, src in enumerate((ln_ctx_g, ln_ctx_b)):
                    act.dma_start(cx_gb[:, a, :], src.rearrange("(k p) -> p k", p=P)).then_inc(gb_in, 16)
                act.dma_start(gates[:, 0:1], g_xattn.partition_broadcast(P)).then_inc(gate_in, 16)
                act.dma_start(gates[:, 1:2], g_ffn.partition_broadcast(P)).then_inc(gate_in, 16)
            act.wait_ge(gate_in, 16 * 2)
            act.activation(tg, gates, ACT.Tanh).then_inc(tanh_done, 1)
            act.preload_act_table_set("natural_log_exp_and_others")
            act.wait_ge(wq_in, 16)
            for k in range(DK):
                act.activation(Wqh[:, k, :], wq_raw[:, k, :], ACT.Copy).then_inc(wq_hi, 1)

            def keys(b):
                for n in range(2):
                    act.wait_ge(pe_k, 2 * b + n + 1)
                    act.activation(kn[0:J, b, 512 * n:512 * n + 512], ps[0:J, BT[n], :],
                                   ACT.Copy).then_inc(k_copied, 1)

            def squared_keys(b):
                act.wait_ge(k_copied, 2 * b + 2)
                act.wait_ge(nullk_in, 16 * B)
                act.activation(ksq[:, b, :], kn[:, b, :], ACT.Square).then_inc(k_squared, 1)

            def key_norms():
                act.wait_ge(kss_ready, 1)
                chain[0] += 1
                act.activation(krt, kss, ACT.Ln).then_inc(act_chain, 1)
                act.wait_ge(act_chain, chain[0])
                act.activation(krk, krt, ACT.Exp, scale=-0.5).then_inc(kr_guess, 1)

            def values(g):
                i0, n = VG[g]
                act.wait_ge(zeroed, 1)
                act.wait_ge(pe_v, g + 1)
                src = ps[:, VBK[g], 0:n * B * J].rearrange("p (i b j) -> p i b j", i=n, b=B)
                for s in range(2):
                    half = slice(HD * s, HD * s + HD)
                    at = P + KEYS * s
                    act.activation(VB[half, i0:i0 + n, at:at + J], src[half, :, 0, :], ACT.Copy).then_inc(vb_ready, 1)
                act.activation(VC[:, i0:i0 + n, :], src[:, :, 1, :], ACT.Copy).then_inc(vb_ready, 1)

            def key_blocks_high(b):
                act.wait_ge(zeroed, 3)
                act.wait_ge(qk_ready, 1)
                for g in range(2):
                    act.wait_ge(pe_kT, PAIRS * b + 4 * g + 4)
                    for s in range(2):
                        half = slice(HD * s, HD * s + HD)
                        act.activation(kb_block(KBh, b, g, s), kt_block(g, half), ACT.Copy,
                                       scale=qk[half, :]).then_inc(kb_hi, 1)

            def values_out(n):
                if n is None:
                    return
                b, m = VWJ[n]
                act.wait_ge(pe_vwp, n + 1)
                act.activation(VWh[:, b, m:m + 2, :], ps[:, VW_BANK[n], :].rearrange("p (r c) -> p r c", r=2),
                               ACT.Copy).then_inc(vw_hi, 1)

            def xn_high(c):
                if c >= QC:
                    return
                act.wait_ge(xn_full, DK * c + DK)
                if c:
                    act.wait_ge(pe_q, QG * c)
                act.activation(xnh[:, :, :], xf[:, :, :], ACT.Copy).then_inc(xn_hi, 1)

            def queries(n):
                if n >= QC * QG:
                    return
                c, g = n // QG, n % QG
                act.wait_ge(pe_q, n + 1)
                if n:
                    act.wait_ge(q_lo, n)
                    act.wait_ge(sq_hi, n)
                act.activation(qf[:, :], ps[:, BQ, :], ACT.Copy).then_inc(q_full, 1)
                act.wait_ge(q_full, n + 1)
                if c >= 2:
                    act.wait_ge(pe_scores, 4 * QT * (c - 1))
                act.activation(qh[c % 2][:, 2 * g:2 * g + 2, :],
                               qf[:, :].rearrange("p (i t) -> p i t", i=2), ACT.Copy).then_inc(q_hi, 1)

            def squares(n):
                if n >= QC * QG:
                    return
                if n:
                    act.wait_ge(sq_lo, n)
                if n >= 2:
                    act.wait_ge(pe_ss, n - 1)
                act.activation(sq[:, :], qf[:, :], ACT.Square)
                act.activation(sqh[:, n % 2, :], qf[:, :], ACT.Square).then_inc(sq_hi, 1)

            def query_norms(c):
                if c >= QC:
                    return
                act.wait_ge(sums_read, c + 1)
                act.activation(rqt, rqv, ACT.Ln).then_inc(act_chain, 1)
                chain[0] += 1
                act.wait_ge(act_chain, chain[0])
                act.activation(rq, rqt, ACT.Exp, scale=-0.5).then_inc(rq_guess, 1)

            def row_norms(t):
                (n0, n1), par = norms(t), t % 2
                act.wait_ge(var_ready, t + 1)
                act.activation(rt_n[:, par, n0:n1], var_n[:, par, n0:n1], ACT.Ln).then_inc(act_chain, 1)
                chain[0] += 1
                act.wait_ge(act_chain, chain[0])
                act.activation(rs_n[:, t, n0:n1], rt_n[:, par, n0:n1], ACT.Exp, scale=-0.5).then_inc(rs_guess, 1)

            def exps(t):
                if t >= TILES:
                    return
                act.wait_ge(scaled, 4 * t + 4)
                act.activation(E[:, t % 2, 0:PACK], E[:, t % 2, 0:PACK], ACT.Exp).then_inc(exped, 1)

            def attention_out(s):
                if not 0 <= s < TILES:
                    return
                act.wait_ge(pe_vw, s + 1)
                act.activation(ob[:, s % 2, :], ps[:, BV, 0:D], ACT.Copy).then_inc(o_copied, 1)

            def norm_out(s):
                if not 0 <= s < TILES:
                    return
                par = s % 2
                t = s + 2
                act.wait_ge(rs_ready, t + 1)
                if s >= 2:
                    act.wait_ge(x1_ready, s - 1)
                act.activation(u[:, par, :], ob[:, par, :], ACT.Identity, scale=rs_n[:, t, 1:2],
                               bias=nb_n[:, t, 1:2]).then_inc(u_ready, 1)

            def norm_x(s):
                if s >= TILES:
                    return
                t = s - CT
                act.wait_ge(rs_ready, t + 1)
                act.wait_ge(pe_xT, t // QT + 1)
                act.activation(z[:, s % CT, :], resid[:, s, :], ACT.Identity, scale=rs_n[:, t, 0:1],
                               bias=nb_n[:, t, 0:1]).then_inc(z_ready, 1)

            def probs_high(s, g):
                if not 0 <= s < TILES:
                    return
                k0, k1 = PG[g]
                n = len(PG) * s + g
                act.wait_ge(pe_pT, n + 1)
                act.activation(ph[:, k0:k1, :],
                               ps[:, BT[n % 2], 0:P * (k1 - k0)].rearrange("p (m t) -> p m t", t=P),
                               ACT.Copy).then_inc(p_hi, 1)

            def ffn_in(f):
                act.wait_ge(rs_ready, CT * f + CT + 3)
                act.wait_ge(pe_ss, QC * QG)
                if f:
                    act.wait_ge(pe_cT, DK * f)
                for k in range(CT):
                    s = CT * f + k
                    act.activation(zF[:, k, :], resid[:, s, :], ACT.Identity, scale=rs_f[:, s:s + 1],
                                   bias=nb_f[:, s:s + 1]).then_inc(zf_ready, 1)

            def xc_high(f):
                for h in range(DK):
                    act.wait_ge(pe_cT, DK * f + h + 1)
                    act.activation(xch[:, f % 2, h, :], ps[:, BCF[f][h], :], ACT.Copy).then_inc(xc_hi, 1)

            def hidden_high(n):
                f, j = n // FT, n % FT
                act.wait_ge(pe_h, n + 1)
                act.activation(hh[f % 2][:, j, :], ps[:, hidden_bank(n), :], ACT.Relu,
                               accum_out=hs[:, j, f:f + 1]).then_inc(h_hi, 1)

            def wm_high(h):
                act.wait_ge(wm_in, 32)
                act.activation(Wmh[:, h, :], wm_raw[:, h, :], ACT.Copy).then_inc(wm_hi, 1)

            def wp_high(h):
                act.wait_ge(pe_scores, 4 * (TILES - QT))
                act.activation(Wph[:, 4 * h:4 * h + 4, :], wp_raw[:, 4 * h:4 * h + 4, :], ACT.Copy).then_inc(wp_hi, 1)

            chain = [0]
            xn_high(0)
            queries(0)
            squares(0)
            keys(0)
            queries(1)
            squares(1)
            squared_keys(0)
            keys(1)
            squared_keys(1)
            queries(2)
            squares(2)
            key_norms()
            values(0)
            values(1)
            queries(3)
            squares(3)
            values(2)
            key_blocks_high(0)
            for n in range(VWN - 1):
                values_out(n)
            key_blocks_high(1)
            values_out(VWN - 1)
            for t in range(TILES - QT):
                c = t // QT + 1
                nxt = QG * c + t % QT * 2
                if t % QT == 0:
                    query_norms(c - 1)
                    attention_out(t - 2)
                    probs_high(t - 1, 0)
                    xn_high(c)
                    probs_high(t - 1, 1)
                    queries(nxt)
                    probs_high(t - 1, 2)
                    squares(nxt)
                    exps(t)
                    queries(nxt + 1)
                    squares(nxt + 1)
                    row_norms(t)
                    norm_out(t - 2)
                    values_out(VW_STEP.get(t))
                    norm_x(t + CT)
                else:
                    attention_out(t - 2)
                    probs_high(t - 1, 0)
                    queries(nxt)
                    squares(nxt)
                    probs_high(t - 1, 1)
                    queries(nxt + 1)
                    probs_high(t - 1, 2)
                    exps(t)
                    squares(nxt + 1)
                    row_norms(t)
                    norm_out(t - 2)
                    norm_x(t + CT)
                    values_out(VW_STEP.get(t))
            t = TILES - 2
            query_norms(QC - 1)
            attention_out(t - 2)
            probs_high(t - 1, 0)
            probs_high(t - 1, 1)
            wm_high(0)
            probs_high(t - 1, 2)
            exps(t)
            wm_high(1)
            ffn_in(0)
            row_norms(t)
            norm_out(t - 2)
            t += 1
            attention_out(t - 2)
            probs_high(t - 1, 0)
            probs_high(t - 1, 1)
            xc_high(0)
            probs_high(t - 1, 2)
            exps(t)
            hidden_high(0)
            row_norms(t)
            norm_out(t - 2)
            hidden_high(1)
            t += 1
            attention_out(t - 2)
            probs_high(t - 1, 0)
            probs_high(t - 1, 1)
            hidden_high(2)
            probs_high(t - 1, 2)
            hidden_high(3)
            wp_high(0)
            row_norms(t)
            norm_out(t - 2)
            hidden_high(4)
            wp_high(1)
            ffn_in(1)

            for f in range(CH):
                if f == 1:
                    xc_high(1)
                    ffn_in(2)
                elif f == 2:
                    ffn_in(3)
                for j in range(EARLY if f == 0 else 0, FT):
                    hidden_high(FT * f + j)
                    if j == 1 and f in (1, 2):
                        xc_high(f + 1)
                    if f == 0 and j in (FT - 3, FT - 1):
                        t = TILES + 1 + j // (FT - 1)
                        attention_out(t - 2)
                        row_norms(t)
                        norm_out(t - 2)
            act.wait_ge(h_lo, FT * CH)
            for n, bank in enumerate((0, 5, 3)):
                act.wait_ge(search_pe, 4 + n)
                act.activation(ck[:, ITER * n:ITER * n + ITER], ps[:, bank:bank + 2, :].rearrange("p b n -> p (b n)"),
                               ACT.Copy).then_inc(ck_copied, 1)

            act.wait_ge(flag_ready, 1)
            go = act.value_load(flag[0:1, 0:1])
            with act.If(go > 0):
                with act.Fori(0, 3) as s:
                    with act.Fori(0, FTF) as j:
                        for c in range(CH):
                            act.wait_ge(g_h, CH * (s * FTF + j) + c + 1)
                            act.wait_ge(g_y, CH * (s * FTF + j) + CH)
                            act.sem_inc(held, 1)
                            act.activation(ghm[:, c, :], ps[:, c, :], ACT.Relu,
                                           scale=gmask[:, 0, c // CPB, bass.ds(j, 1)]).then_inc(g_relu, 1)
                    for b in range(B):
                        act.wait_ge(g_pe, s * G_PE + 2 + 2 * b)
                        act.activation(grow[:, :], ps[:, 0:6, :].rearrange("p b n -> p (b n)"),
                                       ACT.Copy).then_inc(g_copy, 1)
            with act.Else():
                act.nop()

        @block.vector
        def _(dve):
            chain = Chain(dve, dve_chain)
            do, put = chain.do, chain.put

            def first_norm(c):
                dve.wait_ge(x_in[c], 16)
                for k in range(CT):
                    (put if k < CT - 1 else do)(dve.bn_stats(st_z[:, k, :], resid[:, CT * c + k, :]))
                for k in range(CT):
                    (put if k < CT - 1 else do)(dve.bn_aggr(mv_z[:, k, :], st_z[:, k, :]))
                do(dve.tensor_scalar(nw_z[:, 0, :], mv_z[:, :, 1], 1.0 + LN_EPS, LN_EPS * LN_EPS, ALU.mult, ALU.add))
                rsqrt(dve, do, nw_z[:, 1, :], nw_z[:, 0, :], nw_z[:, 2, :])
                for k in range(CT):
                    dve.tensor_scalar(z[:, k, :], resid[:, CT * c + k, :], mv_z[:, k, 0:1], nw_z[:, 1, k:k + 1],
                                      ALU.subtract, ALU.mult).then_inc(z_ready, 1)

            def xn_whole(c):
                if c >= QC:
                    return
                dve.wait_ge(pe_xT, c + 1)
                if c == 0:
                    dve.wait_ge(gb_in, 16 * 4)
                if c:
                    dve.wait_ge(xn_hi, c)
                    dve.wait_ge(xn_lo, c)
                for k in range(DK):
                    dve.tensor_scalar(xf[:, k, :], ps[:, BX, QW * k:QW * k + QW], in_gb[:, 0, k:k + 1],
                                      in_gb[:, 1, k:k + 1], ALU.mult, ALU.add).then_inc(xn_full, 1)

            def queries_low(n):
                if n >= QC * QG:
                    return
                c, g = n // QG, n % QG
                dve.wait_ge(q_hi, n + 1)
                dve.tensor_tensor(ql[c % 2][:, 2 * g:2 * g + 2, :], qf[:, :].rearrange("p (i t) -> p i t", i=2),
                                  qh[c % 2][:, 2 * g:2 * g + 2, :].bitcast(F32), ALU.subtract).then_inc(q_lo, 1)

            def copy_sums(c):
                if c >= QC:
                    return
                dve.wait_ge(pe_ss, QG * c + QG)
                dve.tensor_copy(ssT[:, :], ps[0:HEADS, BX, 0:QW]).then_inc(ss_copied, 1)

            def read_sums(c):
                if c >= QC:
                    return
                dve.wait_ge(pe_rT, c + 1)
                dve.tensor_scalar(rqv, ps[:, BX, 0:QT * HEADS], NORM_EPS * NORM_EPS, None,
                                  ALU.max).then_inc(sums_read, 1)

            def query_norms(c):
                if c >= QC:
                    return
                dve.wait_ge(rq_guess, c + 1)
                do(dve.tensor_tensor(rqt, rq, rq, ALU.mult))
                do(dve.scalar_tensor_tensor(rqt, rqt, -0.5, rqv, ALU.mult, ALU.mult))
                dve.scalar_tensor_tensor(rq, rqt, 1.5, rq, ALU.add, ALU.mult).then_inc(rq_ready, 1)

            def scale_scores(t, g):
                if t >= TILES:
                    return
                n = 4 * t + g
                if t % QT == 0 and g == 0:
                    dve.wait_ge(rq_ready, t // QT + 1)
                dve.wait_ge(pe_scores, n + 1)
                r = rq[:, HEADS * (t % QT) + 4 * g:HEADS * (t % QT) + 4 * g + 4]
                dve.tensor_tensor(
                    E[:, t % 2, 4 * KEYS * g:4 * KEYS * g + 4 * KEYS].rearrange("p (h j) -> p h j", h=4),
                    ps[:, BS[n % 3], 0:4 * KEYS].rearrange("p (h j) -> p h j", h=4),
                    r.unsqueeze(2).to_broadcast([P, 4, KEYS]), ALU.mult).then_inc(scaled, 1)

            def sum_exps(t):
                if t >= TILES:
                    return
                dve.wait_ge(exped, t + 1)
                do(dve.tensor_reduce(den[:, t % 2, :], E[:, t % 2, 0:PACK].rearrange("p (h j) -> p h j", h=HEADS),
                                     AX.X, ALU.add))
                dve.reciprocal(rden[:, t % 2, :], den[:, t % 2, :]).then_inc(den_ready, 1)

            def stats(t, n):
                if not norms(t)[0] <= n < norms(t)[1]:
                    return
                if n == 0:
                    if t % CT == 0:
                        dve.wait_ge(x_in[t // CT + 1], 16)
                    v = resid[:, t + CT, :]
                elif n == 1:
                    dve.wait_ge(o_copied, t - 1)
                    v = ob[:, t % 2, :]
                else:
                    dve.wait_ge(x1_ready, t - 2)
                    v = resid[:, t - 3, :]
                do(dve.bn_stats(st_n[:, n, :], v))
                do(dve.bn_aggr(mv_n[:, t % 2, n, :], st_n[:, n, :]))

            def variances(t):
                n0, n1 = norms(t)
                par = t % 2
                if n0 == 0:
                    ins = dve.tensor_scalar(var_n[:, par, 0:1], mv_n[:, par, 0, 1:2], 1.0 + LN_EPS, LN_EPS * LN_EPS,
                                            ALU.mult, ALU.add)
                    if n1 == 1:
                        ins.then_inc(var_ready, 1)
                m0 = max(n0, 1)
                if n1 > m0:
                    dve.tensor_scalar(var_n[:, par, m0:n1], mv_n[:, par, m0:n1, 1], LN_EPS, None,
                                      ALU.add).then_inc(var_ready, 1)

            def inverse_roots(t):
                n0, n1 = norms(t)
                par = t % 2
                y, v, tt = rs_n[:, t, n0:n1], var_n[:, par, n0:n1], rt_n[:, par, n0:n1]
                dve.wait_ge(rs_guess, t + 1)
                do(dve.tensor_tensor(tt, y, y, ALU.mult))
                do(dve.scalar_tensor_tensor(tt, tt, -0.5, v, ALU.mult, ALU.mult))
                do(dve.scalar_tensor_tensor(y, tt, 1.5, y, ALU.add, ALU.mult))
                dve.scalar_tensor_tensor(nb_n[:, t, n0:n1], mv_n[:, par, n0:n1, 0], -1.0, y,
                                         ALU.mult, ALU.mult).then_inc(rs_ready, 1)

            def probs_low(s, g):
                if not 0 <= s < TILES:
                    return
                k0, k1 = PG[g]
                n = len(PG) * s + g
                dve.wait_ge(p_hi, n + 1)
                dve.tensor_tensor(pl[:, k0:k1, :],
                                  ps[:, BT[n % 2], 0:P * (k1 - k0)].rearrange("p (m t) -> p m t", t=P),
                                  ph[:, k0:k1, :].bitcast(F32), ALU.subtract).then_inc(p_lo, 1)

            def xc_low(f):
                for h in range(DK):
                    dve.wait_ge(xc_hi, DK * f + h + 1)
                    dve.tensor_tensor(xcl[:, f % 2, h, :], ps[:, BCF[f][h], :],
                                      xch[:, f % 2, h, :].bitcast(F32), ALU.subtract).then_inc(xc_lo, 1)

            def context():
                dve.wait_ge(ctx_dma, 16)
                for b in range(B):
                    (put if b < B - 1 else do)(dve.bn_stats(st_a[0:J, b, :], cx[:, b, :]))
                for b in range(B):
                    (put if b < B - 1 else do)(dve.bn_aggr(mv_a[0:J, b, :], st_a[0:J, b, :]))
                do(dve.tensor_scalar(nw_a[0:J, 0, :], mv_a[0:J, :, 1], LN_EPS, None, ALU.add))
                rsqrt(dve, do, nw_a[0:J, 1, :], nw_a[0:J, 0, :], nw_a[0:J, 2, :])
                for b in range(B):
                    dve.tensor_scalar(cz[:, b, :], cx[:, b, :], mv_a[0:J, b, 0:1], nw_a[0:J, 1, b:b + 1],
                                      ALU.subtract, ALU.mult).then_inc(cz_ready, 1)

            def key_factors():
                dve.wait_ge(par_in, 16 * 6)
                dve.tensor_scalar(qk, sc2[:, 0:1], sc2[:, 1:2], SCALE, ALU.mult, ALU.mult).then_inc(qk_ready, 1)

            def context_turned():
                dve.wait_ge(pe_czT, 1)
                for k in range(DK):
                    dve.tensor_scalar(cT[:, k, :], ps[:, BT[0], B * J * k:B * J * k + B * J],
                                      cx_gb[:, 0, k:k + 1], cx_gb[:, 1, k:k + 1],
                                      ALU.mult, ALU.add).then_inc(cT_ready, 1)

            def null_values():
                dve.wait_ge(zeroed, 1)
                for s in range(2):
                    half = slice(HD * s, HD * s + HD)
                    at = P + KEYS * s + J
                    dve.tensor_copy(VB[half, :, at:at + 1],
                                    nv[half, :].unsqueeze(1).to_broadcast([HD, PAIRS, 1])).then_inc(nullv_put, 1)

            def key_norms():
                for b in range(B):
                    dve.wait_ge(k_squared, b + 1)
                    (put if b < B - 1 else do)(dve.tensor_reduce(
                        krt[:, HEADS * b:HEADS * b + HEADS], ksq[:, b, :].rearrange("p (h d) -> p h d", d=HD),
                        AX.X, ALU.add))
                dve.tensor_scalar(kss, krt, NORM_EPS * NORM_EPS, None, ALU.max).then_inc(kss_ready, 1)

            def scale_keys():
                dve.wait_ge(kr_guess, 1)
                do(dve.tensor_tensor(krt, krk, krk, ALU.mult))
                do(dve.scalar_tensor_tensor(krt, krt, -0.5, kss, ALU.mult, ALU.mult))
                do(dve.scalar_tensor_tensor(krk, krt, 1.5, krk, ALU.add, ALU.mult))
                for b in range(B):
                    kv = kn[:, b, :].rearrange("p (h d) -> p h d", d=HD)
                    dve.tensor_tensor(kv, kv, krk[:, HEADS * b:HEADS * b + HEADS].unsqueeze(2).to_broadcast(
                        [KEYS, HEADS, HD]), ALU.mult).then_inc(khat_ready, 1)

            def key_blocks_low(b):
                for g in range(2):
                    dve.wait_ge(kb_hi, 4 * b + 2 * g + 2)
                    for s in range(2):
                        half = slice(HD * s, HD * s + HD)
                        dve.scalar_tensor_tensor(kb_block(KBl, b, g, s), kt_block(g, half), qk[half, :],
                                                 kb_block(KBh, b, g, s).bitcast(F32),
                                                 ALU.mult, ALU.subtract).then_inc(kb_lo, 1)

            def values_low(n):
                if n is None:
                    return
                b, m = VWJ[n]
                dve.wait_ge(vw_hi, n + 1)
                dve.tensor_tensor(VWl[:, b, m:m + 2, :], ps[:, VW_BANK[n], :].rearrange("p (r c) -> p r c", r=2),
                                  VWh[:, b, m:m + 2, :].bitcast(F32), ALU.subtract).then_inc(vw_lo, 1)

            def hidden_low(n):
                f, j = n // FT, n % FT
                dve.wait_ge(h_hi, n + 1)
                dve.scalar_tensor_tensor(hl[f % 2][:, j, :], ps[:, hidden_bank(n), :], 0.0,
                                         hh[f % 2][:, j, :].bitcast(F32), ALU.max, ALU.subtract).then_inc(h_lo, 1)

            def wm_low(h):
                dve.wait_ge(wm_hi, h + 1)
                dve.tensor_tensor(Wml[:, h, :], wm_raw[:, h, :], Wmh[:, h, :].bitcast(F32),
                                  ALU.subtract).then_inc(wm_lo, 1)

            first_norm(0)
            context()
            xn_whole(0)
            for h in range(DK):
                dve.wait_ge(wq_hi, h + 1)
                dve.tensor_tensor(Wql[:, h, :], wq_raw[:, h, :], Wqh[:, h, :].bitcast(F32),
                                  ALU.subtract).then_inc(wq_lo, 1)
            context_turned()
            key_factors()
            queries_low(0)
            null_values()
            queries_low(1)
            queries_low(2)
            key_norms()
            scale_keys()
            queries_low(3)
            key_blocks_low(0)
            for n in range(2):
                values_low(n)
            copy_sums(0)
            for n in range(2, VWN - 1):
                values_low(n)
            key_blocks_low(1)
            values_low(VWN - 1)
            for t in range(TILES - QT):
                c = t // QT + 1
                nxt = QG * c + t % QT * 2
                if t % QT == 0:
                    read_sums(c - 1)
                    query_norms(c - 1)
                    scale_scores(t, 0)
                    xn_whole(c)
                    scale_scores(t, 1)
                    probs_low(t - 1, 0)
                    stats(t, 1)
                    probs_low(t - 1, 1)
                    scale_scores(t, 2)
                    scale_scores(t, 3)
                    queries_low(nxt)
                    stats(t, 0)
                    stats(t, 2)
                    probs_low(t - 1, 2)
                    sum_exps(t)
                    queries_low(nxt + 1)
                    variances(t)
                    inverse_roots(t)
                    values_low(VW_STEP.get(t))
                else:
                    scale_scores(t, 0)
                    scale_scores(t, 1)
                    probs_low(t - 1, 0)
                    stats(t, 1)
                    queries_low(nxt)
                    scale_scores(t, 2)
                    probs_low(t - 1, 1)
                    scale_scores(t, 3)
                    stats(t, 0)
                    stats(t, 2)
                    variances(t)
                    probs_low(t - 1, 2)
                    sum_exps(t)
                    queries_low(nxt + 1)
                    inverse_roots(t)
                    copy_sums(c)
                    values_low(VW_STEP.get(t))
            t = TILES - 2
            read_sums(QC - 1)
            query_norms(QC - 1)
            scale_scores(t, 0)
            scale_scores(t, 1)
            probs_low(t - 1, 0)
            stats(t, 1)
            probs_low(t - 1, 1)
            scale_scores(t, 2)
            scale_scores(t, 3)
            wm_low(0)
            sum_exps(t)
            wm_low(1)
            stats(t, 2)
            probs_low(t - 1, 2)
            variances(t)
            inverse_roots(t)
            t += 1
            scale_scores(t, 0)
            scale_scores(t, 1)
            probs_low(t - 1, 0)
            stats(t, 1)
            probs_low(t - 1, 1)
            scale_scores(t, 2)
            scale_scores(t, 3)
            probs_low(t - 1, 2)
            xc_low(0)
            stats(t, 2)
            sum_exps(t)
            hidden_low(0)
            variances(t)
            inverse_roots(t)
            hidden_low(1)
            t += 1
            probs_low(t - 1, 0)
            stats(t, 1)
            probs_low(t - 1, 1)
            hidden_low(2)
            probs_low(t - 1, 2)
            stats(t, 2)
            variances(t)
            inverse_roots(t)
            hidden_low(3)
            hidden_low(4)

            def h_low(f):
                for j in range(EARLY if f == 0 else 0, FT):
                    hidden_low(FT * f + j)
                    if j == 1 and f in (1, 2):
                        xc_low(f + 1)
                    if f == 0 and j in (FT - 3, FT - 1):
                        t = TILES + 1 + j // (FT - 1)
                        stats(t, 1)
                        stats(t, 2)
                        variances(t)
                        inverse_roots(t)

            def add_ffn(f, tiles=range(CT)):
                if f >= 2 and 0 in tiles:
                    dve.wait_ge(y_out[f - 2], 16)
                for k in tiles:
                    t = CT * f + k
                    dve.wait_ge(pe_y, t + 1)
                    dve.scalar_tensor_tensor(yo[:, f % 2, k, :], ps[:, BY[t % 2], 0:D], tg[:, 1:2],
                                             resid[:, t, :], ALU.mult, ALU.add).then_inc(y_ready, 1)

            h_low(0)
            xc_low(1)
            add_ffn(0)
            h_low(1)
            add_ffn(1)
            h_low(2)
            h_low(3)
            dve.tensor_reduce(hb[:, :, :], hs[:, :, :].rearrange("p j (b c) -> p j b c", b=B), AX.X,
                              ALU.add).then_inc(search_dve, 1)
            add_ffn(2, [0])
            bm, lo, w, pid, thr, cnt, ind, c_old, c_new, short = (srch[:, n:n + 1] for n in range(10))
            dve.wait_ge(search_pe, 1)
            dve.tensor_scalar(pooled[:, :], ps[0:B, BC[0], 0:D], 1.0 / N, None, ALU.mult).then_inc(search_dve, 1)
            add_ffn(2, [1])
            dve.wait_ge(search_pe, 2)
            dve.tensor_copy(plT[:, :, :].rearrange("p k b -> p (k b)"), ps[:, BC[1], 0:DK * B]).then_inc(search_dve, 1)
            dve.wait_ge(search_pe, 3)
            for b in range(B):
                dve.tensor_scalar(rT[:, HD * b:HD * b + HD], ps[0:HID, BC[0], b:b + 1].to_broadcast([HID, HD]),
                                  0.0, None, ALU.max).then_inc(search_dve, 1)
            dve.wait_ge(g_iota, 1)
            do(dve.tensor_copy(pid, part_i[:, :]))
            do(dve.tensor_scalar(thr, pid, SPREAD - 0.5, -float(SPREAD), ALU.is_gt, ALU.mult))
            do(dve.scalar_tensor_tensor(pid, pid, 1.0, thr, ALU.add, ALU.add))
            for n in range(3):
                dve.wait_ge(ck_copied, n + 1)
                (put if n < 2 else do)(dve.tensor_reduce(cmax[:, n:n + 1], ck[:, ITER * n:ITER * n + ITER], AX.X, ALU.max,
                                      apply_absolute_value=True))
                if n == 1:
                    add_ffn(2, [2])
            do(dve.tensor_reduce(bm, cmax, AX.X, ALU.max))
            put(dve.tensor_scalar(lo, bm, -1.01, -1e-30, ALU.mult, ALU.add))
            do(dve.tensor_scalar(w, bm, 2.02 / SPREAD, 2e-30 / SPREAD, ALU.mult, ALU.add))
            for n in range(2):
                do(dve.tensor_scalar(thr, pid, w, lo, ALU.mult, ALU.add))
                do(dve.tensor_scalar(over[:, :], ck[:, :], thr, None, ALU.is_gt, ALU.add, accum_out=cnt))
                dve.tensor_scalar(ind, cnt, ITER - 0.5, None, ALU.is_gt).then_inc(search_dve, 1)
                if n == 0:
                    add_ffn(2, [3])
                    add_ffn(3, [0])
                else:
                    add_ffn(3, [1])
                dve.wait_ge(search_pe, 7 + n)
                do(dve.tensor_scalar(lo, ps[:, BC[0], 0:1], w, lo, ALU.mult, ALU.add))
                do(dve.tensor_scalar(w, w, 1.0 / SPREAD, None, ALU.mult))
            put(dve.tensor_scalar(over[:, 0:ITER], ck[:, 0:ITER], lo, None, ALU.is_gt, ALU.add, accum_out=c_old))
            add_ffn(3, [2])
            do(dve.tensor_scalar(over[:, ITER:FULL], ck[:, ITER:FULL], lo, None, ALU.is_gt, ALU.add, accum_out=c_new))
            add_ffn(3, [3])
            do(dve.tensor_tensor(cnt, c_old, c_new, ALU.add))
            dve.tensor_scalar(short, cnt, ITER - 0.5, None, ALU.is_lt).then_inc(search_dve, 1)
            dve.wait_ge(search_pe, 9)
            do(dve.tensor_copy(srch[0:1, 10:12], ps[0:1, BC[1], 0:2]))
            do(dve.tensor_scalar(srch[0:1, 12:13], srch[0:1, 11:12], float(FULL), srch[0:1, 10:11],
                                 ALU.mult, ALU.add))
            dve.tensor_scalar(flag[:, :], srch[0:1, 12:13], NEW_MAX, None, ALU.is_gt).then_inc(flag_ready, 1)
            dve.wait_ge(flag_ready, 1)

            go = dve.value_load(flag[0:1, 0:1])
            with dve.If(go > 0):
                general_dve(dve)
            with dve.Else():
                dve.nop()

        @block.tensor
        def _(pe):
            def three(dst, lh, ll, rh, rl, first, last):
                pe.matmul(dst, lh, rh, start=first, stop=False)
                pe.matmul(dst, lh, rl, start=False, stop=False)
                return pe.matmul(dst, ll, rh, start=False, stop=last)

            def turn_x(c):
                if c >= QC:
                    return
                pe.wait_ge(z_ready, QT * c + QT)
                if c:
                    pe.wait_ge(sums_read, c)
                for h in range(DK):
                    for k in range(QT):
                        at = QW * h + P * k
                        mm = pe.transpose(ps[:, BX, at:at + P], z[:, (QT * c + k) % CT, P * h:P * h + P], ident[:, :])
                mm.then_inc(pe_xT, 1)

            def queries(n):
                if n >= QC * QG:
                    return
                c, g = n // QG, n % QG
                if g == 0:
                    pe.wait_ge(xn_hi, c + 1)
                    pe.wait_ge(xn_lo, c + 1)
                if n:
                    pe.wait_ge(q_full, n)
                before = QT * (c - 1) + g // 2 - 1
                if g % 2 == 0 and before in VW_STEP:
                    pe.wait_ge(vw_lo, VW_STEP[before] + 1)
                for i in range(2):
                    for k in range(DK):
                        w = slice(P * (2 * g + i), P * (2 * g + i) + P)
                        mm = three(ps[:, BQ, QW * i:QW * i + QW], Wqh[:, k, w], Wql[:, k, w], xnh[:, k, :],
                                   xnl[:, k, :], k == 0, k == DK - 1)
                mm.then_inc(pe_q, 1)

            def sums(n):
                if n >= QC * QG:
                    return
                g = n % QG
                pe.wait_ge(sq_hi, n + 1)
                pe.wait_ge(sq_lo, n + 1)
                dst = ps[0:HEADS, BX, 0:QW]
                for i in range(2):
                    pair, at = 2 * g + i, slice(QW * i, QW * i + QW)
                    pe.matmul(dst, head_of[:, pair, :], sqh[:, n % 2, at], start=pair == 0, stop=False)
                    mm = pe.matmul(dst, head_of[:, pair, :], sql[:, at], start=False, stop=pair == PAIRS - 1)
                mm.then_inc(pe_ss, 1)

            def turn_sums(c):
                if c >= QC:
                    return
                pe.wait_ge(ss_copied, c + 1)
                for k in range(QT):
                    mm = pe.transpose(ps[:, BX, HEADS * k:HEADS * k + HEADS], ssT[:, P * k:P * k + P],
                                      ident[0:HEADS, 0:HEADS])
                mm.then_inc(pe_rT, 1)

            def context_turn():
                pe.wait_ge(cz_ready, B)
                for k in range(DK):
                    for b in range(B):
                        mm = pe.transpose(ps[:, BT[0], J * (B * k + b):J * (B * k + b) + J],
                                          cz[:, b, P * k:P * k + P], ident[0:J, 0:J])
                mm.then_inc(pe_czT, 1)

            def keys(b):
                pe.wait_ge(cT_ready, DK)
                pe.wait_ge(wk_in, 16)
                for n in range(2):
                    if b:
                        pe.wait_ge(k_copied, 2 * b - 1 + n)
                    for k in range(DK):
                        mm = pe.matmul(ps[0:J, BT[n], :], cT[:, k, J * b:J * b + J],
                                       Wkv_s[:, k, 512 * n:512 * n + 512], start=k == 0, stop=k == DK - 1)
                    mm.then_inc(pe_k, 1)

            def values():
                pe.wait_ge(wv_in, 16)
                for g, (i0, n) in enumerate(VG):
                    for i in range(n):
                        for k in range(DK):
                            at = INNER + P * (i0 + i)
                            mm = pe.matmul(ps[:, VBK[g], B * J * i:B * J * i + B * J], Wkv_s[:, k, at:at + P],
                                           cT[:, k, :], start=k == 0, stop=k == DK - 1)
                    mm.then_inc(pe_v, 1)

            def key_turns(b):
                pe.wait_ge(khat_ready, b + 1)
                for i in range(PAIRS):
                    if b and i % 4 == 0:
                        pe.wait_ge(kb_lo, 2 * (i // 4) + 2)
                    pe.transpose(ps[:, BT[i // 4], KEYS * (i % 4):KEYS * (i % 4) + KEYS],
                                 kn[:, b, P * i:P * i + P], ident[0:KEYS, 0:KEYS]).then_inc(pe_kT, 1)

            def values_times_wo(n):
                if n is None:
                    return
                b, m = VWJ[n]
                if n == 0:
                    pe.wait_ge(vb_ready, 3 * len(VG))
                    pe.wait_ge(nullv_put, 2)
                    pe.wait_ge(wo_in, 16)
                elif n < VWN:
                    if n >= 2:
                        pe.wait_ge(vw_lo, n - 1)
                else:
                    pe.wait_ge(vb_again, 2)
                    pe.wait_ge(q_full, QG * (VW_AT[n] // QT + 1) + VW_AT[n] % QT * 2 + 2)
                for r in range(2):
                    lo, hi = P * (m + r), min(P * (m + r) + P, PACK)
                    over = [i for i in range(PAIRS) if PAIRW * i < hi and PAIRW * (i + 1) > lo]
                    for i in over:
                        at = P + lo - PAIRW * i
                        mm = pe.matmul(ps[:, VW_BANK[n], D * r:D * r + D], VB[:, i, at:at + P],
                                       Wo_s[:, i, :], start=i == over[0], stop=i == over[-1])
                mm.then_inc(pe_vwp, 1)

            def scores(t, g):
                if t >= TILES:
                    return
                c, k, b, n = t // QT, t % QT, t // QT // QPB, 4 * t + g
                if n >= 3:
                    pe.wait_ge(scaled, n - 2)
                elif n == 0:
                    pe.wait_ge(vb_ready, 3 * len(VG))
                elif n == 2:
                    pe.wait_ge(vw_lo, VWN)
                if t % QT == 0 and g == 0:
                    pe.wait_ge(q_hi, QG * c + QG)
                    pe.wait_ge(q_lo, QG * c + QG)
                if n == 0:
                    pe.wait_ge(kb_lo, 4)
                elif n == 3:
                    pe.wait_ge(kb_lo, 4 * B)
                for i in range(2):
                    pair = 2 * g + i
                    w = (b * PAIRS + pair) * PAIRW
                    w = slice(w, w + WIN)
                    tile = slice(P * k, P * k + P)
                    mm = three(ps[:, BS[n % 3], PAIRW * i:PAIRW * i + WIN], qh[c % 2][:, pair, tile],
                               ql[c % 2][:, pair, tile], KBh[:, w], KBl[:, w], True, True)
                mm.then_inc(pe_scores, 1)

            def attend(s, g):
                if s < 0:
                    return
                b = s // CT // CPB
                if s % (TILES // B) == 0 and g == 0:
                    pe.wait_ge(vw_lo, (b + 1) * VWN)
                if s and g == 0:
                    pe.wait_ge(o_copied, s)
                pe.wait_ge(p_hi, len(PG) * s + g + 1)
                pe.wait_ge(p_lo, len(PG) * s + g + 1)
                for m in range(*PG[g]):
                    mm = three(ps[:, BV, 0:D], ph[:, m, :], pl[:, m, :], VWh[:, b, m, :], VWl[:, b, m, :],
                               m == 0, m == KT - 1)
                if g == len(PG) - 1:
                    mm.then_inc(pe_vw, 1)

            def turn_probs(s, g):
                if s < 0:
                    return
                n = len(PG) * s + g
                if g == 0:
                    pe.wait_ge(normed, s + 1)
                if s < 2 and g == 0:
                    pe.wait_ge(zeroed, 4)
                if n >= 2:
                    pe.wait_ge(p_lo, n - 1)
                k0, k1 = PG[g]
                for m in range(k0, k1):
                    mm = pe.transpose(ps[:, BT[n % 2], P * (m - k0):P * (m - k0) + P],
                                      E[:, s % 2, P * m:P * m + P], ident[:, :])
                mm.then_inc(pe_pT, 1)

            def turn_ffn_in(f):
                pe.wait_ge(zf_ready, CT * f + CT)
                if f == 0:
                    pe.wait_ge(sums_read, QC)
                    pe.wait_ge(q_full, QC * QG)
                else:
                    pe.wait_ge(scaled, 4 * TILES)
                    if f > 1:
                        pe.wait_ge(xc_lo, DK * f)
                for h in range(DK):
                    for k in range(CT):
                        mm = pe.transpose(ps[:, BCF[f][h], P * k:P * k + P], zF[:, k, P * h:P * h + P], ident[:, :])
                    mm.then_inc(pe_cT, 1)

            def hidden_tile(n):
                f, j = n // FT, n % FT
                if n == 0:
                    pe.wait_ge(wm_lo, DK)
                if j == 0:
                    pe.wait_ge(xc_hi, DK * (f + 1))
                    pe.wait_ge(xc_lo, DK * (f + 1))
                before = [m for m in range(n) if hidden_bank(m) == hidden_bank(n)]
                if before:
                    pe.wait_ge(h_lo, before[-1] + 1)
                elif n >= EARLY:
                    pe.wait_ge(p_lo, len(PG) * TILES)
                for k in range(DK):
                    w = slice(P * j, P * j + P)
                    mm = three(ps[:, hidden_bank(n), :], Wmh[:, k, w], Wml[:, k, w],
                               xch[:, f % 2, k, :], xcl[:, f % 2, k, :], k == 0, k == DK - 1)
                mm.then_inc(pe_h, 1)

            def hidden(f):
                for j in range(EARLY if f == 0 else 0, FT):
                    hidden_tile(FT * f + j)

            pe.wait_ge(consts, 1)
            turn_x(0)
            context_turn()
            pe.wait_ge(wq_lo, DK)
            pe.wait_ge(wq_hi, DK)
            queries(0)
            keys(0)
            queries(1)
            pe.wait_ge(head_ready, 1)
            sums(0)
            keys(1)
            queries(2)
            sums(1)
            values()
            queries(3)
            sums(2)
            key_turns(0)
            for n in range(2):
                values_times_wo(n)
            sums(3)
            for n in range(2, VWN - 1):
                values_times_wo(n)
            key_turns(1)
            values_times_wo(VWN - 1)
            for t in range(TILES - QT):
                c = t // QT + 1
                nxt = QG * c + t % QT * 2
                if t % QT == 0:
                    scores(t, 0)
                    scores(t, 1)
                    turn_sums(c - 1)
                    turn_x(c)
                    turn_probs(t - 1, 0)
                    turn_probs(t - 1, 1)
                    scores(t, 2)
                    attend(t - 1, 0)
                    queries(nxt)
                    scores(t, 3)
                    turn_probs(t - 1, 2)
                    queries(nxt + 1)
                    sums(nxt)
                    attend(t - 1, 1)
                    attend(t - 1, 2)
                    values_times_wo(VW_STEP.get(t))
                else:
                    scores(t, 0)
                    scores(t, 1)
                    sums(nxt - 1)
                    turn_probs(t - 1, 0)
                    queries(nxt)
                    turn_probs(t - 1, 1)
                    scores(t, 2)
                    queries(nxt + 1)
                    scores(t, 3)
                    turn_probs(t - 1, 2)
                    attend(t - 1, 0)
                    sums(nxt)
                    attend(t - 1, 1)
                    attend(t - 1, 2)
                    values_times_wo(VW_STEP.get(t))
                    sums(nxt + 1)
            t = TILES - 2
            scores(t, 0)
            turn_sums(QC - 1)
            scores(t, 1)
            turn_probs(t - 1, 0)
            turn_probs(t - 1, 1)
            scores(t, 2)
            scores(t, 3)
            turn_probs(t - 1, 2)
            attend(t - 1, 0)
            attend(t - 1, 1)
            attend(t - 1, 2)
            t += 1
            scores(t, 0)
            scores(t, 1)
            turn_probs(t - 1, 0)
            turn_probs(t - 1, 1)
            turn_ffn_in(0)
            scores(t, 2)
            scores(t, 3)
            turn_probs(t - 1, 2)
            attend(t - 1, 0)
            hidden_tile(0)
            attend(t - 1, 1)
            attend(t - 1, 2)
            hidden_tile(1)
            t += 1
            hidden_tile(2)
            turn_probs(t - 1, 0)
            turn_probs(t - 1, 1)
            hidden_tile(3)
            attend(t - 1, 0)
            turn_probs(t - 1, 2)
            hidden_tile(4)
            attend(t - 1, 1)
            attend(t - 1, 2)

            def project(f, tiles=range(CT)):
                if f == 0:
                    pe.wait_ge(wp_lo, 2)
                    pe.wait_ge(o_copied, TILES)
                for k in tiles:
                    t = CT * f + k
                    if t >= 2:
                        pe.wait_ge(y_ready, t - 1)
                    for j in range(FT):
                        pe.wait_ge(h_lo, FT * f + j + 1)
                        w = slice(P * k, P * k + P)
                        mm = three(ps[:, BY[t % 2], 0:D], hh[f % 2][:, j, w], hl[f % 2][:, j, w],
                                   Wph[:, j, :], Wpl[:, j, :], j == 0, j == FT - 1)
                    mm.then_inc(pe_y, 1)

            hidden(0)
            turn_ffn_in(1)
            project(0)
            turn_ffn_in(2)
            hidden(1)
            project(1)
            turn_ffn_in(3)
            hidden(2)
            hidden(3)
            project(2, [0])
            pe.wait_ge(search_dve, 1)
            for j in range(FT):
                mm = pe.matmul(ps[0:B, BC[0], 0:D], hb[:, j, :], wp_raw[:, j, :], start=j == 0, stop=j == FT - 1)
            mm.then_inc(search_pe, 1)
            project(2, [1])
            pe.wait_ge(search_dve, 2)
            for k in range(DK):
                mm = pe.transpose(ps[:, BC[1], B * k:B * k + B], pooled[:, P * k:P * k + P], ident[0:B, 0:B])
            mm.then_inc(search_pe, 1)
            pe.wait_ge(search_dve, 3)
            pe.wait_ge(wc_in, 32)
            for k in range(DK):
                mm = pe.matmul(ps[0:HID, BC[0], 0:B], w_c1[:, k, :], plT[:, k, :], start=k == 0, stop=k == DK - 1)
            mm.then_inc(search_pe, 1)
            pe.wait_ge(search_dve, 3 + B)
            for j, bank in enumerate((0, 1, 5, 6, 3, 4)):
                mm = pe.matmul(ps[:, bank, :], rT[:, :], w_c2[:, 512 * j:512 * j + 512], start=True, stop=True)
                if j % 2:
                    mm.then_inc(search_pe, 1)
            project(2, [2, 3])
            for n in range(2):
                project(3, [0] if n == 0 else [1, 2])
                pe.wait_ge(search_dve, 4 + B + n)
                pe.wait_ge(ck_copied, 3)
                pe.matmul(ps[:, BC[0], 0:1], ones_b[:, :], srch[:, 6:7], start=True, stop=True).then_inc(search_pe, 1)
            project(3, [3])
            pe.wait_ge(search_dve, 6 + B)
            for n in range(2):
                for h in range(B):
                    mm = pe.matmul(ps[0:1, BC[1], n:n + 1], ident[:, HD * h:HD * h + 1], srch[:, 8 + n:9 + n],
                                   start=h == 0, stop=h == B - 1)
            mm.then_inc(search_pe, 1)

            pe.wait_ge(flag_ready, 1)
            go = pe.value_load(flag[0:1, 0:1])
            with pe.If(go > 0):
                for t in range(TILES):
                    pe.wait_ge(g_z, 2 * t + 1)
                    for k in range(DK):
                        mm = pe.transpose(ps[:, t % 2, P * k:P * k + P], zF[:, 0, P * k:P * k + P], ident[:, :])
                    mm.then_inc(g_turn, 1)
                with pe.Fori(0, 3) as s:
                    pe.wait_ge(g_small, s * G_SMALL + 1)
                    pe.sem_inc(held, 1)
                    with pe.Fori(0, FTF) as j:
                        n0 = CH * (s * FTF + j)
                        pe.wait_ge(g_w, (s * FTF + j) * 32 + 32)
                        pe.wait_ge(g_relu, n0 + CH)
                        for c in range(CH):
                            for k in range(DK):
                                mm = pe.matmul(ps[:, c, :], gwm[:, k, :], gx[:, k, CW * c:CW * c + CW],
                                               start=k == 0, stop=k == DK - 1)
                            mm.then_inc(g_h, 1)
                        for c in range(CH):
                            pe.wait_ge(g_relu, n0 + CH + c + 1)
                            pe.wait_ge(g_add, n0 + CH + c - 1)
                            for k in range(DK):
                                mm = pe.matmul(ps[:, 4 + 2 * (c % 2) + k, :], gwp[:, P * k:P * k + P], ghm[:, c, :],
                                               start=True, stop=True)
                            mm.then_inc(g_y, 1)
                    pe.wait_ge(g_small, s * G_SMALL + 2)
                    for k in range(DK):
                        mm = pe.matmul(ps[0:HID, 7, 0:B], w_c1[:, k, :], gs[:, 8 + B * k:8 + B * k + B],
                                       start=k == 0, stop=k == DK - 1)
                    mm.then_inc(g_pe, 1)
                    pe.wait_ge(g_small, s * G_SMALL + 3)
                    for b in range(B):
                        if b:
                            pe.wait_ge(g_small, s * G_SMALL + 3 + b)
                        for j in range(6):
                            mm = pe.matmul(ps[:, j, :], gr[:, b, :], w_c2[:, 512 * j:512 * j + 512],
                                           start=True, stop=True)
                        mm.then_inc(g_pe, 1)
                        pe.wait_ge(g_copy, s * B + b + 1)
                        pe.sem_inc(held, 1)
                        for j in range(FTF):
                            mm = pe.transpose(ps[:, 6, j:j + 1], grow[0:1, P * j:P * j + P], ident[0:1, 0:1])
                        mm.then_inc(g_pe, 1)
                    pe.wait_ge(g_small, s * G_SMALL + 4 + B)
                    pe.matmul(ps[:, 7, 0:1], gones[:, :], gs[:, 3:4], start=True, stop=True).then_inc(g_pe, 1)
                pe.wait_ge(g_small, 3 * G_SMALL + 1)
                for t in range(TILES):
                    if t >= 2:
                        pe.wait_ge(g_out, t - 1)
                    for k in range(DK):
                        mm = pe.transpose(ps[:, t % 2, P * k:P * k + P], gx[:, k, P * t:P * t + P], ident[:, :])
                    mm.then_inc(g_pe, 1)
            with pe.Else():
                pe.nop()


_INS = ["x", "ctx_1024", "g_xattn", "g_ffn", "L0_xattn_Wq", "L0_xattn_Wkv", "L0_xattn_Wo", "L0_xattn_null_kv",
        "L0_xattn_q_scale", "L0_xattn_k_scale", "L0_xattn_ln_in_g", "L0_xattn_ln_in_b", "L0_xattn_ln_ctx_g",
        "L0_xattn_ln_ctx_b", "L0_xattn_ln_out_g", "L0_xattn_ln_out_b", "L0_ffn_Wm", "L0_ffn_Wp", "L0_ffn_Wc1",
        "L0_ffn_Wc2"]


def kernel(**inputs):
    import numpy as _np
    import concourse.bacc as _bacc
    from concourse import mybir as _mybir
    from concourse.bass_utils import run_bass_kernel_spmd as _run

    nc = _bacc.Bacc("TRN2", target_bir_lowering=False, num_devices=1)
    arrays, args = {}, []
    for name in _INS:
        a = _np.asarray(inputs[name])
        if name.startswith("L0_ffn_"):
            a = a.T
        a = _np.ascontiguousarray(a)
        arrays[f"in_{name}_dram"] = a
        args.append(nc.dram_tensor(f"in_{name}_dram", a.shape, _mybir.dt.from_np(a.dtype), kind="ExternalInput").ap())
    shape = inputs["x"].shape
    args.append(nc.dram_tensor("out_0_dram", shape, _mybir.dt.float32, kind="ExternalOutput").ap())
    flamingo_block(nc, *args)
    r = _run(nc, [arrays], core_ids=[0])
    return r.results[0]["out_0_dram"]
```
